# Optimizing a Trainium2 kernel written in Bass

```python
import numpy as np
import jax
import jax.numpy as jnp

def _softmax(x, axis=-1):
    return jax.nn.softmax(x, axis=axis)

def _gelu(x):
    return jax.nn.gelu(x, approximate=True)

def _silu(x):
    return jax.nn.silu(x)

def _sigmoid(x):
    return jax.nn.sigmoid(x)

def _layernorm(x, axis=-1, eps=1e-05):
    m = jnp.mean(x, axis=axis, keepdims=True)
    v = jnp.var(x, axis=axis, keepdims=True)
    return (x - m) / jnp.sqrt(v + eps)

def _scatter_add(tgt, idx, src, axis=0):
    return tgt.at[idx].add(src)

def _segment_sum(src, seg, n):
    return jax.ops.segment_sum(src, seg, n)
kernel_name = 'mk_macaron_d1_jaxref_r8_2fbd1a'

def setup_inputs(seed: int=0):
    np.random.seed(seed)
    _w = jnp.asarray

    def _L0_attn_setup():
        import jax, jax.numpy as jnp
        import numpy as np
        B, S, D = (1, 256, 512)
        H = 32
        Q_RANK, KV_RANK = (192, 64)
        NOPE, ROPE, VD = (128, 64, 128)
        QD = NOPE + ROPE
        EPS = 1e-06
        THETA = 10000.0

        def _rmsnorm(x, w):
            return x * jax.lax.rsqrt(jnp.mean(x * x, axis=-1, keepdims=True) + EPS) * w

        def _rotate_half(x):
            h = x.shape[-1] // 2
            return jnp.concatenate([-x[..., h:], x[..., :h]], axis=-1)

        def _apply_rope(x, cos, sin):
            xp = jnp.concatenate([x[..., 0::2], x[..., 1::2]], axis=-1)
            return xp * cos + _rotate_half(xp) * sin

        def _mla_forward(hidden_states, Wq_a, q_a_ln_w, Wq_b, Wkv_a, kv_a_ln_w, Wkv_b, Wo):
            b, s, _ = hidden_states.shape
            q = _rmsnorm(hidden_states @ Wq_a, q_a_ln_w) @ Wq_b
            q = q.reshape(b, s, H, QD).transpose(0, 2, 1, 3)
            q_nope, q_pe = (q[..., :NOPE], q[..., NOPE:])
            ckv = hidden_states @ Wkv_a
            compressed, k_pe = (ckv[..., :KV_RANK], ckv[..., KV_RANK:])
            kv = _rmsnorm(compressed, kv_a_ln_w) @ Wkv_b
            kv = kv.reshape(b, s, H, NOPE + VD).transpose(0, 2, 1, 3)
            k_nope, v = (kv[..., :NOPE], kv[..., NOPE:])
            k_pe = k_pe[:, None, :, :]
            inv_freq = 1.0 / THETA ** (jnp.arange(0, ROPE, 2, dtype=jnp.float32) / ROPE)
            freqs = jnp.outer(jnp.arange(s, dtype=jnp.float32), inv_freq)
            emb = jnp.concatenate([freqs, freqs], axis=-1)
            cos = jnp.cos(emb)[None, None].astype(hidden_states.dtype)
            sin = jnp.sin(emb)[None, None].astype(hidden_states.dtype)
            q_pe = _apply_rope(q_pe, cos, sin)
            k_pe = _apply_rope(k_pe, cos, sin)
            qf = jnp.concatenate([q_nope, q_pe], axis=-1)
            kf = jnp.concatenate([k_nope, jnp.broadcast_to(k_pe, (b, H, s, ROPE))], axis=-1)
            scale = QD ** (-0.5)
            scores = jnp.einsum('bhqd,bhkd->bhqk', qf, kf) * scale
            causal = jnp.tril(jnp.ones((s, s), dtype=bool))
            scores = jnp.where(causal, scores, jnp.finfo(scores.dtype).min)
            probs = jax.nn.softmax(scores, axis=-1)
            o = jnp.einsum('bhqk,bhkd->bhqd', probs, v)
            o = o.transpose(0, 2, 1, 3).reshape(b, s, H * VD)
            return o @ Wo
        key = jax.random.key(seed)
        ks = jax.random.split(key, 8)
        std = 0.02
        return {'hidden_states': jax.random.normal(ks[0], (B, S, D), jnp.float32), 'Wq_a': jax.random.normal(ks[1], (D, Q_RANK), jnp.float32) * std, 'q_a_ln_w': jnp.ones((Q_RANK,), jnp.float32), 'Wq_b': jax.random.normal(ks[2], (Q_RANK, H * QD), jnp.float32) * std, 'Wkv_a': jax.random.normal(ks[3], (D, KV_RANK + ROPE), jnp.float32) * std, 'kv_a_ln_w': jnp.ones((KV_RANK,), jnp.float32), 'Wkv_b': jax.random.normal(ks[4], (KV_RANK, H * (NOPE + VD)), jnp.float32) * std, 'Wo': jax.random.normal(ks[5], (H * VD, D), jnp.float32) * std}
    _L0_attn_in = _L0_attn_setup()

    def _L0_ffn_setup():
        import jax, jax.numpy as jnp
        import numpy as np
        D_MODEL = 512
        D_HIDDEN = 1376
        RANK = 16
        BATCH, SEQ = (2, 256)

        def _matmul_lora(x, w, a, b, scale=1.0):
            out = jnp.einsum('bsd,hd->bsh', x, w)
            out = out + jnp.einsum('bsr,hr->bsh', jnp.einsum('bsd,rd->bsr', x, a), b) * scale
            return out
        key = jax.random.key(seed)
        ks = jax.random.split(key, 10)
        s = 0.02
        return {'x': jax.random.normal(ks[0], (BATCH, SEQ, D_MODEL), jnp.float32), 'gate_w': jax.random.normal(ks[1], (D_HIDDEN, D_MODEL), jnp.float32) * s, 'up_w': jax.random.normal(ks[2], (D_HIDDEN, D_MODEL), jnp.float32) * s, 'down_w': jax.random.normal(ks[3], (D_MODEL, D_HIDDEN), jnp.float32) * s, 'gate_a': jax.random.normal(ks[4], (RANK, D_MODEL), jnp.float32) * s, 'gate_b': jax.random.normal(ks[5], (D_HIDDEN, RANK), jnp.float32) * s, 'up_a': jax.random.normal(ks[6], (RANK, D_MODEL), jnp.float32) * s, 'up_b': jax.random.normal(ks[7], (D_HIDDEN, RANK), jnp.float32) * s, 'down_a': jax.random.normal(ks[8], (RANK, D_HIDDEN), jnp.float32) * s, 'down_b': jax.random.normal(ks[9], (D_MODEL, RANK), jnp.float32) * s}
    _L0_ffn_in = _L0_ffn_setup()
    _d = {'L0_attn_hidden_states': _L0_attn_in['hidden_states'], 'L0_attn_Wq_a': _L0_attn_in['Wq_a'], 'L0_attn_q_a_ln_w': _L0_attn_in['q_a_ln_w'], 'L0_attn_Wq_b': _L0_attn_in['Wq_b'], 'L0_attn_Wkv_a': _L0_attn_in['Wkv_a'], 'L0_attn_kv_a_ln_w': _L0_attn_in['kv_a_ln_w'], 'L0_attn_Wkv_b': _L0_attn_in['Wkv_b'], 'L0_attn_Wo': _L0_attn_in['Wo'], 'L0_ffn_gate_w': _L0_ffn_in['gate_w'], 'L0_ffn_up_w': _L0_ffn_in['up_w'], 'L0_ffn_down_w': _L0_ffn_in['down_w'], 'L0_ffn_gate_a': _L0_ffn_in['gate_a'], 'L0_ffn_gate_b': _L0_ffn_in['gate_b'], 'L0_ffn_up_a': _L0_ffn_in['up_a'], 'L0_ffn_up_b': _L0_ffn_in['up_b'], 'L0_ffn_down_a': _L0_ffn_in['down_a'], 'L0_ffn_down_b': _L0_ffn_in['down_b']}
    _x0 = _d['L0_attn_hidden_states']
    _d['L0_attn_hidden_states'] = jax.random.normal(jax.random.fold_in(jax.random.key(seed), 1), (2, 512, 512), dtype=_x0.dtype)
    del _x0
    return _d

def reference(L0_attn_hidden_states, L0_attn_Wq_a, L0_attn_q_a_ln_w, L0_attn_Wq_b, L0_attn_Wkv_a, L0_attn_kv_a_ln_w, L0_attn_Wkv_b, L0_attn_Wo, L0_ffn_gate_w, L0_ffn_up_w, L0_ffn_down_w, L0_ffn_gate_a, L0_ffn_gate_b, L0_ffn_up_a, L0_ffn_up_b, L0_ffn_down_a, L0_ffn_down_b):

    def _L0_attn_ref(hidden_states, Wq_a, q_a_ln_w, Wq_b, Wkv_a, kv_a_ln_w, Wkv_b, Wo):
        import jax, jax.numpy as jnp
        import numpy as np
        B, S, D = (1, 256, 512)
        H = 32
        Q_RANK, KV_RANK = (192, 64)
        NOPE, ROPE, VD = (128, 64, 128)
        QD = NOPE + ROPE
        EPS = 1e-06
        THETA = 10000.0

        def _rmsnorm(x, w):
            return x * jax.lax.rsqrt(jnp.mean(x * x, axis=-1, keepdims=True) + EPS) * w

        def _rotate_half(x):
            h = x.shape[-1] // 2
            return jnp.concatenate([-x[..., h:], x[..., :h]], axis=-1)

        def _apply_rope(x, cos, sin):
            xp = jnp.concatenate([x[..., 0::2], x[..., 1::2]], axis=-1)
            return xp * cos + _rotate_half(xp) * sin

        def _mla_forward(hidden_states, Wq_a, q_a_ln_w, Wq_b, Wkv_a, kv_a_ln_w, Wkv_b, Wo):
            b, s, _ = hidden_states.shape
            q = _rmsnorm(hidden_states @ Wq_a, q_a_ln_w) @ Wq_b
            q = q.reshape(b, s, H, QD).transpose(0, 2, 1, 3)
            q_nope, q_pe = (q[..., :NOPE], q[..., NOPE:])
            ckv = hidden_states @ Wkv_a
            compressed, k_pe = (ckv[..., :KV_RANK], ckv[..., KV_RANK:])
            kv = _rmsnorm(compressed, kv_a_ln_w) @ Wkv_b
            kv = kv.reshape(b, s, H, NOPE + VD).transpose(0, 2, 1, 3)
            k_nope, v = (kv[..., :NOPE], kv[..., NOPE:])
            k_pe = k_pe[:, None, :, :]
            inv_freq = 1.0 / THETA ** (jnp.arange(0, ROPE, 2, dtype=jnp.float32) / ROPE)
            freqs = jnp.outer(jnp.arange(s, dtype=jnp.float32), inv_freq)
            emb = jnp.concatenate([freqs, freqs], axis=-1)
            cos = jnp.cos(emb)[None, None].astype(hidden_states.dtype)
            sin = jnp.sin(emb)[None, None].astype(hidden_states.dtype)
            q_pe = _apply_rope(q_pe, cos, sin)
            k_pe = _apply_rope(k_pe, cos, sin)
            qf = jnp.concatenate([q_nope, q_pe], axis=-1)
            kf = jnp.concatenate([k_nope, jnp.broadcast_to(k_pe, (b, H, s, ROPE))], axis=-1)
            scale = QD ** (-0.5)
            scores = jnp.einsum('bhqd,bhkd->bhqk', qf, kf) * scale
            causal = jnp.tril(jnp.ones((s, s), dtype=bool))
            scores = jnp.where(causal, scores, jnp.finfo(scores.dtype).min)
            probs = jax.nn.softmax(scores, axis=-1)
            o = jnp.einsum('bhqk,bhkd->bhqd', probs, v)
            o = o.transpose(0, 2, 1, 3).reshape(b, s, H * VD)
            return o @ Wo
        return _mla_forward(hidden_states, Wq_a, q_a_ln_w, Wq_b, Wkv_a, kv_a_ln_w, Wkv_b, Wo)

    def _L0_ffn_ref(x, gate_w, up_w, down_w, gate_a, gate_b, up_a, up_b, down_a, down_b):
        import jax, jax.numpy as jnp
        import numpy as np
        D_MODEL = 512
        D_HIDDEN = 1376
        RANK = 16
        BATCH, SEQ = (2, 256)

        def _matmul_lora(x, w, a, b, scale=1.0):
            out = jnp.einsum('bsd,hd->bsh', x, w)
            out = out + jnp.einsum('bsr,hr->bsh', jnp.einsum('bsd,rd->bsr', x, a), b) * scale
            return out
        gate = _matmul_lora(x, gate_w, gate_a, gate_b)
        up = _matmul_lora(x, up_w, up_a, up_b)
        hidden = jax.nn.silu(gate) * up
        out = _matmul_lora(hidden, down_w, down_a, down_b)
        return out
    x = L0_attn_hidden_states
    x = x + 0.5 * _L0_ffn_ref(_layernorm(x, axis=-1), L0_ffn_gate_w, L0_ffn_up_w, L0_ffn_down_w, L0_ffn_gate_a, L0_ffn_gate_b, L0_ffn_up_a, L0_ffn_up_b, L0_ffn_down_a, L0_ffn_down_b)
    x = x + _L0_attn_ref(_layernorm(x, axis=-1), L0_attn_Wq_a, L0_attn_q_a_ln_w, L0_attn_Wq_b, L0_attn_Wkv_a, L0_attn_kv_a_ln_w, L0_attn_Wkv_b, L0_attn_Wo)
    x = x + 0.5 * _L0_ffn_ref(_layernorm(x, axis=-1), L0_ffn_gate_w, L0_ffn_up_w, L0_ffn_down_w, L0_ffn_gate_a, L0_ffn_gate_b, L0_ffn_up_a, L0_ffn_up_b, L0_ffn_down_a, L0_ffn_down_b)
    return x

_drawn_inputs = setup_inputs


def setup_inputs(seed=0):
    import zlib

    import numpy as np

    out = dict(_drawn_inputs(seed))
    spreads = {'L0_attn_q_a_ln_w': (1.0, 0.6), 'L0_attn_kv_a_ln_w': (1.0, 0.6)}
    factors = {'L0_attn_Wq_a': 8.0,
     'L0_attn_Wq_b': 8.0,
     'L0_ffn_gate_a': 8.0,
     'L0_ffn_gate_b': 8.0,
     'L0_ffn_up_a': 5.742,
     'L0_ffn_up_b': 5.777,
     'L0_ffn_down_a': 5.895,
     'L0_ffn_down_b': 5.965}
    for name, (base, spread) in spreads.items():
        noise = np.random.default_rng([zlib.crc32(name.encode()), seed]).standard_normal(out[name].shape)
        drawn = base * np.exp(spread * noise) if base else spread * noise
        out[name] = jnp.asarray(drawn.astype(out[name].dtype))
    for name, factor in factors.items():
        out[name] = (out[name] * factor).astype(out[name].dtype)
    return out
```

```python
from contextlib import ExitStack

import numpy as np

import concourse.bass as bass
from concourse import mybir

F32 = mybir.dt.float32
F32R = mybir.dt.float32r
ALU = mybir.AluOpType
ACT = mybir.ActivationFunctionType

P = 128
D = 512
KD = D // P
T = 1024
TT = T // P
CH = 512
CT = CH // P
NC = T // CH
HID = 1376
HT = (HID + P - 1) // P
RANK = 16
LN_EPS = 1e-5
HEADS, NOPE, ROPE, VD = 32, 128, 64, 128
N_TABLES = 6
QD = NOPE + ROPE
QR, CR = 192, 64
LAT = QR + CR + ROPE
SEQ = 512
QT4 = SEQ // P
PAIRS = 4
GROUPS = HEADS // 2 // PAIRS
UNITS = 4 * PAIRS
RMS_EPS = 1e-6
SCALE = float(QD) ** -0.5
MASKED = -1e30
SCORE = {3: (0, 0, 0), 2: (1, 0, 512), 0: (1, 384, 896), 1: (2, 0, 1024)}
TURNED = {0: (0, 0, 0), 1: (1, 0, 512), 3: (1, 384, 896), 2: (2, 0, 1024)}
TURNED_N = (512, 512, 256)
RAW = 4
ROW_G, ROW_U, ROW_D = 0, 32, 64
LROWS = ROW_D + RANK


def q_ring():
    order = [("wq", 0), ("kv", 0), ("ab", 0), ("wvo", 0), ("rot", 0), ("q0", 0), ("q1", 0)]
    for u in range(UNITS):
        p = u // 4 + 1
        if u % 4 == 0 and p < PAIRS:
            order += [("wq", p), ("kv", p)]
        if u % 4 == 1 and p < PAIRS:
            order += [("ab", p), ("wvo", p)]
        if u % 2 == 0 and u + 2 < UNITS:
            order += [(n, u // 2 + 1) for n in ("rot", "q0", "q1")]
    order += [("out", t) for t in range(TT)]
    return {use: n for n, use in enumerate(order)}


def slot(j):
    return HT - 1 - j


def rows_of(j):
    return min(P, HID - j * P)


def prog(nc, x_in, Wq_a, q_ln, Wq_b, Wkv_a, kv_ln, Wkv_b, Wo, gate_w, up_w, down_w, gate_a, gate_b, up_a, up_b,
         down_a, down_b, rope_tok, rope_t, mask_in, w_scratch, out):
    with ExitStack() as ctx:
        def sem(name):
            return ctx.enter_context(nc.semaphore(name))

        def sb(name, shape, dt=F32, where=ctx):
            return where.enter_context(nc.sbuf_tensor(name, shape, dt))

        bank = [ctx.enter_context(nc.psum_tensor(f"bank{i}", [P, 512], F32)) for i in range(8)]
        xres = sb("xres", [P, TT, D])
        ident = sb("ident", [P, P])
        stat6 = sb("stat6", [P, TT, 6])
        mv = sb("mv", [P, TT, 2])
        free_mark = sb("free_mark", [P, 1])
        wait_mark = sb("wait_mark", [P, 8])
        pool_mark = sb("pool_mark", [P, 1])
        nhalf = sb("nhalf", [P, TT])
        rstd = sb("rstd", [P, TT])
        identr = sb("identr", [P, P], F32R)
        mask0 = sb("mask0", [P, P])
        mask = sb("mask", [P, P], F32R)
        with ExitStack() as ffn:
            with ExitStack() as prep:
                raw_gu = sb("raw_gu", [P, RAW, 2, D], F32, prep)
                raw_d = sb("raw_d", [P, RAW, KD, P], F32, prep)
                LA = sb("LA", [LROWS, HID], F32, prep)
                LBT = sb("LBT", [LROWS, HID], F32, prep)
                lb_gu = sb("lb_gu", [P, HT, 48], F32, prep)
                lb_d = sb("lb_d", [P, KD, LROWS], F32, prep)
            XT = sb("XT", [P, 2, KD, CH], F32R, ffn)
            XN = sb("XN", [P, CT, D], F32, ffn)
            S = sb("S", [P, 2, CH], F32, ffn)
            H = sb("H", [P, 2, CH], F32, ffn)
            HH = sb("HH", [P, 2, CH], F32R, ffn)
            HL = sb("HL", [P, 2, CH], F32R, ffn)
            pad = sb("pad", [P, 14 * 256], F32, ffn)
            W = sb("W", [P, HT, 6, 512], F32R, ffn)
        with ExitStack() as att:
            with ExitStack() as lat:
                WAraw = sb("WAraw", [P, KD, LAT], F32, lat)
                WA = sb("WA", [P, 2, KD, LAT], F32R, lat)
                XN2 = sb("XN2", [P, 2, D], F32, lat)
                XT2 = sb("XT2", [P, 2, 2, KD, P], F32R, lat)
                LQ = sb("LQ", [P, 2, 4, P], F32, lat)
                junk = sb("junk", [P, 2, QR], F32, lat)
                ropes = sb("ropes", [P, 2, 4, 32], F32, lat)
            OT = sb("OT", [P, 2, PAIRS, T], F32R, att)
            WVO = sb("WVO", [P, 2, PAIRS, D], F32R, att)
            QT0 = sb("QT0", [P, 2, T], F32R, att)
            QT1 = sb("QT1", [P, T], F32R, att)
            KT = sb("KT", [P, 2, 2, T], F32R, att)
            CV = sb("CV", [P, TT, CR], F32, att)
            tables = sb("tables", [P, 3, SEQ], F32, att)
            tok_table = sb("tok_table", [P, TT, 2, 32], F32, att)
            lnw = sb("lnw", [P, 4], F32, att)
            stat = sb("stat", [P, TT, 2], F32, att)
            small = sb("small", [P, 4, 2, 4], F32, att)
            rawq = sb("rawq", [P, 2, 2, 2, QD], F32, att)
            rawkv = sb("rawkv", [CR, 2, 2, 256], F32, att)
            rawo = sb("rawo", [VD, 2, 2, D], F32, att)
            WTkv = sb("WTkv", [P, 2, 2, CR], F32, att)
            WTq = sb("WTq", [P, 2, 2, P], F32, att)
            A = sb("A", [P, 2, 3, 4, P], F32R, att)
            SB2 = sb("SB2", [P, SEQ], F32, att)
            QF = sb("QF", [P, 2, SEQ], F32, att)
            QH = sb("QH", [P, 2, 2, SEQ], F32R, att)
            QL = sb("QL", [P, 2, 2, SEQ], F32R, att)
            PR = sb("PR", [P, 2, 1280], F32, att)
            PT = sb("PT", [P, 2, 1280], F32, att)

        s_x = sem("s_x")
        s_lora_in = sem("s_lora_in")
        s_pad = sem("s_pad")
        s_mask = sem("s_mask")
        s_idr = sem("s_idr")
        s_ident = sem("s_ident")
        s_raw = [sem(f"s_raw{i}") for i in range(RAW)]
        s_bt = sem("s_bt")
        s_btc = sem("s_btc")
        s_wt = sem("s_wt")
        s_whi = sem("s_whi")
        s_wlo = sem("s_wlo")
        s_stats = [sem(f"s_stats{n}") for n in range(3)]
        s_rstd = [sem(f"s_rstd{n}") for n in range(3)]
        s_xn = [sem(f"s_xn{n}") for n in range(3)]
        s_xt = [sem(f"s_xt{n}") for n in range(3)]
        s_xhi = [sem(f"s_xhi{n}") for n in range(3)]
        s_xlo = [sem(f"s_xlo{n}") for n in range(3)]
        s_gate = [sem("s_gate0"), None, sem("s_gate1")]
        s_up = [sem("s_up0"), None, sem("s_up1")]
        s_silu = [sem("s_silu0"), None, sem("s_silu1")]
        s_mul = [sem("s_mul0"), None, sem("s_mul1")]
        s_hhi = [sem("s_hhi0"), None, sem("s_hhi1")]
        s_hlo = [sem("s_hlo0"), None, sem("s_hlo1")]
        s_down = [sem("s_down0"), None, sem("s_down1")]
        s_y = [sem("s_y0"), None, sem("s_y1")]
        s_pehi = sem("s_pehi")
        s_chain = sem("s_chain")
        s_store = sem("s_store")
        s_wl = [sem(f"s_wl{j}") for j in range(HT)]
        s_tab = sem("s_tab")
        s_wraw = sem("s_wraw")
        s_wahi = sem("s_wahi")
        s_walo = sem("s_walo")
        s_lat = sem("s_lat")
        s_lsq = sem("s_lsq")
        s_lss = sem("s_lss")
        s_lrs = sem("s_lrs")
        s_lq = sem("s_lq")
        s_cv = sem("s_cv")
        s_ckk = sem("s_ckk")
        s_lturn = sem("s_lturn")
        s_lhi = sem("s_lhi")
        s_llo = sem("s_llo")
        s_rawq0 = sem("s_rawq0")
        s_rawq1 = sem("s_rawq1")
        s_kvs = sem("s_kvs")
        s_pewts = sem("s_pewts")
        s_tkv = sem("s_tkv")
        s_tw = sem("s_tw")
        s_twq = sem("s_twq")
        s_ab = sem("s_ab")
        s_wvo = sem("s_wvo")
        s_abhi = sem("s_abhi")
        s_ablo = sem("s_ablo")
        s_wvohi = sem("s_wvohi")
        s_wvolo = sem("s_wvolo")
        s_qp = sem("s_qp")
        s_rope = sem("s_rope")
        s_qadd = sem("s_qadd")
        s_qhi = sem("s_qhi")
        s_qlo = sem("s_qlo")
        s_sc = sem("s_sc")
        s_mx = sem("s_mx")
        s_nb = sem("s_nb")
        s_exp = sem("s_exp")
        s_rcp = sem("s_rcp")
        s_norm = sem("s_norm")
        s_tr = sem("s_tr")
        s_ptA = sem("s_ptA")
        s_ptD = sem("s_ptD")
        s_pv = sem("s_pv")
        s_othi = sem("s_othi")
        s_otlo = sem("s_otlo")
        s_op = sem("s_op")
        s_xadd = sem("s_xadd")
        s_out = sem("s_out")

        ring = q_ring()
        uses = list(ring)
        frees = {"kv": (s_tw, PAIRS, 1), "wq": (s_twq, PAIRS, 1), "ab": (s_ablo, PAIRS, 1), "wvo": (s_wvolo, PAIRS, 1),
                 "rot": (s_rope, 24, 3), "q0": (s_rope, 24, 3), "q1": (s_rope, 24, 3), "out": (s_xadd, TT, 1)}

        def q_bank(*use):
            return bank[6 + ring[use] % 2]

        def q_bank_free(pe, g, *use):
            n = ring[use]
            if n < 2:
                return
            name, i = uses[n - 2]
            done, per_group, per_use = frees[name]
            pe.wait_ge(done, g * per_group + per_use * i + (("rot", "q0", "q1").index(name) + 1 if per_use == 3 else 1))

        block = ctx.enter_context(nc.Block())

        @block.sync
        def _(sp):
            def WAraw_dst(i):
                sp.wait_ge(s_y[0], CT * (NC + 1))
                sp.wait_ge(s_store, 16 * HT)
                return WAraw[:, :, 0:QR] if i == 0 else WAraw[:, :, QR:LAT]

            for src, row in ((gate_a, ROW_G), (up_a, ROW_U), (down_a, ROW_D)):
                sp.dma_start(LA[row:row + RANK, 0:src.shape[1]], src).then_inc(s_lora_in, 16)
            full = (HT - 1) * P
            sp.dma_start(mask0[:], mask_in).then_inc(s_mask, 16)
            sp.wait_ge(s_pad, 3)
            for src, col in ((gate_b, 0), (up_b, 32)):
                sp.dma_start(lb_gu[:, 0:HT - 1, col:col + RANK],
                             src[0:full].rearrange("(j p) r -> p j r", p=P)).then_inc(s_lora_in, 16)
                sp.dma_start(lb_gu[0:HID - full, HT - 1, col:col + RANK], src[full:HID]).then_inc(s_lora_in, 16)
            sp.dma_start(lb_d[:, :, ROW_D:LROWS], down_b.rearrange("(k p) r -> p k r", p=P)).then_inc(s_lora_in, 16)
            for j in range(HT):
                p = rows_of(j)
                if j >= RAW:
                    sp.wait_ge(s_wt, 3 * (j - RAW + 1))
                sp.dma_start(raw_gu[0:p, j % RAW, 0, :], gate_w[j * P:j * P + p]).then_inc(s_raw[j % RAW], 16)
                sp.dma_start(raw_gu[0:p, j % RAW, 1, :], up_w[j * P:j * P + p]).then_inc(s_raw[j % RAW], 16)
                sp.dma_start(raw_d[:, j % RAW, :, 0:p],
                             down_w[:, j * P:j * P + p].rearrange("(k q) h -> q k h", q=P)).then_inc(s_raw[j % RAW], 16)
                if j == 1:
                    sp.dma_start(xres[:], x_in.rearrange("(t p) d -> p t d", p=P)).then_inc(s_x, 16)

            for j in range(HT):
                sp.wait_ge(s_wlo, 3 * (j + 1))
                sp.dma_start(w_scratch[j], W[:, slot(j)].rearrange("p a n -> p (a n)").bitcast(F32)).then_inc(s_store, 16)
            sp.dma_start(WAraw_dst(0), Wq_a.rearrange("(k p) n -> p k n", p=P)).then_inc(s_wraw, 16)
            sp.dma_start(WAraw_dst(1), Wkv_a.rearrange("(k p) n -> p k n", p=P)).then_inc(s_wraw, 16)
            sp.dma_start(tables[:], rope_t).then_inc(s_tab, 16)
            sp.dma_start(tok_table[:], rope_tok).then_inc(s_tab, 16)
            sp.dma_start(lnw[:, 0:1], q_ln[0:P]).then_inc(s_tab, 16)
            sp.dma_start(lnw[0:QR - P, 1:2], q_ln[P:QR]).then_inc(s_tab, 16)
            sp.dma_start(lnw[QR - P:P, 1:2], q_ln[P:QR]).then_inc(s_tab, 16)
            sp.dma_start(lnw[0:CR, 2:3], kv_ln).then_inc(s_tab, 16)

            def load_pair(q, r):
                wq = Wq_b[:, bass.ds(q * 2 * QD, 2 * QD)].rearrange("r (h n) -> r h n", h=2)
                done = (s_rawq0, s_rawq1)[r]
                sp.dma_start(rawq[:, r, 0], wq[0:P]).then_inc(done, 16)
                sp.dma_start(rawq[0:QR - P, r, 1], wq[P:QR]).then_inc(done, 16)
                sp.dma_start(rawq[QR - P:P, r, 1], wq[P:QR]).then_inc(done, 16)
                sp.dma_start(rawkv[:, r], Wkv_b[:, bass.ds(q * 512, 512)].rearrange("c (h n) -> c h n", h=2)).then_inc(done, 16)
                sp.dma_start(rawo[:, r], Wo[bass.ds(q * 2 * VD, 2 * VD)].rearrange("(h v) n -> v h n", h=2)).then_inc(done, 16)

            load_pair(0, 0)
            load_pair(1, 1)
            for j in range(2):
                sp.wait_ge(s_store, 16 * HT)
                sp.dma_start(W[:, slot(j)].rearrange("p a n -> p (a n)").bitcast(F32), w_scratch[j]).then_inc(s_wl[j], 16)
            with sp.Fori(0, HEADS // 4 - 1) as i:
                for r in range(2):
                    sp.wait_ge(s_wvo, 2 * i + r + 1)
                    sp.wait_ge(s_pewts, 2 * i + r + 1)
                    load_pair(2 * i + r + 2, r)
            sp.wait_ge(s_pv, 2 * PAIRS * GROUPS)
            for j in range(2, HT):
                sp.dma_start(W[:, slot(j)].rearrange("p a n -> p (a n)").bitcast(F32), w_scratch[j]).then_inc(s_wl[j], 16)
            o = out.rearrange("(t p) d -> p t d", p=P)
            for c in range(NC):
                sp.wait_ge(s_y[2], CT * (c + 2))
                sp.dma_start(o[:, CT * c:CT * (c + 1)], xres[:, CT * c:CT * (c + 1), :]).then_inc(s_out, 16)
            sp.wait_ge(s_out, 16 * NC)

        @block.gpsimd
        def _(pool):
            nc.gpsimd.memset(lb_gu[:], 0.0).then_inc(s_pad, 1)
            nc.gpsimd.memset(lb_d[:], 0.0).then_inc(s_pad, 1)
            nc.gpsimd.memset(W[:, slot(HT - 1)].bitcast(F32), 0.0).then_inc(s_pad, 1)
            nc.gpsimd.memset(nhalf[:], -0.5)
            nc.gpsimd.memset(ident[:], 1.0).then_inc(s_ident, 1)
            pool.wait_ge(s_ident, 1)
            nc.gpsimd.affine_select(out=ident[:], in_=ident[:], compare_op=ALU.is_equal, fill=0.0, base=0,
                                    pattern=[[-1, P]], channel_multiplier=1).then_inc(s_ident, 1)

            pool.wait_ge(s_ident, 2)
            pool.wait_ge(s_mask, 16)
            nc.gpsimd.tensor_copy(identr[:], ident[:]).then_inc(s_idr, 1)
            nc.gpsimd.tensor_copy(mask[:], mask0[:]).then_inc(s_idr, 1)

            def ln_rstd(n):
                pool.wait_ge(s_stats[n], 1)
                nc.gpsimd.tensor_scalar(rstd[:], mv[:, :, 1], LN_EPS, None, ALU.add).then_inc(s_rstd[n], 1)
                pool.wait_ge(s_rstd[n], 1)
                nc.gpsimd.tensor_tensor(rstd[:], rstd[:], nhalf[:], ALU.pow).then_inc(s_rstd[n], 1)
                pool.wait_ge(s_rstd[n], 2)

            def ffn_norm(n):
                ln_rstd(n)
                for t in range(TT):
                    if t >= CT:
                        pool.wait_ge(s_xt[n], t - CT + 1)
                    nc.gpsimd.tensor_scalar(XN[:, t % CT, :], xres[:, t, :], mv[:, t, 0:1], rstd[:, t:t + 1],
                                            ALU.subtract, ALU.mult).then_inc(s_xn[n], 1)

            def latents():
                ln_rstd(1)
                pool.wait_ge(s_wraw, 32)
                nc.gpsimd.tensor_copy(WA[:, 0], WAraw[:]).then_inc(s_wahi, 1)
                pool.wait_ge(s_wahi, 1)
                nc.gpsimd.tensor_tensor(WA[:, 1], WAraw[:], WA[:, 0].bitcast(F32), ALU.subtract).then_inc(s_walo, 1)
                for t in range(TT + 1):
                    if t < TT:
                        if t >= 2:
                            pool.wait_ge(s_xt[1], t - 1)
                        nc.gpsimd.tensor_scalar(XN2[:, t % 2, :], xres[:, t, :], mv[:, t, 0:1], rstd[:, t:t + 1],
                                                ALU.subtract, ALU.mult).then_inc(s_xn[1], 1)
                    if t >= 1:
                        q = t - 1
                        pool.wait_ge(s_lsq, 2 * t)
                        nc.gpsimd.tensor_scalar(stat[:, q, 0:1], stat[:, q, 0:1], 1.0 / QR, RMS_EPS, ALU.mult, ALU.add)
                        nc.gpsimd.tensor_scalar(stat[:, q, 1:2], stat[:, q, 1:2], 1.0 / CR, RMS_EPS, ALU.mult,
                                                ALU.add).then_inc(s_lss, 1)
                        pool.wait_ge(s_lss, t)
                        nc.gpsimd.tensor_tensor(stat[:, q, :], stat[:, q, :], nhalf[:, 0:2], ALU.pow).then_inc(s_lrs, 1)

            def attention():
                pool.wait_ge(s_tab, 16 * N_TABLES)
                with pool.Fori(0, GROUPS) as g:
                    marks = iter(range(8))

                    def carry_wait():
                        n = next(marks)
                        nc.gpsimd.tensor_tensor(wait_mark[:, n:n + 1], nhalf[:, 0:1], nhalf[:, 0:1], ALU.mult)

                    def scale_kv(p):
                        pool.wait_ge((s_rawq0, s_rawq1)[p % 2], 80 * (g * 2 + p // 2 + 1))
                        kv = rawkv[:, p % 2].rearrange("c h n -> c (h n)")
                        carry_wait()
                        nc.gpsimd.tensor_scalar(kv, kv, lnw[0:CR, 2:3], None, ALU.mult).then_inc(s_kvs, 1)

                    def rotary_weights(p):
                        if p >= 2:
                            pool.wait_ge(s_qp, g * 24 + 6 * (p - 1))
                            carry_wait()
                        hi, lo = A[:, p % 2, :, 0::2, :], A[:, p % 2, :, 1::2, :]
                        for h in range(2):
                            c0 = 64 * h
                            for tile, eo in ((h, 0), (h, 1), (2, 0), (2, 1)):
                                src = rawq[:, p % 2, :, h, NOPE + eo:QD:2]
                                at = c0 + 32 * (eo if tile < 2 else 1 - eo)
                                nc.gpsimd.tensor_copy(hi[:, tile, :, at:at + 32], src)
                        nc.gpsimd.tensor_copy(pool_mark[:], nhalf[:, 0:1]).then_inc(s_pehi, 1)
                        pool.wait_ge(s_pehi, g * PAIRS + p + 1)
                        for h in range(2):
                            c0 = 64 * h
                            for tile, eo in ((h, 0), (h, 1), (2, 0), (2, 1)):
                                src = rawq[:, p % 2, :, h, NOPE + eo:QD:2]
                                at = c0 + 32 * (eo if tile < 2 else 1 - eo)
                                last = nc.gpsimd.tensor_tensor(lo[:, tile, :, at:at + 32], src,
                                                               hi[:, tile, :, at:at + 32].bitcast(F32), ALU.subtract)
                        last.then_inc(s_pewts, 1)

                    def rotate(pb):
                        for h in range(2):
                            pool.wait_ge(s_rope, g * 24 + 3 * pb + 2 + h)
                            r = slice(64 * h, 64 * h + 64)
                            if h == 1:
                                pool.wait_ge(s_qadd, g * 16 + 2 * pb + 1)
                            nc.gpsimd.tensor_tensor(QF[r, h, :], QF[r, h, :], SB2[r, :], ALU.add).then_inc(s_qadd, 1)
                        pool.wait_ge(s_qadd, g * 16 + 2 * pb + 2)
                        for h in range(2):
                            pool.wait_ge(s_qhi, g * 16 + 2 * pb + h + 1)
                            nc.gpsimd.tensor_tensor(QL[:, pb % 2, h, :], QF[:, h, :], QH[:, pb % 2, h, :].bitcast(F32),
                                                    ALU.subtract).then_inc(s_qlo, 1)

                    scale_kv(0)
                    rotary_weights(0)
                    rotate(0)
                    for u in range(UNITS):
                        if u % 4 == 0 and u + 4 < UNITS:
                            scale_kv(u // 4 + 1)
                            rotary_weights(u // 4 + 1)
                        if u % 2 == 0 and u + 2 < UNITS:
                            rotate(u // 2 + 1)
                    pool.wait_ge(s_qp, (g + 1) * 24)
                    carry_wait()

            pool.wait_ge(s_wt, 3 * HT)
            ffn_norm(0)
            latents()
            attention()
            ffn_norm(2)

        @block.tensor
        def _(pe):
            def prep_weights():
                pe.wait_ge(s_lora_in, 16 * 8)
                pe.wait_ge(s_ident, 2)
                for j in range(HT):
                    p = rows_of(j)
                    mm = pe.matmul(bank[j // 4][0:48, (j % 4) * P:(j % 4) * P + p], lb_gu[0:p, j, :], ident[0:p, 0:p],
                                   start=(j % 4 == 0), stop=True, is_transpose=True, skip_group_check=True)
                for k in range(KD):
                    mm = pe.matmul(bank[3][0:LROWS, k * P:(k + 1) * P], lb_d[:, k, :], ident[:],
                                   start=(k == 0), stop=True, is_transpose=True, skip_group_check=True)
                mm.then_inc(s_bt, 1)
                pe.wait_ge(s_btc, 5)
                for j in range(HT):
                    p = rows_of(j)
                    g, u, d = (bank[3 * (j % 2) + i] for i in range(3))
                    pe.wait_ge(s_raw[j % RAW], 48 * (j // RAW + 1))
                    if j >= 2:
                        pe.wait_ge(s_wlo, 3 * (j - 1))
                    for i, b in enumerate((g, u)):
                        for k in range(KD):
                            pe.matmul(b[:, k * P:k * P + p], raw_gu[0:p, j % RAW, i, k * P:(k + 1) * P], ident[0:p, 0:p],
                                      start=(k == 0), stop=False, is_transpose=True, skip_group_check=True)
                    for k in range(KD):
                        pe.matmul(d[0:p, k * P:(k + 1) * P], raw_d[:, j % RAW, k, 0:p], ident[:],
                                  start=(k == 0), stop=False, is_transpose=True, skip_group_check=True)
                    for i, (b, r) in enumerate(((g, ROW_G), (u, ROW_U))):
                        for k in range(KD):
                            mm = pe.matmul(b[:, k * P:k * P + p], LA[r:r + RANK, k * P:(k + 1) * P],
                                           LBT[r:r + RANK, j * P:j * P + p], start=False, stop=True,
                                           skip_group_check=True)
                        mm.then_inc(s_wt, 1)
                    pe.matmul(d[0:p, :], LA[ROW_D:LROWS, j * P:j * P + p], LBT[ROW_D:LROWS, 0:D],
                              start=False, stop=True, skip_group_check=True).then_inc(s_wt, 1)

            def gate_up(n, c, j):
                p = rows_of(j)
                if n == 2:
                    pe.wait_ge(s_wl[j], 16)
                if j >= 2:
                    pe.wait_ge(s_mul[n], c * HT + j - 1)
                for i, done in enumerate((s_gate[n], s_up[n])):
                    b = bank[2 * (j % 2) + i]
                    for k in range(KD):
                        for w, x in ((0, 0), (0, 1), (1, 0)):
                            mm = pe.matmul(b[0:p, :], W[:, slot(j), 2 * i + w, k * P:k * P + p], XT[:, x, k, :],
                                           start=(k == 0 and w == 0 and x == 0), stop=(k == KD - 1 and w == 1))
                    mm.then_inc(done, 1)

            def down(n, c, j):
                p = rows_of(j)
                pe.wait_ge(s_hlo[n], c * HT + j + 1)
                if j == 0:
                    pe.wait_ge(s_y[n], (c + 1) * CT)
                for t in range(CT):
                    for h, w in ((HH, 4), (HH, 5), (HL, 4)):
                        mm = pe.matmul(bank[4 + t][:], h[0:p, j % 2, t * P:(t + 1) * P], W[0:p, slot(j), w, :],
                                       start=(j == 0 and h is HH and w == 4), stop=(j == HT - 1 and h is HL))
                    mm.then_inc(s_down[n], 1)

            def ffn(n):
                with pe.Fori(0, NC) as c:
                    for t in range(CT):
                        pe.wait_ge(s_xn[n], c * CT + t + 1)
                        for k in range(KD):
                            mm = pe.matmul(bank[t][:, k * P:(k + 1) * P], XN[:, t, k * P:(k + 1) * P], ident[:],
                                           start=(k == 0), stop=True, is_transpose=True, skip_group_check=True)
                        mm.then_inc(s_xt[n], 1)
                    pe.wait_ge(s_xlo[n], (c + 1) * CT)
                    gate_up(n, c, 0)
                    for j in range(1, HT):
                        gate_up(n, c, j)
                        down(n, c, j - 1)
                    down(n, c, HT - 1)
                    pe.wait_ge(s_mul[n], (c + 1) * HT)

            def latents():
                def turn_x(t):
                    pe.wait_ge(s_xn[1], t + 1)
                    if t >= 2:
                        pe.wait_ge(s_xlo[1], t - 1)
                    for k in range(KD):
                        mm = pe.matmul(bank[t % 2][:, k * P:(k + 1) * P], XN2[:, t % 2, k * P:(k + 1) * P], ident[:],
                                       start=(k == 0), stop=True, is_transpose=True, skip_group_check=True)
                    mm.then_inc(s_xt[1], 1)

                def project(t):
                    pe.wait_ge(s_xlo[1], t + 1)
                    if t == 0:
                        pe.wait_ge(s_walo, 1)
                    if t >= 2:
                        pe.wait_ge(s_lq, 3 * (t - 1))
                        pe.wait_ge(s_ckk, t - 1)
                    for k in range(KD):
                        for x, w in ((0, 0), (0, 1), (1, 0)):
                            mm = pe.matmul(bank[2 + t % 2][:, 0:LAT], XT2[:, t % 2, x, k, :], WA[:, w, k, :],
                                           start=(k == 0 and x == 0 and w == 0), stop=(k == KD - 1 and x == 1))
                    mm.then_inc(s_lat, 1)

                def turn_latents(t):
                    pe.wait_ge(s_lq, 3 * (t + 1))
                    pe.wait_ge(s_ckk, t + 1)
                    if t >= 2:
                        pe.wait_ge(s_llo, 3 * (t - 1))
                    for k in range(4):
                        mm = pe.matmul(bank[4 + t % 2][:, k * P:(k + 1) * P], LQ[:, t % 2, k, :], ident[:],
                                       start=(k == 0), stop=True, is_transpose=True, skip_group_check=True)
                    mm.then_inc(s_lturn, 1)

                for t in range(TT + 2):
                    if t < TT:
                        turn_x(t)
                    if 1 <= t <= TT:
                        project(t - 1)
                    if t >= 2:
                        turn_latents(t - 2)
                pe.wait_ge(s_llo, 3 * TT)
                pe.wait_ge(s_idr, 2)

            def attention():
                with pe.Fori(0, GROUPS) as g:
                    def turn_weights(p):
                        r = p % 2
                        pe.wait_ge(s_kvs, g * PAIRS + p + 1)
                        q_bank_free(pe, g, "wq", p)
                        q_bank_free(pe, g, "kv", p)
                        b = q_bank("wq", p)
                        for h in range(2):
                            for i in range(2):
                                n = 2 * h + i
                                mm = pe.matmul(b[:, n * P:(n + 1) * P], rawq[:, r, i, h, 0:NOPE], ident[:],
                                               start=(n == 0), stop=True, is_transpose=True, skip_group_check=True)
                        mm.then_inc(s_tkv, 1)
                        b = q_bank("kv", p)
                        for h in range(2):
                            for kv in range(2):
                                i = 2 * h + kv
                                mm = pe.matmul(b[:, i * CR:(i + 1) * CR], rawkv[:, r, h, kv * P:(kv + 1) * P],
                                               ident[0:CR, 0:CR], start=(i == 0), stop=True, is_transpose=True,
                                               skip_group_check=True)
                        mm.then_inc(s_tkv, 1)

                    def absorb(p):
                        pe.wait_ge(s_tw, g * PAIRS + p + 1)
                        pe.wait_ge(s_twq, g * PAIRS + p + 1)
                        q_bank_free(pe, g, "ab", p)
                        b = q_bank("ab", p)
                        for h in range(2):
                            for i in range(2):
                                n = 2 * h + i
                                mm = pe.matmul(b[:, n * CR:(n + 1) * CR], WTq[:, h, i, :], WTkv[:, h, 0, :],
                                               start=True, stop=True)
                        mm.then_inc(s_ab, 1)
                        q_bank_free(pe, g, "wvo", p)
                        b = q_bank("wvo", p)
                        for h in range(2):
                            mm = pe.matmul(b[64 * h:64 * h + 64, :], WTkv[:, h, 1, :], rawo[:, p % 2, h, :],
                                           start=True, stop=True)
                        mm.then_inc(s_wvo, 1)

                    def queries(pb):
                        p, b = pb // 2, pb % 2
                        c = slice(b * SEQ, (b + 1) * SEQ)
                        if b == 0:
                            pe.wait_ge(s_ablo, g * PAIRS + p + 1)
                            pe.wait_ge(s_pewts, g * PAIRS + p + 1)
                        for name, tile in (("rot", 2), ("q0", 0), ("q1", 1)):
                            q_bank_free(pe, g, name, pb)
                            o = q_bank(name, pb)
                            w = A[:, p % 2, tile]
                            pe.matmul(o[:], w[:, 0], QT0[:, 0, c], start=True, stop=False)
                            pe.matmul(o[:], w[:, 0], QT0[:, 1, c], start=False, stop=False)
                            pe.matmul(o[:], w[:, 1], QT0[:, 0, c], start=False, stop=False)
                            pe.matmul(o[:], w[:, 2], QT1[:, c], start=False, stop=False)
                            pe.matmul(o[:], w[0:64, 3], QT1[0:64, c], start=False, stop=True).then_inc(s_qp, 1)

                    def scores(u):
                        pb, h = u // 2, u % 2
                        b = pb % 2
                        pe.wait_ge(s_qlo, g * 16 + u + 1)
                        k = KT[:, :, 1 - h, b * SEQ:(b + 1) * SEQ]
                        for n, tiles in enumerate(((3,), (2, 0), (1,))):
                            if u >= 1:
                                pe.wait_ge(s_exp, g * 4 * UNITS + 4 * (u - 1) + (1, 3, 4)[n])
                            for q in tiles:
                                o, N = SCORE[q][1], (q + 1) * P
                                s = bank[n]
                                qs = slice(q * P, (q + 1) * P)
                                pe.matmul(s[:, o:o + N], QH[:, pb % 2, h, qs], k[:, 0, 0:N], start=True, stop=False)
                                pe.matmul(s[:, o:o + N], QH[:, pb % 2, h, qs], k[:, 1, 0:N], start=False, stop=False)
                                pe.matmul(s[:, o:o + N], QL[:, pb % 2, h, qs], k[:, 0, 0:N], start=False, stop=False)
                                mm = pe.matmul(s[:, o + N - P:o + N], identr[:], mask[:], start=False, stop=True)
                            mm.then_inc(s_sc, 1)

                    def turn_probs(u):
                        pe.wait_ge(s_norm, g * UNITS + u + 1)
                        for n, blocks in enumerate(((0,), (1, 3), (2,))):
                            m = 3 * u + n
                            if m >= 2:
                                v, i = divmod(m - 2, 3)
                                if i == 1:
                                    pe.wait_ge(s_ptD, g * UNITS + v + 1)
                                else:
                                    pe.wait_ge(s_ptA, g * 2 * UNITS + 2 * v + i // 2 + 1)
                            for k in blocks:
                                for q in range(k, 4):
                                    o = TURNED[k][1] + (q - k) * P
                                    i = SCORE[q][2] + k * P
                                    mm = pe.matmul(bank[3 + m % 2][:, o:o + P], PR[:, u % 2, i:i + P], ident[:],
                                                   start=(k == blocks[0] and q == k), stop=True, is_transpose=True,
                                                   skip_group_check=True)
                            mm.then_inc(s_tr, 1)

                    def values(pb):
                        b = pb % 2
                        pe.wait_ge(s_ptA, g * 2 * UNITS + 4 * pb + 4)
                        pe.wait_ge(s_ptD, g * UNITS + 2 * pb + 2)
                        if pb >= 1:
                            pe.wait_ge(s_otlo, g * 2 * PAIRS + pb)
                        for k in range(4):
                            for h in range(2):
                                i, N = TURNED[k][2], SEQ - k * P
                                mm = pe.matmul(bank[5][64 * h:64 * h + 64, k * P:SEQ], CV[:, 4 * b + k, :],
                                               PT[:, h, i:i + N], start=(k == 0), stop=(k == 3),
                                               skip_group_check=True)
                        mm.then_inc(s_pv, 1)

                    def out_product():
                        pe.wait_ge(s_otlo, (g + 1) * 2 * PAIRS)
                        for t in range(TT):
                            q_bank_free(pe, g, "out", t)
                            o = q_bank("out", t)
                            for p in range(PAIRS):
                                for a, w in ((0, 0), (0, 1), (1, 0)):
                                    mm = pe.matmul(o[:], OT[:, a, p, t * P:(t + 1) * P], WVO[:, w, p, :],
                                                   start=(p == 0 and a == 0 and w == 0),
                                                   stop=(p == PAIRS - 1 and a == 1))
                            mm.then_inc(s_op, 1)

                    turn_weights(0)
                    absorb(0)
                    queries(0)
                    for u in range(UNITS):
                        scores(u)
                        if u % 2 == 1 and u >= 3:
                            values((u - 3) // 2)
                        p = u // 4 + 1
                        if u % 4 == 0 and p < PAIRS:
                            turn_weights(p)
                        if u % 4 == 1 and p < PAIRS:
                            absorb(p)
                        if u % 2 == 0 and u + 2 < UNITS:
                            queries(u // 2 + 1)
                        if u >= 1:
                            turn_probs(u - 1)
                    turn_probs(UNITS - 1)
                    values(UNITS // 2 - 1)
                    out_product()
                    pe.wait_ge(s_xadd, (g + 1) * TT)

            prep_weights()
            pe.wait_ge(s_wlo, 3 * HT)
            ffn(0)
            latents()
            attention()
            ffn(2)

        @block.scalar
        def _(act):
            def prep_weights():
                act.wait_ge(s_pad, 3)
                for j in range(HT):
                    p = rows_of(j)
                    for i in range(3):
                        act.wait_ge(s_wt, 3 * j + i + 1)
                        b = bank[3 * (j % 2) + i]
                        if i < 2:
                            nc.scalar.copy(W[:, slot(j), 2 * i, :].rearrange("q (k h) -> q k h", k=KD)[:, :, 0:p],
                                           b[:].rearrange("q (k h) -> q k h", k=KD)[:, :, 0:p]).then_inc(s_whi, 1)
                        else:
                            nc.scalar.copy(W[0:p, slot(j), 4, :], b[0:p, :]).then_inc(s_whi, 1)

            def ffn(n):
                with act.Fori(0, NC) as c:
                    for t in range(CT):
                        act.wait_ge(s_xt[n], c * CT + t + 1)
                        nc.scalar.copy(XT[:, 0, :, t * P:(t + 1) * P],
                                       bank[t][:].rearrange("q (k h) -> q k h", k=KD)).then_inc(s_xhi[n], 1)
                    for j in range(HT):
                        p = rows_of(j)
                        act.wait_ge(s_gate[n], c * HT + j + 1)
                        if j >= 2:
                            act.wait_ge(s_mul[n], c * HT + j - 1)
                        nc.scalar.activation(S[0:p, j % 2, :], bank[2 * (j % 2)][0:p, :], ACT.Silu).then_inc(s_silu[n], 1)
            def latents():
                act.wait_ge(s_tab, 16 * N_TABLES)

                def copy_x(t):
                    act.wait_ge(s_xt[1], t + 1)
                    if t >= 2:
                        act.wait_ge(s_lat, t - 1)
                    nc.scalar.copy(XT2[:, t % 2, 0], bank[t % 2][:].rearrange("q (k h) -> q k h", k=KD)).then_inc(s_xhi[1], 1)

                def squares(t):
                    act.wait_ge(s_lat, t + 1)
                    b = bank[2 + t % 2]
                    nc.scalar.activation(junk[:, 0, :], b[:, 0:QR], ACT.Square, accum_out=stat[:, t, 0:1]).then_inc(s_lsq, 1)
                    nc.scalar.activation(junk[:, 1, 0:CR], b[:, QR:QR + CR], ACT.Square,
                                         accum_out=stat[:, t, 1:2]).then_inc(s_lsq, 1)

                def scaled(t):
                    act.wait_ge(s_lrs, t + 1)
                    if t >= 2:
                        act.wait_ge(s_lturn, t - 1)
                    b = bank[2 + t % 2]
                    q = LQ[:, t % 2].rearrange("p a n -> p (a n)")
                    nc.scalar.activation(q[:, 0:QR], b[:, 0:QR], ACT.Copy, scale=stat[:, t, 0:1]).then_inc(s_lq, 1)
                    nc.scalar.activation(q[:, QR:2 * P], b[:, P:QR], ACT.Copy, scale=stat[:, t, 0:1]).then_inc(s_lq, 1)
                    nc.scalar.activation(CV[:, t, :], b[:, QR:QR + CR], ACT.Copy, scale=stat[:, t, 1:2]).then_inc(s_lq, 1)

                def turned(t):
                    act.wait_ge(s_lturn, t + 1)
                    b = bank[4 + t % 2]
                    c = slice(t * P, (t + 1) * P)
                    nc.scalar.activation(QT0[:, 0, c], b[:, 0:P], ACT.Copy, scale=lnw[:, 0:1]).then_inc(s_lhi, 1)
                    nc.scalar.activation(QT1[:, c], b[:, P:2 * P], ACT.Copy, scale=lnw[:, 1:2]).then_inc(s_lhi, 1)
                    nc.scalar.copy(KT[:, 0, :, c], b[:, 2 * P:4 * P].rearrange("p (a n) -> p a n", a=2)).then_inc(s_lhi, 1)

                for t in range(TT + 2):
                    if t < TT:
                        copy_x(t)
                    if 1 <= t <= TT:
                        squares(t - 1)
                        scaled(t - 1)
                    if t >= 2:
                        turned(t - 2)

            def attention():
                with act.Fori(0, GROUPS) as g:
                    def absorbed(p):
                        act.wait_ge(s_ab, g * PAIRS + p + 1)
                        b = q_bank("ab", p)
                        for h in range(2):
                            last = nc.scalar.copy(A[:, p % 2, h, 0::2, 64 * (1 - h):64 * (1 - h) + CR],
                                                  b[:, h * P:(h + 1) * P].rearrange("p (i c) -> p i c", i=2))
                            last.then_inc(s_abhi, 1)
                        act.wait_ge(s_wvo, g * PAIRS + p + 1)
                        nc.scalar.copy(WVO[:, 0, p, :], q_bank("wvo", p)[:]).then_inc(s_wvohi, 1)

                    def weights_turned(p):
                        act.wait_ge(s_tkv, (g * PAIRS + p) * 2 + 1)
                        nc.scalar.copy(WTq[:].rearrange("p h i r -> p (h i r)"), q_bank("wq", p)[:]).then_inc(s_twq, 1)

                    def queries_hi(pb):
                        for h in range(2):
                            act.wait_ge(s_qadd, g * 16 + 2 * pb + h + 1)
                            nc.scalar.copy(QH[:, pb % 2, h, :], QF[:, h, :]).then_inc(s_qhi, 1)

                    def exponentials(u):
                        act.wait_ge(s_nb, g * UNITS + u + 1)
                        for q in (3, 2, 0, 1):
                            n, o, i = SCORE[q]
                            N = (q + 1) * P
                            nc.scalar.activation(PR[:, u % 2, i:i + N], bank[n][:, o:o + N], ACT.Exp,
                                                 bias=small[:, 1, u % 2, q:q + 1], scale=SCALE,
                                                 accum_out=small[:, 2, u % 2, q:q + 1]).then_inc(s_exp, 1)

                    def probs_turned(u):
                        for n in (0, 2):
                            m = 3 * u + n
                            act.wait_ge(s_tr, g * 3 * UNITS + m + 1)
                            i, N = (0, 512) if n == 0 else (1024, 256)
                            nc.scalar.copy(PT[:, u % 2, i:i + N], bank[3 + m % 2][:, 0:N]).then_inc(s_ptA, 1)

                    def values_hi(pb):
                        act.wait_ge(s_pv, g * 2 * PAIRS + pb + 1)
                        p, b = pb // 2, pb % 2
                        nc.scalar.copy(OT[:, 0, p, b * SEQ:(b + 1) * SEQ], bank[5][:]).then_inc(s_othi, 1)

                    weights_turned(0)
                    absorbed(0)
                    queries_hi(0)
                    for u in range(UNITS):
                        exponentials(u)
                        if u % 2 == 1 and u >= 3:
                            values_hi((u - 3) // 2)
                        p = u // 4 + 1
                        if u % 4 == 0 and p < PAIRS:
                            weights_turned(p)
                        if u % 4 == 1 and p < PAIRS:
                            absorbed(p)
                        if u % 2 == 0 and u + 2 < UNITS:
                            queries_hi(u // 2 + 1)
                        if u >= 1:
                            probs_turned(u - 1)
                    probs_turned(UNITS - 1)
                    values_hi(UNITS // 2 - 1)

            prep_weights()
            ffn(0)
            latents()
            attention()
            ffn(2)

        @block.vector
        def _(dve):
            link_count = [0]

            def link(ins):
                link_count[0] += 1
                ins.then_inc(s_chain, 1)
                dve.wait_ge(s_chain, link_count[0])

            def ln_stats(m):
                for t in range(TT):
                    ins = nc.vector.bn_stats(stat6[:, t, :], xres[:, t, :])
                link(ins)
                for t in range(TT):
                    ins = nc.vector.bn_aggr(mv[:, t, :], stat6[:, t, :])
                ins.then_inc(s_stats[m], 1)

            def prep_weights():
                dve.wait_ge(s_bt, 1)
                for q in range(3):
                    n = min(512, HID - 512 * q)
                    nc.vector.tensor_copy(LBT[0:48, 512 * q:512 * q + n], bank[q][0:48, 0:n]).then_inc(s_btc, 1)
                nc.vector.tensor_copy(LBT[ROW_D:LROWS, 0:D], bank[3][ROW_D:LROWS, :]).then_inc(s_btc, 2)
                for j in range(HT):
                    p = rows_of(j)
                    for i in range(3):
                        dve.wait_ge(s_whi, 3 * j + i + 1)
                        b = bank[3 * (j % 2) + i]
                        if i < 2:
                            v = [a.rearrange("q (k h) -> q k h", k=KD)[:, :, 0:p]
                                 for a in (W[:, slot(j), 2 * i + 1, :], b[:], W[:, slot(j), 2 * i, :].bitcast(F32))]
                        else:
                            v = [W[0:p, slot(j), 5, :], b[0:p, :], W[0:p, slot(j), 4, :].bitcast(F32)]
                        nc.vector.tensor_tensor(*v, ALU.subtract).then_inc(s_wlo, 1)

            def ffn(n):
                dve.wait_ge(s_stats[n], 1)
                nc.vector.memset(free_mark[:], 0.0).then_inc(s_y[n], CT)
                with dve.Fori(0, NC) as c:
                    for t in range(CT):
                        dve.wait_ge(s_xhi[n], c * CT + t + 1)
                        nc.vector.tensor_tensor(XT[:, 1, :, t * P:(t + 1) * P],
                                                bank[t][:].rearrange("q (k h) -> q k h", k=KD),
                                                XT[:, 0, :, t * P:(t + 1) * P].bitcast(F32),
                                                ALU.subtract).then_inc(s_xlo[n], 1)
                    for j in range(HT):
                        p = rows_of(j)
                        r = j % 2
                        dve.wait_ge(s_silu[n], c * HT + j + 1)
                        dve.wait_ge(s_up[n], c * HT + j + 1)
                        nc.vector.tensor_tensor(H[0:p, r, :], bank[2 * r + 1][0:p, :], S[0:p, r, :],
                                                ALU.mult).then_inc(s_mul[n], 1)
                        if j >= 2:
                            dve.wait_ge(s_down[n], CT * (c * HT + j - 1))
                        dve.wait_ge(s_mul[n], c * HT + j + 1)
                        nc.vector.tensor_copy(HH[0:p, r, :], H[0:p, r, :]).then_inc(s_hhi[n], 1)
                        dve.wait_ge(s_hhi[n], c * HT + j + 1)
                        nc.vector.tensor_tensor(HL[0:p, r, :], H[0:p, r, :], HH[0:p, r, :].bitcast(F32),
                                                ALU.subtract).then_inc(s_hlo[n], 1)
                    for t in range(CT):
                        dve.wait_ge(s_down[n], CT * (c * HT + HT - 1) + t + 1)
                        xt = xres[:, bass.ds(c * CT + t, 1), :]
                        nc.vector.scalar_tensor_tensor(xt, bank[4 + t][:].rearrange("q (o d) -> q o d", o=1), 0.5, xt, ALU.mult, ALU.add).then_inc(s_y[n], 1)

            def latents():
                def split_x(t):
                    dve.wait_ge(s_xhi[1], t + 1)
                    nc.vector.tensor_tensor(XT2[:, t % 2, 1], bank[t % 2][:].rearrange("q (k h) -> q k h", k=KD),
                                            XT2[:, t % 2, 0].bitcast(F32), ALU.subtract).then_inc(s_xlo[1], 1)

                def keys(t):
                    dve.wait_ge(s_lq, 3 * (t + 1))
                    b = bank[2 + t % 2]
                    r = t % 2
                    if t >= 2:
                        dve.wait_ge(s_lturn, t - 1)
                    ck, kc = LQ[:, r, 2, :], LQ[:, r, 3, :]
                    nc.vector.tensor_copy(ck[:, 0:CR], CV[:, t, :])
                    nc.vector.tensor_copy(kc[:, CR:P], CV[:, t, :])
                    e, o = b[:, QR + CR:LAT:2], b[:, QR + CR + 1:LAT:2]
                    cos, sin = tok_table[:, t, 0, :], tok_table[:, t, 1, :]
                    for n, (x, y) in enumerate(((e, cos), (o, sin), (o, cos), (e, sin))):
                        ins = nc.vector.tensor_tensor(ropes[:, r, n, :], x, y, ALU.mult)
                    link(ins)
                    for dst in (ck[:, CR:P], kc[:, 0:CR]):
                        nc.vector.tensor_tensor(dst[:, 0:32], ropes[:, r, 0, :], ropes[:, r, 1, :], ALU.subtract)
                        ins = nc.vector.tensor_tensor(dst[:, 32:64], ropes[:, r, 2, :], ropes[:, r, 3, :], ALU.add)
                    ins.then_inc(s_ckk, 1)

                def split_turned(t):
                    b = bank[4 + t % 2]
                    c = slice(t * P, (t + 1) * P)
                    dve.wait_ge(s_lhi, 3 * (t + 1))
                    nc.vector.scalar_tensor_tensor(QT0[:, 1, c], b[:, 0:P], lnw[:, 0:1], QT0[:, 0, c].bitcast(F32),
                                                   ALU.mult, ALU.subtract).then_inc(s_llo, 1)
                    nc.vector.scalar_tensor_tensor(QT1[64:P, c], b[64:P, P:2 * P], lnw[64:P, 1:2],
                                                   QT1[64:P, c].bitcast(F32), ALU.mult, ALU.subtract).then_inc(s_llo, 1)
                    nc.vector.tensor_tensor(KT[:, 1, :, c], b[:, 2 * P:4 * P].rearrange("p (a n) -> p a n", a=2),
                                            KT[:, 0, :, c].bitcast(F32), ALU.subtract).then_inc(s_llo, 1)

                dve.wait_ge(s_tab, 16 * N_TABLES)
                for t in range(TT + 2):
                    if t < TT:
                        split_x(t)
                    if 1 <= t <= TT:
                        keys(t - 1)
                    if t >= 2:
                        split_turned(t - 2)

            def attention():
                with dve.Fori(0, GROUPS) as g:
                    def weights_turned(p):
                        dve.wait_ge(s_tkv, (g * PAIRS + p + 1) * 2)
                        nc.vector.tensor_copy(WTkv[:].rearrange("p h i c -> p (h i c)"),
                                              q_bank("kv", p)[:, 0:4 * CR]).then_inc(s_tw, 1)

                    def absorbed(p):
                        dve.wait_ge(s_abhi, (g * PAIRS + p + 1) * 2)
                        b = q_bank("ab", p)
                        for h in range(2):
                            c = slice(64 * (1 - h), 64 * (1 - h) + CR)
                            last = nc.vector.tensor_tensor(A[:, p % 2, h, 1::2, c],
                                                           b[:, h * P:(h + 1) * P].rearrange("p (i c) -> p i c", i=2),
                                                           A[:, p % 2, h, 0::2, c].bitcast(F32), ALU.subtract)
                        last.then_inc(s_ablo, 1)
                        dve.wait_ge(s_wvohi, g * PAIRS + p + 1)
                        nc.vector.tensor_tensor(WVO[:, 1, p, :], q_bank("wvo", p)[:], WVO[:, 0, p, :].bitcast(F32),
                                                ALU.subtract).then_inc(s_wvolo, 1)

                    def rotary(pb):
                        if pb >= 1:
                            dve.wait_ge(s_qlo, g * 16 + 2 * pb)
                        for n, (name, dst, table) in enumerate((("rot", SB2[:], 2), ("q0", QF[:, 0, :], 0),
                                                                ("q1", QF[:, 1, :], 1))):
                            dve.wait_ge(s_qp, g * 24 + 3 * pb + n + 1)
                            nc.vector.tensor_tensor(dst, q_bank(name, pb)[:], tables[:, table, :],
                                                    ALU.mult).then_inc(s_rope, 1)

                    def row_max(u):
                        r = u % 2
                        for n, tiles in enumerate(((3,), (2, 0), (1,))):
                            dve.wait_ge(s_sc, g * 3 * UNITS + 3 * u + n + 1)
                            for q in tiles:
                                o, N = SCORE[q][1], (q + 1) * P
                                ins = nc.vector.tensor_reduce(small[:, 0, r, q:q + 1], bank[n][:, o:o + N],
                                                              mybir.AxisListType.X, ALU.max)
                        ins.then_inc(s_mx, 1)
                        dve.wait_ge(s_mx, g * UNITS + u + 1)
                        nc.vector.tensor_scalar(small[:, 1, r, :], small[:, 0, r, :], -SCALE, None,
                                                ALU.mult).then_inc(s_nb, 1)

                    def normalize(u):
                        r = u % 2
                        dve.wait_ge(s_exp, g * 4 * UNITS + 4 * (u + 1))
                        nc.vector.reciprocal(small[:, 3, r, :], small[:, 2, r, :]).then_inc(s_rcp, 1)
                        dve.wait_ge(s_rcp, g * UNITS + u + 1)
                        for q in range(4):
                            i, N = SCORE[q][2], (q + 1) * P
                            ins = nc.vector.tensor_scalar(PR[:, r, i:i + N], PR[:, r, i:i + N], small[:, 3, r, q:q + 1],
                                                          None, ALU.mult)
                        ins.then_inc(s_norm, 1)

                    def probs_turned(u):
                        m = 3 * u + 1
                        dve.wait_ge(s_tr, g * 3 * UNITS + m + 1)
                        nc.vector.tensor_copy(PT[:, u % 2, 512:1024], bank[3 + m % 2][:]).then_inc(s_ptD, 1)

                    def values_lo(pb):
                        dve.wait_ge(s_othi, g * 2 * PAIRS + pb + 1)
                        p, b = pb // 2, pb % 2
                        c = slice(b * SEQ, (b + 1) * SEQ)
                        nc.vector.tensor_tensor(OT[:, 1, p, c], bank[5][:], OT[:, 0, p, c].bitcast(F32),
                                                ALU.subtract).then_inc(s_otlo, 1)

                    weights_turned(0)
                    absorbed(0)
                    rotary(0)
                    for u in range(UNITS):
                        row_max(u)
                        if u % 2 == 1 and u >= 3:
                            values_lo((u - 3) // 2)
                        p = u // 4 + 1
                        if u % 4 == 0 and p < PAIRS:
                            weights_turned(p)
                        if u % 4 == 1 and p < PAIRS:
                            absorbed(p)
                        if u % 2 == 0 and u + 2 < UNITS:
                            rotary(u // 2 + 1)
                        if u >= 1:
                            probs_turned(u - 1)
                        normalize(u)
                    probs_turned(UNITS - 1)
                    values_lo(UNITS // 2 - 1)
                    for t in range(TT):
                        dve.wait_ge(s_op, g * TT + t + 1)
                        nc.vector.tensor_tensor(xres[:, t, :], q_bank("out", t)[:], xres[:, t, :],
                                                ALU.add).then_inc(s_xadd, 1)
                    dve.wait_ge(s_qlo, (g + 1) * 16)

            prep_weights()
            dve.wait_ge(s_x, 16)
            ln_stats(0)
            ffn(0)
            dve.wait_ge(s_y[0], CT * (NC + 1))
            ln_stats(1)
            latents()
            dve.wait_ge(s_tab, 16 * N_TABLES)
            attention()
            dve.wait_ge(s_xadd, TT * GROUPS)
            ln_stats(2)
            ffn(2)


def rope_tables():
    inv = (1.0 / np.float32(10000.0) ** (np.arange(0, ROPE, 2, dtype=np.float32) / np.float32(ROPE))).astype(np.float32)
    freqs = np.outer(np.arange(SEQ, dtype=np.float32), inv).astype(np.float32)
    cos, sin = np.cos(freqs).astype(np.float32), np.sin(freqs).astype(np.float32)
    tok = np.zeros((P, TT, 2, 32), np.float32)
    for t in range(TT):
        rows = slice((t * P) % SEQ, (t * P) % SEQ + P)
        tok[:, t, 0], tok[:, t, 1] = cos[rows], sin[rows]
    turned = np.ones((P, 3, SEQ), np.float32)
    turned[0:64, 0] = turned[64:128, 1] = np.concatenate([cos.T, cos.T])
    turned[0:64, 2] = turned[64:128, 2] = np.concatenate([-sin.T, sin.T])
    return tok, turned


def kernel(**inputs):
    import concourse.bacc as bacc
    from concourse.bass_utils import run_bass_kernel_spmd as run

    nc = bacc.Bacc("TRN2", target_bir_lowering=False, num_devices=1)
    tok, turned = rope_tables()
    named = [("x", np.ascontiguousarray(inputs["L0_attn_hidden_states"]).reshape(T, D))]
    for n in ("Wq_a", "q_a_ln_w", "Wq_b", "Wkv_a", "kv_a_ln_w", "Wkv_b", "Wo"):
        a = np.ascontiguousarray(inputs["L0_attn_" + n])
        named.append((n, a.reshape(-1, 1) if a.ndim == 1 else a))
    for n in ("gate_w", "up_w", "down_w", "gate_a", "gate_b", "up_a", "up_b", "down_a", "down_b"):
        named.append((n, np.ascontiguousarray(inputs["L0_ffn_" + n])))
    named += [("rope_tok", tok), ("rope_t", turned),
              ("mask", np.triu(np.full((P, P), MASKED, np.float32), 1))]
    args = [nc.dram_tensor("in_" + n, a.shape, F32, kind="ExternalInput").ap() for n, a in named]
    args.append(nc.dram_tensor("w_scratch", (HT, P, 6 * 512), F32, kind="Internal").ap())
    args.append(nc.dram_tensor("out", (T, D), F32, kind="ExternalOutput").ap())
    prog(nc, *args)
    r = run(nc, [{"in_" + n: a for n, a in named}], core_ids=[0])
    return r.results[0]["out"].reshape(2, SEQ, D)
```

```python
from contextlib import ExitStack

import numpy as np

import concourse.bass as bass
from concourse import mybir

F32 = mybir.dt.float32
F32R = mybir.dt.float32r
ALU = mybir.AluOpType
ACT = mybir.ActivationFunctionType

P = 128
D = 512
KD = D // P
T = 1024
TT = T // P
CH = 512
CT = CH // P
NC = T // CH
HID = 1376
HT = (HID + P - 1) // P
RANK = 16
LN_EPS = 1e-5
HEADS, NOPE, ROPE, VD = 32, 128, 64, 128
N_TABLES = 9
QD = NOPE + ROPE
QR, CR = 192, 64
LAT = QR + CR + ROPE
SEQ = 512
QT4 = SEQ // P
PAIRS = 4
GROUPS = HEADS // 2 // PAIRS
UNITS = 4 * PAIRS
RMS_EPS = 1e-6
SCALE = float(QD) ** -0.5
MASKED = -1e30
SCORE = {3: (0, 0, 0), 2: (1, 0, 512), 0: (1, 384, 896), 1: (2, 0, 1024)}
TURNED = {0: (0, 0, 0), 1: (1, 0, 512), 3: (1, 384, 896), 2: (2, 0, 1024)}
TURNED_N = (512, 512, 256)
RAW = 4
ROWS_3 = (0, 32, 64)
LROWS = ROWS_3[2] + RANK
A_COLS = {"gate": 0, "up": D, "down": 2 * D}
B_COLS = {"gate": 0, "up": HID, "down": 2 * HID}
A_WIDTH, B_WIDTH = 2 * D + HID, 2 * HID + D
B_BLOCKS = {"gate": (0, HT, 0), "up": (HT, HT, 3), "down": (2 * HT, KD, 6)}


def fills(u, last):
    work = []
    if u % 4 == 2 and not (last and u >= 10):
        work.append(("turn", u // 4 + 2))
    if u % 2 == 0 and 4 <= u:
        work.append(("values", (u - 4) // 2))
    if u % 4 == 3 and not (last and u >= 11):
        work.append(("absorb", u // 4 + 2))
        if u // 4 + 2 < PAIRS:
            work.append(("wvo", u // 4 + 2))
    if u % 2 == 1 and not (last and u >= 13):
        work.append(("queries", (u + 3) // 2))
    return work


FIRST = 2
STEPS = range(FIRST, FIRST + UNITS)
RING_USES = {"turn": ("wq", "kv"), "absorb": ("ab",), "wvo": ("wvo",), "queries": ("rot", "q0", "q1"), "values": ()}


def q_ring():
    before = [("turn", 0), ("absorb", 0), ("turn", 1), ("absorb", 1), ("queries", 0), ("queries", 1), ("queries", 2),
              ("wvo", 0), ("wvo", 1)]
    first = [(n, i) for work, i in before for n in RING_USES[work]]
    body, last = ([(n, i) for u in STEPS for work, i in fills(u, is_last) for n in RING_USES[work]]
                  + [("out", t) for t in range(TT)] for is_last in (False, True))
    body += [("wvo", PAIRS), ("wvo", PAIRS + 1)]
    assert len(body) % 2 == 0
    return first, body, last


def slot(j):
    return HT - 1 - j


def b_banks():
    out = []
    for name, (_, count, b) in B_BLOCKS.items():
        width = HID if count == HT else D
        for q in range(0, width, 512):
            out.append((b + q // 512, B_COLS[name] + q, min(512, width - q)))
    return out


def rows_of(j):
    return min(P, HID - j * P)


def prog(nc, x_in, Wq_a, q_ln, Wq_b, Wkv_a, kv_ln, Wkv_b, Wo, gate_w, up_w, down_w, gate_a, gate_b, up_a, up_b,
         down_a, down_b, rope_tok, rope_t, mask_in, w_scratch, out):
    with ExitStack() as ctx:
        def sem(name):
            return ctx.enter_context(nc.semaphore(name))

        def sb(name, shape, dt=F32, where=ctx):
            return where.enter_context(nc.sbuf_tensor(name, shape, dt))

        bank = [ctx.enter_context(nc.psum_tensor(f"bank{i}", [P, 512], F32)) for i in range(8)]
        xres = sb("xres", [P, TT, D])
        ident = sb("ident", [P, P])
        stat6 = sb("stat6", [P, TT, 6])
        mv = sb("mv", [P, TT, 2])
        free_mark = sb("free_mark", [P, 1])
        wait_mark = sb("wait_mark", [P, 16])
        pool_mark = sb("pool_mark", [P, 1])
        lnw = sb("lnw", [P, 5])
        nhalf = sb("nhalf", [P, TT])
        rstd = sb("rstd", [P, TT])
        identr = sb("identr", [P, P], F32R)
        mask0 = sb("mask0", [P, P])
        mask = sb("mask", [P, P], F32R)
        with ExitStack() as ffn:
            with ExitStack() as prep:
                raw_gu = sb("raw_gu", [P, RAW, 2, D], F32, prep)
                raw_d = sb("raw_d", [P, RAW, KD, P], F32, prep)
                SA = sb("SA", [LROWS, A_WIDTH], F32R, prep)
                SBT = sb("SBT", [LROWS, B_WIDTH], F32R, prep)
            XT = sb("XT", [P, 2, KD, CH], F32R, ffn)
            S = sb("S", [P, 2, CH], F32, ffn)
            H = sb("H", [P, 2, CH], F32, ffn)
            HH = sb("HH", [P, 2, CH], F32R, ffn)
            HL = sb("HL", [P, 2, CH], F32R, ffn)
            gap = sb("gap", [P, 15 * 256], F32, ffn)
            XN = sb("XN", [P, CT, D], F32, ffn)
            with ExitStack() as stage:
                lora_a = sb("lora_a", [RANK, A_WIDTH], F32, stage)
                lb = sb("lb", [P, 2 * HT + KD, LROWS], F32, stage)
            W = sb("W", [P, HT, 6, 512], F32R, ffn)
        with ExitStack() as att:
            with ExitStack() as lat:
                WAraw = sb("WAraw", [P, KD, LAT], F32, lat)
                WA = sb("WA", [P, 2, KD, LAT], F32R, lat)
                XN2 = sb("XN2", [P, 2, D], F32, lat)
                XT2 = sb("XT2", [P, 2, 2, KD, P], F32R, lat)
                LQ = sb("LQ", [P, 2, 4, P], F32, lat)
                junk = sb("junk", [P, 2, QR], F32, lat)
                ropes = sb("ropes", [P, 2, 4, 32], F32, lat)
            OT = sb("OT", [P, 2, PAIRS, T], F32R, att)
            WVO = sb("WVO", [P, 2, PAIRS, D], F32R, att)
            QT0 = sb("QT0", [P, 2, T], F32R, att)
            QT1 = sb("QT1", [P, T], F32R, att)
            KT = sb("KT", [P, 2, 2, T], F32R, att)
            CV = sb("CV", [P, TT, CR], F32, att)
            tables = sb("tables", [P, 3, SEQ], F32, att)
            tok_table = sb("tok_table", [P, TT, 2, 32], F32, att)
            stat = sb("stat", [P, TT, 2], F32, att)
            small = sb("small", [P, 4, 2, 4], F32, att)
            rawq = sb("rawq", [P, 2, 2, 2, QD], F32, att)
            rawkv = sb("rawkv", [CR, 2, 2, 256], F32, att)
            rawo = sb("rawo", [VD, 2, 2, D], F32, att)
            WTk = sb("WTk", [P, 2, CR], F32, att)
            WTv = sb("WTv", [P, 2, 2, CR], F32, att)
            WTq = sb("WTq", [P, 2, 2, P], F32, att)
            A = sb("A", [P, 2, 3, 4, P], F32R, att)
            SB2 = sb("SB2", [P, SEQ], F32, att)
            QF = sb("QF", [P, 2, SEQ], F32, att)
            QH = sb("QH", [P, 2, 2, SEQ], F32R, att)
            QL = sb("QL", [P, 2, 2, SEQ], F32R, att)
            PR = sb("PR", [P, 4, 1280], F32, att)
            PT = sb("PT", [P, 3, 1280], F32, att)

        s_x = sem("s_x")
        s_lora_in = sem("s_lora_in")
        s_lorb_in = sem("s_lorb_in")
        s_pad = sem("s_pad")
        s_mask = sem("s_mask")
        s_idr = sem("s_idr")
        s_ident = sem("s_ident")
        s_raw = [sem(f"s_raw{i}") for i in range(RAW)]
        s_bt = sem("s_bt")
        s_split = sem("s_split")
        s_last = sem("s_last")
        s_bhi = sem("s_bhi")
        s_blo = sem("s_blo")
        s_wt = sem("s_wt")
        s_whi = sem("s_whi")
        s_wlo = sem("s_wlo")
        s_stats = [sem(f"s_stats{n}") for n in range(3)]
        s_rstd = [sem(f"s_rstd{n}") for n in range(3)]
        s_xn = [sem(f"s_xn{n}") for n in range(3)]
        s_xt = [sem(f"s_xt{n}") for n in range(3)]
        s_xhi = [sem(f"s_xhi{n}") for n in range(3)]
        s_xlo = [sem(f"s_xlo{n}") for n in range(3)]
        s_gate = [sem("s_gate0"), None, sem("s_gate1")]
        s_up = [sem("s_up0"), None, sem("s_up1")]
        s_silu = [sem("s_silu0"), None, sem("s_silu1")]
        s_mul = [sem("s_mul0"), None, sem("s_mul1")]
        s_hhi = [sem("s_hhi0"), None, sem("s_hhi1")]
        s_hlo = [sem("s_hlo0"), None, sem("s_hlo1")]
        s_down = [sem("s_down0"), None, sem("s_down1")]
        s_y = [sem("s_y0"), None, sem("s_y1")]
        s_ones = sem("s_ones")
        s_st6 = sem("s_st6")
        s_pehi = sem("s_pehi")
        s_chain = sem("s_chain")
        s_store = sem("s_store")
        s_wl = [sem(f"s_wl{j}") for j in range(HT)]
        s_tab = sem("s_tab")
        s_wraw = sem("s_wraw")
        s_wahi = sem("s_wahi")
        s_walo = sem("s_walo")
        s_lat = sem("s_lat")
        s_lsq = sem("s_lsq")
        s_lss = sem("s_lss")
        s_lrs = sem("s_lrs")
        s_lq = sem("s_lq")
        s_cv = sem("s_cv")
        s_ckk = sem("s_ckk")
        s_lturn = sem("s_lturn")
        s_lhi = sem("s_lhi")
        s_llo = sem("s_llo")
        s_rawq0 = sem("s_rawq0")
        s_rawq1 = sem("s_rawq1")
        s_pewts = sem("s_pewts")
        s_tkv = sem("s_tkv")
        s_tw = sem("s_tw")
        s_twq = sem("s_twq")
        s_ab = sem("s_ab")
        s_wvo = sem("s_wvo")
        s_abhi = sem("s_abhi")
        s_ablo = sem("s_ablo")
        s_wvohi = sem("s_wvohi")
        s_wvolo = sem("s_wvolo")
        s_qp = sem("s_qp")
        s_rope = sem("s_rope")
        s_qadd = sem("s_qadd")
        s_qhi = sem("s_qhi")
        s_qlo = sem("s_qlo")
        s_sc = sem("s_sc")
        s_mx = sem("s_mx")
        s_nb = sem("s_nb")
        s_exp = sem("s_exp")
        s_rcp = sem("s_rcp")
        s_norm = sem("s_norm")
        s_tr = sem("s_tr")
        s_pt = sem("s_pt")
        s_ptD = sem("s_ptD")
        s_pv = sem("s_pv")
        s_othi = sem("s_othi")
        s_otlo = sem("s_otlo")
        s_op = sem("s_op")
        s_xadd = sem("s_xadd")
        s_out = sem("s_out")

        ring_first, ring_body, ring_last = q_ring()

        def ring_of(g):
            return ring_last if isinstance(g, int) else ring_body
        frees = {"kv": (s_tw, PAIRS, 1), "wq": (s_twq, PAIRS, 1), "ab": (s_ablo, PAIRS, 1), "wvo": (s_wvolo, PAIRS, 1),
                 "rot": (s_rope, 24, 3), "q0": (s_rope, 24, 3), "q1": (s_rope, 24, 3), "out": (s_xadd, TT, 1)}

        def q_bank(g, *use):
            n = ring_first.index(use) if g is None else len(ring_first) + ring_of(g).index(use)
            return bank[6 + n % 2]

        def q_bank_free(pe, g, *use):
            before = ring_first if g is None else ring_first[-2:] + ring_of(g)
            n = before.index(use, 0 if g is None else 2) - 2
            if n < 0:
                return
            name, i = before[n]
            done, per_group, per_use = frees[name]
            count = per_use * i + (("rot", "q0", "q1").index(name) + 1 if per_use == 3 else 1)
            pe.wait_ge(done, nth(g) * per_group + count)

        def nth(g):
            return 0 if g is None else g

        block = ctx.enter_context(nc.Block())

        @block.sync
        def _(sp):
            def WAraw_dst(i):
                sp.wait_ge(s_y[0], CT * (NC + 1))
                sp.wait_ge(s_store, 16 * HT)
                return WAraw[:, :, 0:QR] if i == 0 else WAraw[:, :, QR:LAT]

            sp.dma_start(mask0[:], mask_in).then_inc(s_mask, 16)
            for j in range(HT):
                p = rows_of(j)
                if j == 1:
                    sp.wait_ge(s_lorb_in, 16 * 5)
                if j >= RAW:
                    sp.wait_ge(s_wt, 3 * (j - RAW + 1))
                sp.dma_start(raw_gu[0:p, j % RAW, 0, :], gate_w[j * P:j * P + p]).then_inc(s_raw[j % RAW], 16)
                sp.dma_start(raw_gu[0:p, j % RAW, 1, :], up_w[j * P:j * P + p]).then_inc(s_raw[j % RAW], 16)
                sp.dma_start(raw_d[:, j % RAW, :, 0:p],
                             down_w[:, j * P:j * P + p].rearrange("(k q) h -> q k h", q=P)).then_inc(s_raw[j % RAW], 16)
                if j == 1:
                    sp.dma_start(xres[:], x_in.rearrange("(t p) d -> p t d", p=P)).then_inc(s_x, 16)

            for j in range(HT):
                sp.wait_ge(s_wlo, 3 * (j + 1))
                sp.dma_start(w_scratch[j], W[:, slot(j)].rearrange("p a n -> p (a n)").bitcast(F32)).then_inc(s_store, 16)
            sp.dma_start(WAraw_dst(0), Wq_a.rearrange("(k p) n -> p k n", p=P)).then_inc(s_wraw, 16)
            sp.dma_start(WAraw_dst(1), Wkv_a.rearrange("(k p) n -> p k n", p=P)).then_inc(s_wraw, 16)
            sp.dma_start(tables[:], rope_t).then_inc(s_tab, 16)
            sp.dma_start(tok_table[:], rope_tok).then_inc(s_tab, 16)
            sp.dma_start(lnw[:, 0:1], q_ln[0:P]).then_inc(s_tab, 16)
            sp.dma_start(lnw[0:QR - P, 1:2], q_ln[P:QR]).then_inc(s_tab, 16)
            sp.dma_start(lnw[QR - P:P, 1:2], q_ln[P:QR]).then_inc(s_tab, 16)
            sp.wait_ge(s_ones, 1)
            for rows, col in ((slice(0, CR), 2), (slice(CR, P), 2), (slice(0, CR), 3), (slice(CR, P), 4)):
                sp.dma_start(lnw[rows, col:col + 1], kv_ln).then_inc(s_tab, 16)

            def load_pair(q, r):
                wq = Wq_b[:, bass.ds(q * 2 * QD, 2 * QD)].rearrange("r (h n) -> r h n", h=2)
                done = (s_rawq0, s_rawq1)[r]
                sp.dma_start(rawq[:, r, 0], wq[0:P]).then_inc(done, 16)
                sp.dma_start(rawq[0:QR - P, r, 1], wq[P:QR]).then_inc(done, 16)
                sp.dma_start(rawq[QR - P:P, r, 1], wq[P:QR]).then_inc(done, 16)
                sp.dma_start(rawkv[:, r], Wkv_b[:, bass.ds(q * 512, 512)].rearrange("c (h n) -> c h n", h=2)).then_inc(done, 16)
                sp.dma_start(rawo[:, r], Wo[bass.ds(q * 2 * VD, 2 * VD)].rearrange("(h v) n -> v h n", h=2)).then_inc(done, 16)

            load_pair(0, 0)
            load_pair(1, 1)
            with sp.Fori(0, HEADS // 4 - 1) as i:
                for r in range(2):
                    sp.wait_ge(s_wvo, 2 * i + r + 1)
                    sp.wait_ge(s_pewts, 2 * i + r + 1)
                    load_pair(2 * i + r + 2, r)
            sp.wait_ge(s_pv, 2 * PAIRS * GROUPS)
            for j in range(HT):
                sp.dma_start(W[:, slot(j)].rearrange("p a n -> p (a n)").bitcast(F32), w_scratch[j]).then_inc(s_wl[j], 16)
            o = out.rearrange("(t p) d -> p t d", p=P)
            for c in range(NC):
                sp.wait_ge(s_y[2], CT * (c + 2))
                sp.dma_start(o[:, CT * c:CT * (c + 1)], xres[:, CT * c:CT * (c + 1), :]).then_inc(s_out, 16)
            sp.wait_ge(s_out, 16 * NC)

        @block.gpsimd
        def _(pool):
            nc.gpsimd.memset(SA[:].bitcast(F32), 0.0).then_inc(s_pad, 1)
            nc.gpsimd.memset(nhalf[:], -0.5)
            nc.gpsimd.memset(lnw[:, 3:5], 1.0).then_inc(s_ones, 1)
            nc.gpsimd.memset(ident[:], 1.0).then_inc(s_ident, 1)
            pool.wait_ge(s_ident, 1)
            nc.gpsimd.affine_select(out=ident[:], in_=ident[:], compare_op=ALU.is_equal, fill=0.0, base=0,
                                    pattern=[[-1, P]], channel_multiplier=1).then_inc(s_ident, 1)

            pool.wait_ge(s_ident, 2)
            pool.wait_ge(s_mask, 16)
            nc.gpsimd.tensor_copy(identr[:], ident[:]).then_inc(s_idr, 1)
            nc.gpsimd.tensor_copy(mask[:], mask0[:]).then_inc(s_idr, 1)
            pool.wait_ge(s_bt, 1)
            pool.wait_ge(s_split, 5)
            nc.gpsimd.memset(W[:, slot(HT - 1)].bitcast(F32), 0.0).then_inc(s_last, 1)

            def ln_rstd(n):
                pool.wait_ge(s_stats[n], 1)
                nc.gpsimd.tensor_scalar(rstd[:], mv[:, :, 1], LN_EPS, None, ALU.add).then_inc(s_rstd[n], 1)
                pool.wait_ge(s_rstd[n], 1)
                nc.gpsimd.tensor_tensor(rstd[:], rstd[:], nhalf[:], ALU.pow).then_inc(s_rstd[n], 1)
                pool.wait_ge(s_rstd[n], 2)

            def ffn_norm(n):
                ln_rstd(n)
                pool.wait_ge(s_xn[n], CT)
                for t in range(CT, TT):
                    pool.wait_ge(s_xt[n], t - CT + 1)
                    nc.gpsimd.tensor_scalar(XN[:, t % CT, :], xres[:, t, :], mv[:, t, 0:1], rstd[:, t:t + 1],
                                            ALU.subtract, ALU.mult).then_inc(s_xn[n], 1)

            def latents():
                ln_rstd(1)
                pool.wait_ge(s_wraw, 32)
                nc.gpsimd.tensor_copy(WA[:, 0], WAraw[:]).then_inc(s_wahi, 1)
                pool.wait_ge(s_wahi, 1)
                nc.gpsimd.tensor_tensor(WA[:, 1], WAraw[:], WA[:, 0].bitcast(F32), ALU.subtract).then_inc(s_walo, 1)
                pool.wait_ge(s_xn[1], 2)
                for t in range(TT + 1):
                    if 2 <= t < TT:
                        pool.wait_ge(s_xt[1], t - 1)
                        nc.gpsimd.tensor_scalar(XN2[:, t % 2, :], xres[:, t, :], mv[:, t, 0:1], rstd[:, t:t + 1],
                                                ALU.subtract, ALU.mult).then_inc(s_xn[1], 1)
                    if t >= 1:
                        q = t - 1
                        pool.wait_ge(s_lsq, 2 * t)
                        nc.gpsimd.tensor_scalar(stat[:, q, 0:1], stat[:, q, 0:1], 1.0 / QR, RMS_EPS, ALU.mult, ALU.add)
                        nc.gpsimd.tensor_scalar(stat[:, q, 1:2], stat[:, q, 1:2], 1.0 / CR, RMS_EPS, ALU.mult,
                                                ALU.add).then_inc(s_lss, 1)
                        pool.wait_ge(s_lss, t)
                        nc.gpsimd.tensor_tensor(stat[:, q, :], stat[:, q, :], nhalf[:, 0:2], ALU.pow).then_inc(s_lrs, 1)

            def attention():
                pool.wait_ge(s_tab, 16 * N_TABLES)
                marks = [0]

                def carry_wait():
                    n = marks[0]
                    marks[0] += 1
                    nc.gpsimd.tensor_tensor(wait_mark[:, n:n + 1], nhalf[:, 0:1], nhalf[:, 0:1], ALU.mult)

                def rotary_weights(g, p):
                    pool.wait_ge((s_rawq0, s_rawq1)[p % 2], 80 * (nth(g) * 2 + p // 2 + 1))
                    carry_wait()
                    if p >= 2:
                        pool.wait_ge(s_qp, nth(g) * 24 + 6 * (p - 1))
                        carry_wait()
                    hi, lo = A[:, p % 2, :, 0::2, :], A[:, p % 2, :, 1::2, :]
                    for h in range(2):
                        c0 = 64 * h
                        for tile, eo in ((h, 0), (h, 1), (2, 0), (2, 1)):
                            src = rawq[:, p % 2, :, h, NOPE + eo:QD:2]
                            at = c0 + 32 * (eo if tile < 2 else 1 - eo)
                            nc.gpsimd.tensor_copy(hi[:, tile, :, at:at + 32], src)
                    nc.gpsimd.tensor_copy(pool_mark[:], nhalf[:, 0:1]).then_inc(s_pehi, 1)
                    pool.wait_ge(s_pehi, nth(g) * PAIRS + p + 1)
                    for h in range(2):
                        c0 = 64 * h
                        for tile, eo in ((h, 0), (h, 1), (2, 0), (2, 1)):
                            src = rawq[:, p % 2, :, h, NOPE + eo:QD:2]
                            at = c0 + 32 * (eo if tile < 2 else 1 - eo)
                            last = nc.gpsimd.tensor_tensor(lo[:, tile, :, at:at + 32], src,
                                                           hi[:, tile, :, at:at + 32].bitcast(F32), ALU.subtract)
                    last.then_inc(s_pewts, 1)

                def rotate(g, pb):
                    for h in range(2):
                        pool.wait_ge(s_rope, nth(g) * 24 + 3 * pb + 2 + h)
                        r = slice(64 * h, 64 * h + 64)
                        if h == 1:
                            pool.wait_ge(s_qadd, nth(g) * 16 + 2 * pb + 1)
                        nc.gpsimd.tensor_tensor(QF[r, h, :], QF[r, h, :], SB2[r, :], ALU.add).then_inc(s_qadd, 1)
                    pool.wait_ge(s_qadd, nth(g) * 16 + 2 * pb + 2)
                    for h in range(2):
                        pool.wait_ge(s_qhi, nth(g) * 16 + 2 * pb + h + 1)
                        nc.gpsimd.tensor_tensor(QL[:, pb % 2, h, :], QF[:, h, :], QH[:, pb % 2, h, :].bitcast(F32),
                                                ALU.subtract).then_inc(s_qlo, 1)

                def group(g, last):
                    marks[0] = 4
                    for u in STEPS:
                        for work, i in fills(u, last):
                            if work == "turn":
                                rotary_weights(g, i)
                            if work == "queries":
                                rotate(g, i)

                for p in range(2):
                    rotary_weights(None, p)
                for pb in range(3):
                    rotate(None, pb)
                with pool.Fori(0, GROUPS - 1) as g:
                    group(g, False)
                group(GROUPS - 1, True)

            ffn_norm(0)
            latents()
            attention()
            ffn_norm(2)

        @block.tensor
        def _(pe):
            def prep_weights():
                pe.wait_ge(s_split, 2)
                pe.wait_ge(s_ident, 2)
                for first, count, b in B_BLOCKS.values():
                    for j in range(count):
                        p = rows_of(j)
                        mm = pe.matmul(bank[b + j // 4][0:LROWS, (j % 4) * P:(j % 4) * P + p], lb[0:p, first + j, :],
                                       ident[0:p, 0:p], start=(j % 4 == 0), stop=True, is_transpose=True,
                                       skip_group_check=True)
                mm.then_inc(s_bt, 1)
                for j in range(HT):
                    p = rows_of(j)
                    g, u, d = (bank[3 * (j % 2) + i] for i in range(3))
                    pe.wait_ge(s_raw[j % RAW], 48 * (j // RAW + 1))
                    if j >= 2:
                        pe.wait_ge(s_wlo, 3 * (j - 1))
                    elif j == 0:
                        pe.wait_ge(s_blo, 7)
                        pe.wait_ge(s_split, 5)
                    for i, b in enumerate((g, u)):
                        for k in range(KD):
                            pe.matmul(b[:, k * P:k * P + p], raw_gu[0:p, j % RAW, i, k * P:(k + 1) * P], ident[0:p, 0:p],
                                      start=(k == 0), stop=False, is_transpose=True, skip_group_check=True)
                    for k in range(KD):
                        pe.matmul(d[0:p, k * P:(k + 1) * P], raw_d[:, j % RAW, k, 0:p], ident[:],
                                  start=(k == 0), stop=False, is_transpose=True, skip_group_check=True)
                    for b, name in ((g, "gate"), (u, "up")):
                        for k in range(KD):
                            a0, b0 = A_COLS[name] + k * P, B_COLS[name] + j * P
                            mm = pe.matmul(b[:, k * P:k * P + p], SA[:, a0:a0 + P], SBT[:, b0:b0 + p],
                                           start=False, stop=True, skip_group_check=True)
                        mm.then_inc(s_wt, 1)
                    a0, b0 = A_COLS["down"] + j * P, B_COLS["down"]
                    pe.matmul(d[0:p, :], SA[:, a0:a0 + p], SBT[:, b0:b0 + D], start=False, stop=True,
                              skip_group_check=True).then_inc(s_wt, 1)

            def gate_up(n, c, j):
                p = rows_of(j)
                if n == 2:
                    pe.wait_ge(s_wl[j], 16)
                if j >= 2:
                    pe.wait_ge(s_mul[n], c * HT + j - 1)
                for i, done in enumerate((s_gate[n], s_up[n])):
                    b = bank[2 * (j % 2) + i]
                    for k in range(KD):
                        for w, x in ((0, 0), (0, 1), (1, 0)):
                            mm = pe.matmul(b[0:p, :], W[:, slot(j), 2 * i + w, k * P:k * P + p], XT[:, x, k, :],
                                           start=(k == 0 and w == 0 and x == 0), stop=(k == KD - 1 and w == 1))
                    mm.then_inc(done, 1)

            def down(n, c, j):
                p = rows_of(j)
                pe.wait_ge(s_hlo[n], c * HT + j + 1)
                if j == 0:
                    pe.wait_ge(s_y[n], (c + 1) * CT)
                for t in range(CT):
                    for h, w in ((HH, 4), (HH, 5), (HL, 4)):
                        mm = pe.matmul(bank[4 + t][:], h[0:p, j % 2, t * P:(t + 1) * P], W[0:p, slot(j), w, :],
                                       start=(j == 0 and h is HH and w == 4), stop=(j == HT - 1 and h is HL))
                    mm.then_inc(s_down[n], 1)

            def ffn(n):
                with pe.Fori(0, NC) as c:
                    for t in range(CT):
                        pe.wait_ge(s_xn[n], c * CT + t + 1)
                        for k in range(KD):
                            mm = pe.matmul(bank[t][:, k * P:(k + 1) * P], XN[:, t, k * P:(k + 1) * P], ident[:],
                                           start=(k == 0), stop=True, is_transpose=True, skip_group_check=True)
                        mm.then_inc(s_xt[n], 1)
                    pe.wait_ge(s_xlo[n], (c + 1) * CT)
                    gate_up(n, c, 0)
                    for j in range(1, HT):
                        gate_up(n, c, j)
                        down(n, c, j - 1)
                    down(n, c, HT - 1)
                    pe.wait_ge(s_mul[n], (c + 1) * HT)

            def latents():
                def turn_x(t):
                    pe.wait_ge(s_xn[1], t + 1)
                    if t >= 2:
                        pe.wait_ge(s_xlo[1], t - 1)
                    for k in range(KD):
                        mm = pe.matmul(bank[t % 2][:, k * P:(k + 1) * P], XN2[:, t % 2, k * P:(k + 1) * P], ident[:],
                                       start=(k == 0), stop=True, is_transpose=True, skip_group_check=True)
                    mm.then_inc(s_xt[1], 1)

                def project(t):
                    pe.wait_ge(s_xlo[1], t + 1)
                    if t == 0:
                        pe.wait_ge(s_walo, 1)
                    if t >= 2:
                        pe.wait_ge(s_lq, 3 * (t - 1))
                        pe.wait_ge(s_ckk, t - 1)
                    for k in range(KD):
                        for x, w in ((0, 0), (0, 1), (1, 0)):
                            mm = pe.matmul(bank[2 + t % 2][:, 0:LAT], XT2[:, t % 2, x, k, :], WA[:, w, k, :],
                                           start=(k == 0 and x == 0 and w == 0), stop=(k == KD - 1 and x == 1))
                    mm.then_inc(s_lat, 1)

                def turn_latents(t):
                    pe.wait_ge(s_lq, 3 * (t + 1))
                    pe.wait_ge(s_ckk, t + 1)
                    if t >= 2:
                        pe.wait_ge(s_llo, 4 * (t - 1))
                    for k in range(4):
                        mm = pe.matmul(bank[4 + t % 2][:, k * P:(k + 1) * P], LQ[:, t % 2, k, :], ident[:],
                                       start=(k == 0), stop=True, is_transpose=True, skip_group_check=True)
                    mm.then_inc(s_lturn, 1)

                for t in range(TT + 2):
                    if t < TT:
                        turn_x(t)
                    if 1 <= t <= TT:
                        project(t - 1)
                    if t >= 2:
                        turn_latents(t - 2)
                pe.wait_ge(s_llo, 4 * TT)
                pe.wait_ge(s_idr, 2)

            def attention():
                def turn_weights(g, p):
                    r = p % 2
                    pe.wait_ge((s_rawq0, s_rawq1)[p % 2], 80 * (nth(g) * 2 + p // 2 + 1))
                    q_bank_free(pe, g, "wq", p)
                    q_bank_free(pe, g, "kv", p)
                    b = q_bank(g, "wq", p)
                    for h in range(2):
                        for i in range(2):
                            n = 2 * h + i
                            mm = pe.matmul(b[:, n * P:(n + 1) * P], rawq[:, r, i, h, 0:NOPE], ident[:],
                                           start=(n == 0), stop=True, is_transpose=True, skip_group_check=True)
                    mm.then_inc(s_tkv, 1)
                    b = q_bank(g, "kv", p)
                    for h in range(2):
                        for kv in range(2):
                            i = 2 * h + kv
                            mm = pe.matmul(b[:, i * CR:(i + 1) * CR], rawkv[:, r, h, kv * P:(kv + 1) * P],
                                           ident[0:CR, 0:CR], start=(i == 0), stop=True, is_transpose=True,
                                           skip_group_check=True)
                    mm.then_inc(s_tkv, 1)

                def absorb(g, p):
                    pe.wait_ge(s_tw, nth(g) * PAIRS + p + 1)
                    pe.wait_ge(s_twq, nth(g) * PAIRS + p + 1)
                    q_bank_free(pe, g, "ab", p)
                    b = q_bank(g, "ab", p)
                    for h in range(2):
                        for i in range(2):
                            n = 2 * h + i
                            mm = pe.matmul(b[:, n * CR:(n + 1) * CR], WTq[:, h, i, :], WTk[:, h, :],
                                           start=True, stop=True)
                    mm.then_inc(s_ab, 1)

                def value_weights(g, p):
                    q_bank_free(pe, g, "wvo", p)
                    b = q_bank(g, "wvo", p)
                    for h in range(2):
                        mm = pe.matmul(b[64 * h:64 * h + 64, :], WTv[:, p % 2, h, :], rawo[:, p % 2, h, :],
                                       start=True, stop=True)
                    mm.then_inc(s_wvo, 1)

                def queries(g, pb):
                    p, b = pb // 2, pb % 2
                    c = slice(b * SEQ, (b + 1) * SEQ)
                    if b == 0:
                        pe.wait_ge(s_ablo, nth(g) * PAIRS + p + 1)
                        pe.wait_ge(s_pewts, nth(g) * PAIRS + p + 1)
                    for name, tile in (("rot", 2), ("q0", 0), ("q1", 1)):
                        q_bank_free(pe, g, name, pb)
                        o = q_bank(g, name, pb)
                        w = A[:, p % 2, tile]
                        pe.matmul(o[:], w[:, 0], QT0[:, 0, c], start=True, stop=False)
                        pe.matmul(o[:], w[:, 0], QT0[:, 1, c], start=False, stop=False)
                        pe.matmul(o[:], w[:, 1], QT0[:, 0, c], start=False, stop=False)
                        pe.matmul(o[:], w[:, 2], QT1[:, c], start=False, stop=False)
                        pe.matmul(o[:], w[0:64, 3], QT1[0:64, c], start=False, stop=True).then_inc(s_qp, 1)

                def scores(g, u, n):
                    pb, h = u // 2, u % 2
                    b = pb % 2
                    if n == 0:
                        pe.wait_ge(s_qlo, nth(g) * 16 + u + 1)
                    k = KT[:, :, 1 - h, b * SEQ:(b + 1) * SEQ]
                    if not (g is None and u == 0):
                        pe.wait_ge(s_exp, nth(g) * 4 * UNITS + 4 * (u - 1) + (1, 3, 4)[n])
                    for q in ((3,), (2, 0), (1,))[n]:
                        o, N = SCORE[q][1], (q + 1) * P
                        s = bank[n]
                        qs = slice(q * P, (q + 1) * P)
                        pe.matmul(s[:, o:o + N], QH[:, pb % 2, h, qs], k[:, 0, 0:N], start=True, stop=False)
                        pe.matmul(s[:, o:o + N], QH[:, pb % 2, h, qs], k[:, 1, 0:N], start=False, stop=False)
                        pe.matmul(s[:, o:o + N], QL[:, pb % 2, h, qs], k[:, 0, 0:N], start=False, stop=False)
                        mm = pe.matmul(s[:, o + N - P:o + N], identr[:], mask[:], start=False, stop=True)
                    mm.then_inc(s_sc, 1)

                def turn_probs(g, u, n):
                    if n == 0:
                        pe.wait_ge(s_norm, nth(g) * UNITS + u + 1)
                    m = 3 * u + n
                    if not (g is None or (u == 0 and n < 2)):
                        pe.wait_ge(s_pt, nth(g) * 3 * UNITS + m - 1)
                    blocks = ((0,), (1, 3), (2,))[n]
                    for k in blocks:
                        for q in range(k, 4):
                            o = TURNED[k][1] + (q - k) * P
                            i = SCORE[q][2] + k * P
                            mm = pe.matmul(bank[3 + m % 2][:, o:o + P], PR[:, u % 4, i:i + P], ident[:],
                                           start=(k == blocks[0] and q == k), stop=True, is_transpose=True,
                                           skip_group_check=True)
                    mm.then_inc(s_tr, 1)

                def values(g, pb):
                    b = pb % 2
                    if pb >= 1:
                        pe.wait_ge(s_otlo, nth(g) * 2 * PAIRS + pb)
                    for k in (0, 1, 3, 2):
                        for h in range(2):
                            if k != 3:
                                pe.wait_ge(s_pt, nth(g) * 3 * UNITS + 3 * (2 * pb + 1) + (1, 2, 3)[k])
                            i, N = TURNED[k][2], SEQ - k * P
                            mm = pe.matmul(bank[5][64 * h:64 * h + 64, k * P:SEQ], CV[:, 4 * b + k, :],
                                           PT[:, (2 * pb + h) % 3, i:i + N], start=(k == 0), stop=(k == 2),
                                           skip_group_check=True)
                    mm.then_inc(s_pv, 1)

                def out_product(g):
                    for t in range(TT):
                        if t % 4 == 0:
                            pe.wait_ge(s_otlo, (nth(g) + 1) * 2 * PAIRS - 1 + t // 4)
                        q_bank_free(pe, g, "out", t)
                        o = q_bank(g, "out", t)
                        for p in range(PAIRS):
                            for a, w in ((0, 0), (0, 1), (1, 0)):
                                mm = pe.matmul(o[:], OT[:, a, p, t * P:(t + 1) * P], WVO[:, w, p, :],
                                               start=(p == 0 and a == 0 and w == 0),
                                               stop=(p == PAIRS - 1 and a == 1))
                        mm.then_inc(s_op, 1)

                work_of = {"turn": turn_weights, "wvo": value_weights, "queries": queries,
                           "values": values}

                def group(g, last):
                    for u in STEPS:
                        if ("absorb", u // 4 + 2) in fills(u, last):
                            absorb(g, u // 4 + 2)
                        for n in range(3):
                            if u < UNITS or not last:
                                scores(g, u, n)
                            turn_probs(g, u - 2, n)
                        for work, i in fills(u, last):
                            if work in work_of:
                                work_of[work](g, i)
                    values(g, UNITS // 2 - 1)
                    out_product(g)
                    if not last:
                        value_weights(g, PAIRS)
                        value_weights(g, PAIRS + 1)

                for p in range(2):
                    turn_weights(None, p)
                    absorb(None, p)
                queries(None, 0)
                queries(None, 1)
                for n in range(3):
                    scores(None, 0, n)
                queries(None, 2)
                for n in range(3):
                    scores(None, 1, n)
                value_weights(None, 0)
                value_weights(None, 1)
                with pe.Fori(0, GROUPS - 1) as g:
                    group(g, False)
                group(GROUPS - 1, True)

            prep_weights()
            pe.wait_ge(s_wlo, 3 * HT)
            ffn(0)
            latents()
            attention()
            ffn(2)

        @block.scalar
        def _(act):
            def prep_weights():
                for src, name in ((gate_a, "gate"), (up_a, "up"), (down_a, "down")):
                    c = A_COLS[name]
                    act.dma_start(lora_a[:, c:c + src.shape[1]], src).then_inc(s_lora_in, 16)
                act.wait_ge(s_pad, 2)
                full = (HT - 1) * P
                for src, name in ((gate_b, "gate"), (up_b, "up")):
                    f = B_BLOCKS[name][0]
                    act.dma_start(lb[:, f:f + HT - 1, 0:RANK],
                                  src[0:full].rearrange("(j p) r -> p j r", p=P)).then_inc(s_lorb_in, 16)
                    act.dma_start(lb[0:HID - full, f + HT - 1, 0:RANK], src[full:HID]).then_inc(s_lorb_in, 16)
                act.dma_start(lb[:, 2 * HT:, 0:RANK], down_b.rearrange("(k p) r -> p k r", p=P)).then_inc(s_lorb_in, 16)
                act.wait_ge(s_bt, 1)
                for b, c, n in b_banks():
                    nc.scalar.copy(SBT[:, c:c + n], bank[b][0:LROWS, 0:n]).then_inc(s_bhi, 1)
                for j in range(HT):
                    p = rows_of(j)
                    for i in range(3):
                        act.wait_ge(s_wt, 3 * j + i + 1)
                        if j == HT - 1:
                            act.wait_ge(s_last, 1)
                        b = bank[3 * (j % 2) + i]
                        if i < 2:
                            nc.scalar.copy(W[:, slot(j), 2 * i, :].rearrange("q (k h) -> q k h", k=KD)[:, :, 0:p],
                                           b[:].rearrange("q (k h) -> q k h", k=KD)[:, :, 0:p]).then_inc(s_whi, 1)
                        else:
                            nc.scalar.copy(W[0:p, slot(j), 4, :], b[0:p, :]).then_inc(s_whi, 1)

            def ffn(n):
                with act.Fori(0, NC) as c:
                    for t in range(CT):
                        act.wait_ge(s_xt[n], c * CT + t + 1)
                        nc.scalar.copy(XT[:, 0, :, t * P:(t + 1) * P],
                                       bank[t][:].rearrange("q (k h) -> q k h", k=KD)).then_inc(s_xhi[n], 1)
                    for j in range(HT):
                        p = rows_of(j)
                        act.wait_ge(s_gate[n], c * HT + j + 1)
                        if j >= 2:
                            act.wait_ge(s_mul[n], c * HT + j - 1)
                        nc.scalar.activation(S[0:p, j % 2, :], bank[2 * (j % 2)][0:p, :], ACT.Silu).then_inc(s_silu[n], 1)
            def latents():
                act.wait_ge(s_tab, 16 * N_TABLES)

                def copy_x(t):
                    act.wait_ge(s_xt[1], t + 1)
                    if t >= 2:
                        act.wait_ge(s_lat, t - 1)
                    nc.scalar.copy(XT2[:, t % 2, 0], bank[t % 2][:].rearrange("q (k h) -> q k h", k=KD)).then_inc(s_xhi[1], 1)

                def squares(t):
                    act.wait_ge(s_lat, t + 1)
                    b = bank[2 + t % 2]
                    nc.scalar.activation(junk[:, 0, :], b[:, 0:QR], ACT.Square, accum_out=stat[:, t, 0:1]).then_inc(s_lsq, 1)
                    nc.scalar.activation(junk[:, 1, 0:CR], b[:, QR:QR + CR], ACT.Square,
                                         accum_out=stat[:, t, 1:2]).then_inc(s_lsq, 1)

                def scaled(t):
                    act.wait_ge(s_lrs, t + 1)
                    if t >= 2:
                        act.wait_ge(s_lturn, t - 1)
                    b = bank[2 + t % 2]
                    q = LQ[:, t % 2].rearrange("p a n -> p (a n)")
                    nc.scalar.activation(q[:, 0:QR], b[:, 0:QR], ACT.Copy, scale=stat[:, t, 0:1]).then_inc(s_lq, 1)
                    nc.scalar.activation(q[:, QR:2 * P], b[:, P:QR], ACT.Copy, scale=stat[:, t, 0:1]).then_inc(s_lq, 1)
                    nc.scalar.activation(CV[:, t, :], b[:, QR:QR + CR], ACT.Copy, scale=stat[:, t, 1:2]).then_inc(s_lq, 1)

                def turned(t):
                    act.wait_ge(s_lturn, t + 1)
                    b = bank[4 + t % 2]
                    c = slice(t * P, (t + 1) * P)
                    nc.scalar.activation(QT0[:, 0, c], b[:, 0:P], ACT.Copy, scale=lnw[:, 0:1]).then_inc(s_lhi, 1)
                    nc.scalar.activation(QT1[:, c], b[:, P:2 * P], ACT.Copy, scale=lnw[:, 1:2]).then_inc(s_lhi, 1)
                    for a in range(2):
                        nc.scalar.activation(KT[:, 0, a, c], b[:, (2 + a) * P:(3 + a) * P], ACT.Copy,
                                             scale=lnw[:, 3 + a:4 + a]).then_inc(s_lhi, 1)

                for t in range(TT + 2):
                    if t < TT:
                        copy_x(t)
                    if 1 <= t <= TT:
                        squares(t - 1)
                        scaled(t - 1)
                    if t >= 2:
                        turned(t - 2)

            def attention():
                def absorbed(g, p):
                    act.wait_ge(s_ab, nth(g) * PAIRS + p + 1)
                    b = q_bank(g, "ab", p)
                    for h in range(2):
                        nc.scalar.copy(A[:, p % 2, h, 0::2, 64 * (1 - h):64 * (1 - h) + CR],
                                       b[:, h * P:(h + 1) * P].rearrange("p (i c) -> p i c", i=2)).then_inc(s_abhi, 1)

                def value_weights(g, p):
                    act.wait_ge(s_wvo, nth(g) * PAIRS + p + 1)
                    nc.scalar.activation(WVO[:, 0, p % PAIRS, :], q_bank(g, "wvo", p)[:], ACT.Copy,
                                         scale=lnw[:, 2:3]).then_inc(s_wvohi, 1)

                def weights_turned(g, p):
                    act.wait_ge(s_tkv, (nth(g) * PAIRS + p) * 2 + 1)
                    nc.scalar.copy(WTq[:].rearrange("p h i r -> p (h i r)"), q_bank(g, "wq", p)[:]).then_inc(s_twq, 1)

                def queries_hi(g, pb):
                    for h in range(2):
                        act.wait_ge(s_qadd, nth(g) * 16 + 2 * pb + h + 1)
                        nc.scalar.copy(QH[:, pb % 2, h, :], QF[:, h, :]).then_inc(s_qhi, 1)

                def exponentials(g, u, n):
                    act.wait_ge(s_mx, nth(g) * 3 * UNITS + 3 * u + n + 1)
                    for q in ((3,), (2, 0), (1,))[n]:
                        _, o, i = SCORE[q]
                        N = (q + 1) * P
                        nc.scalar.activation(PR[:, u % 4, i:i + N], bank[n][:, o:o + N], ACT.Exp,
                                             bias=small[:, 0, u % 2, q:q + 1], scale=1.0,
                                             accum_out=small[:, 2, u % 2, q:q + 1]).then_inc(s_exp, 1)

                def probs_turned(g, u, n):
                    m = 3 * u + n
                    act.wait_ge(s_tr, nth(g) * 3 * UNITS + m + 1)
                    i, N = (0, 512, 1024)[n], TURNED_N[n]
                    nc.scalar.copy(PT[:, u % 3, i:i + N], bank[3 + m % 2][:, 0:N]).then_inc(s_pt, 1)

                def values_hi(g, pb):
                    act.wait_ge(s_pv, nth(g) * 2 * PAIRS + pb + 1)
                    p, b = pb // 2, pb % 2
                    nc.scalar.copy(OT[:, 0, p, b * SEQ:(b + 1) * SEQ], bank[5][:]).then_inc(s_othi, 1)

                work_of = {"turn": weights_turned, "wvo": value_weights, "values": values_hi}

                def group(g, last):
                    for u in STEPS:
                        if ("absorb", u // 4 + 2) in fills(u, last):
                            absorbed(g, u // 4 + 2)
                        for n in range(3):
                            probs_turned(g, u - 2, n)
                            if u < UNITS or not last:
                                exponentials(g, u, n)
                        if u % 2 == 0 and ("queries", u // 2 + 1) in (fills(u - 1, last) if u > 2 else [("queries", 2)]):
                            queries_hi(g, u // 2 + 1)
                        for work, i in fills(u, last):
                            if work in work_of:
                                work_of[work](g, i)
                    values_hi(g, UNITS // 2 - 1)
                    if not last:
                        value_weights(g, PAIRS)
                        value_weights(g, PAIRS + 1)

                for p in range(2):
                    weights_turned(None, p)
                    absorbed(None, p)
                queries_hi(None, 0)
                queries_hi(None, 1)
                for n in range(3):
                    exponentials(None, 0, n)
                for n in range(3):
                    exponentials(None, 1, n)
                value_weights(None, 0)
                value_weights(None, 1)
                with act.Fori(0, GROUPS - 1) as g:
                    group(g, False)
                group(GROUPS - 1, True)

            prep_weights()
            ffn(0)
            latents()
            attention()
            ffn(2)

        @block.vector
        def _(dve):
            link_count = [0]

            def link(ins):
                link_count[0] += 1
                ins.then_inc(s_chain, 1)
                dve.wait_ge(s_chain, link_count[0])

            def tile_stats(t):
                nc.vector.bn_stats(stat6[:, t, :], xres[:, t, :]).then_inc(s_st6, 1)

            def ln_stats(m, tiles, xn):
                dve.wait_ge(s_st6, TT * (m + 1))
                for t in range(TT):
                    ins = nc.vector.bn_aggr(mv[:, t, :], stat6[:, t, :])
                ins.then_inc(s_stats[m], 1)
                dve.wait_ge(s_rstd[m], 2)
                for t in range(tiles):
                    nc.vector.tensor_scalar(xn[:, t, :], xres[:, t, :], mv[:, t, 0:1], rstd[:, t:t + 1],
                                            ALU.subtract, ALU.mult).then_inc(s_xn[m], 1)

            def prep_weights():
                nc.vector.memset(lb[:], 0.0).then_inc(s_pad, 1)
                dve.wait_ge(s_lorb_in, 16 * 5)
                for c in ROWS_3[1:]:
                    nc.vector.tensor_copy(lb[:, :, c:c + RANK], lb[:, :, 0:RANK]).then_inc(s_split, 1)
                dve.wait_ge(s_lora_in, 16 * 3)
                dve.wait_ge(s_pad, 2)
                for r in ROWS_3[:2]:
                    nc.vector.tensor_copy(SA[r:r + RANK, :], lora_a[:]).then_inc(s_split, 1)
                dve.wait_ge(s_split, 4)
                nc.vector.tensor_tensor(SA[ROWS_3[2]:LROWS, :], lora_a[:], SA[0:RANK, :].bitcast(F32),
                                        ALU.subtract).then_inc(s_split, 1)
                for i, (b, c, n) in enumerate(b_banks()):
                    dve.wait_ge(s_bhi, i + 1)
                    r = slice(ROWS_3[1], ROWS_3[1] + RANK)
                    nc.vector.tensor_tensor(SBT[r, c:c + n], bank[b][r, 0:n], SBT[r, c:c + n].bitcast(F32),
                                            ALU.subtract).then_inc(s_blo, 1)
                for j in range(HT):
                    p = rows_of(j)
                    for i in range(3):
                        dve.wait_ge(s_whi, 3 * j + i + 1)
                        b = bank[3 * (j % 2) + i]
                        if i < 2:
                            v = [a.rearrange("q (k h) -> q k h", k=KD)[:, :, 0:p]
                                 for a in (W[:, slot(j), 2 * i + 1, :], b[:], W[:, slot(j), 2 * i, :].bitcast(F32))]
                        else:
                            v = [W[0:p, slot(j), 5, :], b[0:p, :], W[0:p, slot(j), 4, :].bitcast(F32)]
                        nc.vector.tensor_tensor(*v, ALU.subtract).then_inc(s_wlo, 1)
                    if j == 3:
                        dve.wait_ge(s_x, 16)
                    if j >= 3:
                        tile_stats(j - 3)
                ln_stats(0, CT, XN)

            def ffn(n):
                dve.wait_ge(s_stats[n], 1)
                nc.vector.memset(free_mark[:], 0.0).then_inc(s_y[n], CT)
                with dve.Fori(0, NC) as c:
                    for t in range(CT):
                        dve.wait_ge(s_xhi[n], c * CT + t + 1)
                        nc.vector.tensor_tensor(XT[:, 1, :, t * P:(t + 1) * P],
                                                bank[t][:].rearrange("q (k h) -> q k h", k=KD),
                                                XT[:, 0, :, t * P:(t + 1) * P].bitcast(F32),
                                                ALU.subtract).then_inc(s_xlo[n], 1)
                    for j in range(HT):
                        p = rows_of(j)
                        r = j % 2
                        dve.wait_ge(s_silu[n], c * HT + j + 1)
                        dve.wait_ge(s_up[n], c * HT + j + 1)
                        nc.vector.tensor_tensor(H[0:p, r, :], bank[2 * r + 1][0:p, :], S[0:p, r, :],
                                                ALU.mult).then_inc(s_mul[n], 1)
                        if j >= 2:
                            dve.wait_ge(s_down[n], CT * (c * HT + j - 1))
                        dve.wait_ge(s_mul[n], c * HT + j + 1)
                        nc.vector.tensor_copy(HH[0:p, r, :], H[0:p, r, :]).then_inc(s_hhi[n], 1)
                        dve.wait_ge(s_hhi[n], c * HT + j + 1)
                        nc.vector.tensor_tensor(HL[0:p, r, :], H[0:p, r, :], HH[0:p, r, :].bitcast(F32),
                                                ALU.subtract).then_inc(s_hlo[n], 1)
                    for t in range(CT):
                        dve.wait_ge(s_down[n], CT * (c * HT + HT - 1) + t + 1)
                        xt = xres[:, bass.ds(c * CT + t, 1), :]
                        nc.vector.scalar_tensor_tensor(xt, bank[4 + t][:].rearrange("q (o d) -> q o d", o=1), 0.5,
                                                       xt, ALU.mult, ALU.add).then_inc(s_y[n], 1)
                    if n == 0:
                        for t in range(CT):
                            dve.wait_ge(s_y[n], (c + 1) * CT + t + 1)
                            nc.vector.bn_stats(stat6[:, bass.ds(c * CT + t, 1), :],
                                               xres[:, bass.ds(c * CT + t, 1), :]).then_inc(s_st6, 1)

            def latents():
                def split_x(t):
                    dve.wait_ge(s_xhi[1], t + 1)
                    nc.vector.tensor_tensor(XT2[:, t % 2, 1], bank[t % 2][:].rearrange("q (k h) -> q k h", k=KD),
                                            XT2[:, t % 2, 0].bitcast(F32), ALU.subtract).then_inc(s_xlo[1], 1)

                def keys(t):
                    dve.wait_ge(s_lq, 3 * (t + 1))
                    b = bank[2 + t % 2]
                    r = t % 2
                    if t >= 2:
                        dve.wait_ge(s_lturn, t - 1)
                    ck, kc = LQ[:, r, 2, :], LQ[:, r, 3, :]
                    nc.vector.tensor_copy(ck[:, 0:CR], CV[:, t, :])
                    nc.vector.tensor_copy(kc[:, CR:P], CV[:, t, :])
                    e, o = b[:, QR + CR:LAT:2], b[:, QR + CR + 1:LAT:2]
                    cos, sin = tok_table[:, t, 0, :], tok_table[:, t, 1, :]
                    for n, (x, y) in enumerate(((e, cos), (o, sin), (o, cos), (e, sin))):
                        ins = nc.vector.tensor_tensor(ropes[:, r, n, :], x, y, ALU.mult)
                    link(ins)
                    for dst in (ck[:, CR:P], kc[:, 0:CR]):
                        nc.vector.tensor_tensor(dst[:, 0:32], ropes[:, r, 0, :], ropes[:, r, 1, :], ALU.subtract)
                        ins = nc.vector.tensor_tensor(dst[:, 32:64], ropes[:, r, 2, :], ropes[:, r, 3, :], ALU.add)
                    ins.then_inc(s_ckk, 1)

                def split_turned(t):
                    b = bank[4 + t % 2]
                    c = slice(t * P, (t + 1) * P)
                    dve.wait_ge(s_lhi, 4 * (t + 1))
                    nc.vector.scalar_tensor_tensor(QT0[:, 1, c], b[:, 0:P], lnw[:, 0:1], QT0[:, 0, c].bitcast(F32),
                                                   ALU.mult, ALU.subtract).then_inc(s_llo, 1)
                    nc.vector.scalar_tensor_tensor(QT1[64:P, c], b[64:P, P:2 * P], lnw[64:P, 1:2],
                                                   QT1[64:P, c].bitcast(F32), ALU.mult, ALU.subtract).then_inc(s_llo, 1)
                    for a in range(2):
                        nc.vector.scalar_tensor_tensor(KT[:, 1, a, c], b[:, (2 + a) * P:(3 + a) * P],
                                                       lnw[:, 3 + a:4 + a], KT[:, 0, a, c].bitcast(F32),
                                                       ALU.mult, ALU.subtract).then_inc(s_llo, 1)

                dve.wait_ge(s_tab, 16 * N_TABLES)
                for t in range(TT + 2):
                    if t < TT:
                        split_x(t)
                    if 1 <= t <= TT:
                        keys(t - 1)
                    if t >= 2:
                        split_turned(t - 2)

            def attention():
                def weights_turned(g, p):
                    dve.wait_ge(s_tkv, (nth(g) * PAIRS + p + 1) * 2)
                    kv = q_bank(g, "kv", p)[:, 0:4 * CR].rearrange("p (h i c) -> p h i c", h=2, i=2)
                    nc.vector.tensor_copy(WTk[:], kv[:, :, 0, :])
                    nc.vector.tensor_copy(WTv[:, p % 2], kv[:, :, 1, :]).then_inc(s_tw, 1)

                def absorbed(g, p):
                    dve.wait_ge(s_abhi, (nth(g) * PAIRS + p + 1) * 2)
                    b = q_bank(g, "ab", p)
                    for h in range(2):
                        c = slice(64 * (1 - h), 64 * (1 - h) + CR)
                        last = nc.vector.tensor_tensor(A[:, p % 2, h, 1::2, c],
                                                       b[:, h * P:(h + 1) * P].rearrange("p (i c) -> p i c", i=2),
                                                       A[:, p % 2, h, 0::2, c].bitcast(F32), ALU.subtract)
                    last.then_inc(s_ablo, 1)

                def value_weights(g, p):
                    dve.wait_ge(s_wvohi, nth(g) * PAIRS + p + 1)
                    nc.vector.scalar_tensor_tensor(WVO[:, 1, p % PAIRS, :], q_bank(g, "wvo", p)[:], lnw[:, 2:3],
                                                   WVO[:, 0, p % PAIRS, :].bitcast(F32), ALU.mult,
                                                   ALU.subtract).then_inc(s_wvolo, 1)

                def rotary(g, pb):
                    if not (g is None and pb == 0):
                        dve.wait_ge(s_qlo, nth(g) * 16 + 2 * pb)
                    for n, (name, dst, table) in enumerate((("rot", SB2[:], 2), ("q0", QF[:, 0, :], 0),
                                                            ("q1", QF[:, 1, :], 1))):
                        dve.wait_ge(s_qp, nth(g) * 24 + 3 * pb + n + 1)
                        nc.vector.tensor_tensor(dst, q_bank(g, name, pb)[:], tables[:, table, :],
                                                ALU.mult).then_inc(s_rope, 1)

                def row_max(g, u, n):
                    dve.wait_ge(s_sc, nth(g) * 3 * UNITS + 3 * u + n + 1)
                    for q in ((3,), (2, 0), (1,))[n]:
                        o, N = SCORE[q][1], (q + 1) * P
                        ins = nc.vector.tensor_reduce(small[:, 0, u % 2, q:q + 1], bank[n][:, o:o + N],
                                                      mybir.AxisListType.X, ALU.max, negate=True)
                    ins.then_inc(s_mx, 1)

                def normalize(g, u):
                    r = u % 2
                    dve.wait_ge(s_exp, nth(g) * 4 * UNITS + 4 * (u + 1))
                    nc.vector.reciprocal(small[:, 3, r, :], small[:, 2, r, :]).then_inc(s_rcp, 1)
                    dve.wait_ge(s_rcp, nth(g) * UNITS + u + 1)
                    for q in range(4):
                        i, N = SCORE[q][2], (q + 1) * P
                        ins = nc.vector.tensor_scalar(PR[:, u % 4, i:i + N], PR[:, u % 4, i:i + N],
                                                      small[:, 3, r, q:q + 1], None, ALU.mult)
                    ins.then_inc(s_norm, 1)

                def values_lo(g, pb):
                    dve.wait_ge(s_othi, nth(g) * 2 * PAIRS + pb + 1)
                    p, b = pb // 2, pb % 2
                    c = slice(b * SEQ, (b + 1) * SEQ)
                    nc.vector.tensor_tensor(OT[:, 1, p, c], bank[5][:], OT[:, 0, p, c].bitcast(F32),
                                            ALU.subtract).then_inc(s_otlo, 1)

                work_of = {"turn": weights_turned, "wvo": value_weights, "queries": rotary,
                           "values": values_lo}

                def group(g, last):
                    for u in STEPS:
                        if ("absorb", u // 4 + 2) in fills(u, last):
                            absorbed(g, u // 4 + 2)
                        if u < UNITS or not last:
                            for n in range(3):
                                row_max(g, u, n)
                        if u <= UNITS or not last:
                            normalize(g, u - 1)
                        for work, i in fills(u, last):
                            if work in work_of:
                                work_of[work](g, i)
                    values_lo(g, UNITS // 2 - 1)
                    for t in range(TT):
                        dve.wait_ge(s_op, nth(g) * TT + t + 1)
                        nc.vector.tensor_tensor(xres[:, t, :], q_bank(g, "out", t)[:], xres[:, t, :],
                                                ALU.add).then_inc(s_xadd, 1)
                        if last and t >= 1:
                            dve.wait_ge(s_xadd, nth(g) * TT + t)
                            tile_stats(t - 1)
                    if last:
                        dve.wait_ge(s_xadd, (nth(g) + 1) * TT)
                        tile_stats(TT - 1)
                    if not last:
                        value_weights(g, PAIRS)
                        value_weights(g, PAIRS + 1)

                for p in range(2):
                    weights_turned(None, p)
                    absorbed(None, p)
                rotary(None, 0)
                rotary(None, 1)
                for n in range(3):
                    row_max(None, 0, n)
                rotary(None, 2)
                for n in range(3):
                    row_max(None, 1, n)
                normalize(None, 0)
                value_weights(None, 0)
                value_weights(None, 1)
                with dve.Fori(0, GROUPS - 1) as g:
                    group(g, False)
                group(GROUPS - 1, True)

            prep_weights()
            ffn(0)
            ln_stats(1, 2, XN2)
            latents()
            dve.wait_ge(s_tab, 16 * N_TABLES)
            attention()
            ln_stats(2, CT, XN)
            ffn(2)


def rope_tables():
    inv = (1.0 / np.float32(10000.0) ** (np.arange(0, ROPE, 2, dtype=np.float32) / np.float32(ROPE))).astype(np.float32)
    freqs = np.outer(np.arange(SEQ, dtype=np.float32), inv).astype(np.float32)
    cos, sin = np.cos(freqs).astype(np.float32), np.sin(freqs).astype(np.float32)
    tok = np.zeros((P, TT, 2, 32), np.float32)
    for t in range(TT):
        rows = slice((t * P) % SEQ, (t * P) % SEQ + P)
        tok[:, t, 0], tok[:, t, 1] = cos[rows], sin[rows]
    turned = np.ones((P, 3, SEQ), np.float32)
    turned *= np.float32(SCALE)
    cos, sin = cos * np.float32(SCALE), sin * np.float32(SCALE)
    turned[0:64, 0] = turned[64:128, 1] = np.concatenate([cos.T, cos.T])
    turned[0:64, 2] = turned[64:128, 2] = np.concatenate([-sin.T, sin.T])
    return tok, turned


def kernel(**inputs):
    import concourse.bacc as bacc
    from concourse.bass_utils import run_bass_kernel_spmd as run

    nc = bacc.Bacc("TRN2", target_bir_lowering=False, num_devices=1)
    tok, turned = rope_tables()
    named = [("x", np.ascontiguousarray(inputs["L0_attn_hidden_states"]).reshape(T, D))]
    for n in ("Wq_a", "q_a_ln_w", "Wq_b", "Wkv_a", "kv_a_ln_w", "Wkv_b", "Wo"):
        a = np.ascontiguousarray(inputs["L0_attn_" + n])
        named.append((n, a.reshape(-1, 1) if a.ndim == 1 else a))
    for n in ("gate_w", "up_w", "down_w", "gate_a", "gate_b", "up_a", "up_b", "down_a", "down_b"):
        named.append((n, np.ascontiguousarray(inputs["L0_ffn_" + n])))
    named += [("rope_tok", tok), ("rope_t", turned),
              ("mask", np.triu(np.full((P, P), MASKED, np.float32), 1))]
    args = [nc.dram_tensor("in_" + n, a.shape, F32, kind="ExternalInput").ap() for n, a in named]
    args.append(nc.dram_tensor("w_scratch", (HT, P, 6 * 512), F32, kind="Internal").ap())
    args.append(nc.dram_tensor("out", (T, D), F32, kind="ExternalOutput").ap())
    prog(nc, *args)
    r = run(nc, [{"in_" + n: a for n, a in named}], core_ids=[0])
    return r.results[0]["out"].reshape(2, SEQ, D)
```

```python
from contextlib import ExitStack

import numpy as np

import concourse.bass as bass
from concourse import mybir

F32 = mybir.dt.float32
F32R = mybir.dt.float32r
ALU = mybir.AluOpType
ACT = mybir.ActivationFunctionType

P = 128
D = 512
KD = D // P
T = 1024
TT = T // P
CH = 512
CT = CH // P
NC = T // CH
HID = 1376
HT = (HID + P - 1) // P
RANK = 16
LN_EPS = 1e-5
HEADS, NOPE, ROPE, VD = 32, 128, 64, 128
N_LNW = 7
QD = NOPE + ROPE
QR, CR = 192, 64
LAT = QR + CR + ROPE
SEQ = 512
QT4 = SEQ // P
PAIRS = 4
GROUPS = HEADS // 2 // PAIRS
UNITS = 4 * PAIRS
RMS_EPS = 1e-6
SCALE = float(QD) ** -0.5
MASKED = -1e30
SCORE = {3: (0, 0, 0), 2: (1, 0, 512), 0: (1, 384, 896), 1: (2, 0, 1024)}
TURNED = {0: (0, 0, 0), 1: (1, 0, 512), 3: (1, 384, 896), 2: (2, 0, 1024)}
TURNED_N = (512, 512, 256)
RAW = 4
ROWS_3 = (0, 32, 64)
LROWS = ROWS_3[2] + RANK
A_COLS = {"gate": 0, "up": D, "down": 2 * D}
B_COLS = {"gate": 0, "up": HID, "down": 2 * HID}
A_WIDTH, B_WIDTH = 2 * D + HID, 2 * HID + D
B_BLOCKS = {"gate": (0, HT, 0), "up": (HT, HT, 3), "down": (2 * HT, KD, 6)}


def fills(u, last):
    work = []
    if u % 4 == 2 and not (last and u >= 10):
        work.append(("turn", u // 4 + 2))
    if u % 4 == 0 and not (last and u >= 12):
        work.append(("absorb", u // 4 + 1))
    if u % 4 == 0 and u // 4 + 1 < PAIRS:
        work.append(("wvo", u // 4 + 1))
    if u % 2 == 0 and 4 <= u:
        work.append(("values", (u - 4) // 2))
    if u % 2 == 1 and not (last and u >= 13):
        work.append(("queries", (u + 3) // 2))
    return work


FIRST = 2
STEPS = range(FIRST, FIRST + UNITS)
RING_USES = {"turn": ("wq", "kv"), "absorb": ("ab",), "wvo": ("wvo",), "queries": ("q0", "q1"), "values": ()}


def q_ring():
    before = [("turn", 0), ("absorb", 0), ("turn", 1), ("absorb", 1), ("queries", 0), ("wvo", 0), ("wvo", 1),
              ("queries", 1), ("queries", 2)]
    first = [(n, i) for work, i in before for n in RING_USES[work]]
    body, last = ([(n, i) for u in STEPS for work, i in fills(u, is_last) for n in RING_USES[work]]
                  + [("out", t) for t in range(TT)] for is_last in (False, True))
    body += [("wvo", PAIRS), ("wvo", PAIRS + 1)]
    assert len(body) % 2 == 0
    return first, body, last


def slot(j):
    return HT - 1 - j


def b_banks():
    out = []
    for name, (_, count, b) in B_BLOCKS.items():
        width = HID if count == HT else D
        for q in range(0, width, 512):
            out.append((b + q // 512, B_COLS[name] + q, min(512, width - q)))
    return out


def rows_of(j):
    return min(P, HID - j * P)


def prog(nc, x_in, Wq_a, q_ln, Wq_b, Wkv_a, kv_ln, Wkv_b, Wo, gate_w, up_w, down_w, gate_a, gate_b, up_a, up_b,
         down_a, down_b, rope_tok, rope_t, mask_in, w_scratch, out):
    with ExitStack() as ctx:
        def sem(name):
            return ctx.enter_context(nc.semaphore(name))

        def sb(name, shape, dt=F32, where=ctx):
            return where.enter_context(nc.sbuf_tensor(name, shape, dt))

        bank = [ctx.enter_context(nc.psum_tensor(f"bank{i}", [P, 512], F32)) for i in range(8)]
        xres = sb("xres", [P, TT, D])
        ident = sb("ident", [P, P])
        stat6 = sb("stat6", [P, TT, 6])
        mean_var = sb("mean_var", [P, TT, 2])
        free_mark = sb("free_mark", [P, 1])
        wait_mark = sb("wait_mark", [P, 16])
        pool_mark = sb("pool_mark", [P, 1])
        lnw = sb("lnw", [P, 5])
        nhalf = sb("nhalf", [P, TT])
        rstd = sb("rstd", [P, TT])
        identr = sb("identr", [P, P], F32R)
        mask0 = sb("mask0", [P, P])
        mask = sb("mask", [P, 2, P], F32R)
        with ExitStack() as ffn:
            with ExitStack() as prep:
                raw_gu = sb("raw_gu", [P, RAW, 2, D], F32, prep)
                raw_d = sb("raw_d", [P, RAW, KD, P], F32, prep)
                a_stack = sb("a_stack", [LROWS, A_WIDTH], F32R, prep)
                b_stack = sb("b_stack", [LROWS, B_WIDTH], F32R, prep)
            x_turned = sb("x_turned", [P, 2, KD, CH], F32R, ffn)
            silu_out = sb("silu_out", [P, 2, CH], F32, ffn)
            hidden = sb("hidden", [P, 2, CH], F32, ffn)
            hidden_hi = sb("hidden_hi", [P, 2, CH], F32R, ffn)
            hidden_lo = sb("hidden_lo", [P, 2, CH], F32R, ffn)
            gap = sb("gap", [P, 16 * 256], F32, ffn)
            x_norm = sb("x_norm", [P, CT, D], F32, ffn)
            with ExitStack() as stage:
                lora_a = sb("lora_a", [RANK, A_WIDTH], F32, stage)
                b_copies = sb("b_copies", [P, 2 * HT + KD, LROWS], F32, stage)
            w_split = sb("w_split", [P, HT, 6, 512], F32R, ffn)
        with ExitStack() as att:
            with ExitStack() as lat:
                wa_split = sb("wa_split", [P, 2, KD, LAT], F32R, lat)
                latent_x = sb("latent_x", [P, 2, 2, KD, P], F32R, lat)
                latents_tok = sb("latents_tok", [P, 2, 4, P], F32, lat)
                x_norm_b = sb("x_norm_b", [P, CT, D], F32, lat)
                junk = sb("junk", [P, 256], F32, lat)
                ropes = sb("ropes", [P, 2, 4, 32], F32, lat)
                x_norm_a = sb("x_norm_a", [P, CT, D], F32, lat)
                wa_raw = sb("wa_raw", [P, KD, LAT], F32, lat)
            values_t = sb("values_t", [P, TT, 2, PAIRS, P], F32R, att)
            wvo_split = sb("wvo_split", [P, 2, PAIRS, D], F32R, att)
            qlat_0 = sb("qlat_0", [P, 2, T], F32R, att)
            qlat_1 = sb("qlat_1", [P, T], F32R, att)
            keys_t = sb("keys_t", [P, 2, 2, T], F32R, att)
            kv_lat = sb("kv_lat", [P, TT, CR], F32, att)
            tables = sb("tables", [P, 3, SEQ], F32, att)
            tok_table = sb("tok_table", [P, TT, 2, 32], F32, att)
            stat = sb("stat", [P, TT, 2], F32, att)
            small = sb("small", [P, 4, 2, 4], F32, att)
            rawq = sb("rawq", [P, 2, 2, 2, QD], F32, att)
            rawkv = sb("rawkv", [CR, 2, 2, 256], F32, att)
            rawo = sb("rawo", [VD, 2, 2, D], F32, att)
            wk_t = sb("wk_t", [P, 2, CR], F32, att)
            wv_t = sb("wv_t", [P, 2, 2, CR], F32, att)
            wq_t = sb("wq_t", [P, 2, 2, P], F32, att)
            q_weights = sb("q_weights", [P, 2, 2, 4, P], F32R, att)
            q_swap = sb("q_swap", [P, SEQ], F32, att)
            q_full = sb("q_full", [P, 2, SEQ], F32, att)
            q_hi = sb("q_hi", [P, 2, 2, SEQ], F32R, att)
            q_lo = sb("q_lo", [P, 2, 2, SEQ], F32R, att)
            probs = sb("probs", [P, 4, 1280], F32, att)
            probs_t = sb("probs_t", [P, 3, 1280], F32, att)

        s_x_loaded = sem("s_x_loaded")
        s_a_loaded = sem("s_a_loaded")
        s_b_loaded = sem("s_b_loaded")
        s_sa_cleared = sem("s_sa_cleared")
        s_mask_loaded = sem("s_mask_loaded")
        s_mask_ready = sem("s_mask_ready")
        s_ident_ready = sem("s_ident_ready")
        s_raw_loaded = [sem(f"s_raw_loaded{i}") for i in range(RAW)]
        s_b_turned = sem("s_b_turned")
        s_factor_steps = sem("s_factor_steps")
        s_a_hi = sem("s_a_hi")
        s_a_lo_down = sem("s_a_lo_down")
        s_short_tile_cleared = sem("s_short_tile_cleared")
        s_b_hi = sem("s_b_hi")
        s_b_lo = sem("s_b_lo")
        s_w_turned = sem("s_w_turned")
        s_w_hi = sem("s_w_hi")
        s_w_lo = sem("s_w_lo")
        s_mv_ready = [sem(f"s_mv_ready{n}") for n in range(3)]
        s_rstd_steps = [sem(f"s_rstd_steps{n}") for n in range(3)]
        s_x_normed = [sem(f"s_x_normed{n}") for n in range(3)]
        s_x_turned = [sem(f"s_x_turned{n}") for n in range(3)]
        s_x_hi = [sem(f"s_x_hi{n}") for n in range(3)]
        s_x_lo = [sem(f"s_x_lo{n}") for n in range(3)]
        s_gate_done = [sem("s_gate0"), None, sem("s_gate1")]
        s_up_done = [sem("s_up0"), None, sem("s_up1")]
        s_silu_done = [sem("s_silu0"), None, sem("s_silu1")]
        s_hidden_ready = [sem("s_mul0"), None, sem("s_mul1")]
        s_hidden_hi = [sem("s_hhi0"), None, sem("s_hhi1")]
        s_hidden_lo = [sem("s_hlo0"), None, sem("s_hlo1")]
        s_down_done = [sem("s_down0"), None, sem("s_down1")]
        s_y_added = [sem("s_y0"), None, sem("s_y1")]
        s_lnw_ones = sem("s_lnw_ones")
        s_tile_stats = sem("s_tile_stats")
        s_rotary_w_hi = sem("s_rotary_w_hi")
        s_dve_chain = sem("s_dve_chain")
        s_w_stored = sem("s_w_stored")
        s_w_reloaded = [sem(f"s_w_reloaded{j}") for j in range(HT)]
        s_tables_loaded = sem("s_tables_loaded")
        s_tok_loaded = sem("s_tok_loaded")
        s_lnw_loaded = sem("s_lnw_loaded")
        s_wa_loaded = sem("s_wa_loaded")
        s_wa_hi = sem("s_wa_hi")
        s_wa_lo = sem("s_wa_lo")
        s_latents_done = sem("s_latents_done")
        s_squares = sem("s_squares")
        s_mean_squares = sem("s_mean_squares")
        s_latent_rstd = sem("s_latent_rstd")
        s_latents_scaled = sem("s_latents_scaled")
        s_keys_roped = sem("s_keys_roped")
        s_latents_turned = sem("s_latents_turned")
        s_latents_hi = sem("s_latents_hi")
        s_latents_lo = sem("s_latents_lo")
        s_pair_loaded0 = sem("s_pair_loaded0")
        s_pair_loaded1 = sem("s_pair_loaded1")
        s_wo_loaded = [sem("s_rawo0"), sem("s_rawo1")]
        s_rotary_w_ready = sem("s_rotary_w_ready")
        s_pair_turned = sem("s_pair_turned")
        s_wkv_copied = sem("s_wkv_copied")
        s_wq_copied = sem("s_wq_copied")
        s_absorbed = sem("s_absorbed")
        s_wvo_done = sem("s_wvo_done")
        s_absorbed_hi = sem("s_absorbed_hi")
        s_absorbed_lo = sem("s_absorbed_lo")
        s_wvo_hi = sem("s_wvo_hi")
        s_wvo_lo = sem("s_wvo_lo")
        s_queries_done = sem("s_queries_done")
        s_q_swapped = sem("s_q_swapped")
        s_q_by_tables = sem("s_q_by_tables")
        s_q_roped = sem("s_q_roped")
        s_q_hi = sem("s_q_hi")
        s_q_lo = sem("s_q_lo")
        s_scores_ready = sem("s_scores_ready")
        s_max_ready = sem("s_max_ready")
        s_exp_done = sem("s_exp_done")
        s_recip_ready = sem("s_recip_ready")
        s_probs_ready = sem("s_probs_ready")
        s_probs_turned = sem("s_probs_turned")
        s_probs_copied = sem("s_probs_copied")
        s_values_done = sem("s_values_done")
        s_values_hi = sem("s_values_hi")
        s_values_lo = sem("s_values_lo")
        s_out_done = sem("s_out_done")
        s_x_added = sem("s_x_added")
        s_out_stored = sem("s_out_stored")

        def x_bank(n, c, t):
            if n == 0 and isinstance(c, int) and c == 0:
                return bank[(6, 7, 0, 1)[t]]
            return bank[(2 * ((HT - 2) % 2) + t) % 4]

        def prep_bank(j, i):
            return bank[3 * ((HT - j) % 2) + i]

        ring_first, ring_body, ring_last = q_ring()

        def ring_of(g):
            return ring_last if isinstance(g, int) else ring_body
        frees = {"kv": (s_wkv_copied, PAIRS, 1), "wq": (s_wq_copied, PAIRS, 1), "ab": (s_absorbed_lo, PAIRS, 1), "wvo": (s_wvo_lo, PAIRS, 1),
                 "q0": (s_q_by_tables, 24, 3), "q1": (s_q_by_tables, 24, 3), "out": (s_x_added, TT, 1)}

        def q_bank(g, *use):
            n = ring_first.index(use) if g is None else len(ring_first) + ring_of(g).index(use)
            return bank[6 + n % 2]

        def q_bank_free(pe, g, *use):
            before = ring_first if g is None else ring_first[-2:] + ring_of(g)
            n = before.index(use, 0 if g is None else 2) - 2
            if n < 0:
                return
            if g is not None and n < 2:
                pe.wait_ge(s_wvo_lo, nth(g) * PAIRS + 2)
                pe.wait_ge(s_q_by_tables, nth(g) * 24 + 9)
                return
            name, i = before[n]
            done, per_group, per_use = frees[name]
            count = per_use * i + (("q0", "q1").index(name) + 1 if per_use == 3 else 1)
            pe.wait_ge(done, nth(g) * per_group + count)

        def nth(g):
            return 0 if g is None else g

        block = ctx.enter_context(nc.Block())

        @block.sync
        def _(sp):
            sp.dma_start(mask0[:], mask_in).then_inc(s_mask_loaded, 16)
            for j in range(HT):
                p = rows_of(j)
                if j == 1:
                    sp.wait_ge(s_b_loaded, 16 * 5)
                if j >= RAW:
                    sp.wait_ge(s_w_turned, 3 * (j - RAW + 1))
                sp.dma_start(raw_gu[0:p, j % RAW, 0, :], gate_w[j * P:j * P + p]).then_inc(s_raw_loaded[j % RAW], 16)
                sp.dma_start(raw_gu[0:p, j % RAW, 1, :], up_w[j * P:j * P + p]).then_inc(s_raw_loaded[j % RAW], 16)
                sp.dma_start(raw_d[:, j % RAW, :, 0:p],
                             down_w[:, j * P:j * P + p].rearrange("(k q) h -> q k h", q=P)).then_inc(s_raw_loaded[j % RAW], 16)
                if j == RAW - 1:
                    sp.dma_start(xres[:], x_in.rearrange("(t p) d -> p t d", p=P)).then_inc(s_x_loaded, 16)

            sp.dma_start(lnw[:, 0:1], q_ln[0:P]).then_inc(s_lnw_loaded, 16)
            sp.dma_start(lnw[0:QR - P, 1:2], q_ln[P:QR]).then_inc(s_lnw_loaded, 16)
            sp.dma_start(lnw[QR - P:P, 1:2], q_ln[P:QR]).then_inc(s_lnw_loaded, 16)
            sp.wait_ge(s_lnw_ones, 1)
            for rows, col in ((slice(0, CR), 2), (slice(CR, P), 2), (slice(0, CR), 3), (slice(CR, P), 4)):
                sp.dma_start(lnw[rows, col:col + 1], kv_ln).then_inc(s_lnw_loaded, 16)
            for j in range(HT):
                if j == HT - 1:
                    sp.wait_ge(s_w_turned, 3 * HT)
                    sp.dma_start(wa_raw[:, :, 0:QR], Wq_a.rearrange("(k p) n -> p k n", p=P)).then_inc(s_wa_loaded, 16)
                    sp.dma_start(wa_raw[:, :, QR:LAT], Wkv_a.rearrange("(k p) n -> p k n", p=P)).then_inc(s_wa_loaded, 16)
                sp.wait_ge(s_w_lo, 3 * (j + 1))
                sp.dma_start(w_scratch[j], w_split[:, slot(j)].rearrange("p a n -> p (a n)").bitcast(F32)).then_inc(s_w_stored, 16)
            sp.wait_ge(s_w_stored, 16 * HT)
            sp.wait_ge(s_down_done[0], CT * NC * HT)
            sp.dma_start(tok_table[:], rope_tok).then_inc(s_tok_loaded, 16)
            sp.dma_start(tables[:], rope_t).then_inc(s_tables_loaded, 16)

            def load_pair(q, r):
                wq = Wq_b[:, bass.ds(q * 2 * QD, 2 * QD)].rearrange("r (h n) -> r h n", h=2)
                done = (s_pair_loaded0, s_pair_loaded1)[r]
                sp.dma_start(rawq[:, r, 0], wq[0:P]).then_inc(done, 16)
                sp.dma_start(rawq[0:QR - P, r, 1], wq[P:QR]).then_inc(done, 16)
                sp.dma_start(rawq[QR - P:P, r, 1], wq[P:QR]).then_inc(done, 16)
                sp.dma_start(rawkv[:, r], Wkv_b[:, bass.ds(q * 512, 512)].rearrange("c (h n) -> c h n", h=2)).then_inc(done, 16)

            def load_out(q, r):
                done = s_wo_loaded[r]
                sp.dma_start(rawo[:, r], Wo[bass.ds(q * 2 * VD, 2 * VD)].rearrange("(h v) n -> v h n", h=2)).then_inc(done, 16)

            load_pair(0, 0)
            load_pair(1, 1)
            load_out(0, 0)
            load_out(1, 1)
            with sp.Fori(0, HEADS // 4 - 1) as i:
                for r in range(2):
                    sp.wait_ge(s_pair_turned, 2 * (2 * i + r + 1))
                    sp.wait_ge(s_rotary_w_ready, 2 * i + r + 1)
                    load_pair(2 * i + r + 2, r)
                    sp.wait_ge(s_wvo_done, 2 * i + r + 1)
                    load_out(2 * i + r + 2, r)
            sp.wait_ge(s_values_done, 2 * PAIRS * GROUPS)
            for j in range(HT):
                sp.dma_start(w_split[:, slot(j)].rearrange("p a n -> p (a n)").bitcast(F32), w_scratch[j]).then_inc(s_w_reloaded[j], 16)
            o = out.rearrange("(t p) d -> p t d", p=P)
            for c in range(NC):
                sp.wait_ge(s_y_added[2], CT * (c + 2))
                sp.dma_start(o[:, CT * c:CT * (c + 1)], xres[:, CT * c:CT * (c + 1), :]).then_inc(s_out_stored, 16)
            sp.wait_ge(s_out_stored, 16 * NC)

        @block.gpsimd
        def _(pool):
            nc.gpsimd.memset(a_stack[:].bitcast(F32), 0.0).then_inc(s_sa_cleared, 1)
            nc.gpsimd.memset(nhalf[:], -0.5)
            nc.gpsimd.memset(lnw[:, 3:5], 1.0).then_inc(s_lnw_ones, 1)
            nc.gpsimd.memset(ident[:], 1.0).then_inc(s_ident_ready, 1)
            pool.wait_ge(s_ident_ready, 1)
            nc.gpsimd.affine_select(out=ident[:], in_=ident[:], compare_op=ALU.is_equal, fill=0.0, base=0,
                                    pattern=[[-1, P]], channel_multiplier=1).then_inc(s_ident_ready, 1)

            pool.wait_ge(s_ident_ready, 2)
            pool.wait_ge(s_mask_loaded, 16)
            nc.gpsimd.tensor_copy(identr[:], ident[:]).then_inc(s_mask_ready, 1)
            for i in range(2):
                nc.gpsimd.tensor_copy(mask[:, i, :], mask0[:]).then_inc(s_mask_ready, 1)
            pool.wait_ge(s_mask_ready, 3)
            pool.wait_ge(s_a_loaded, 16 * 3)
            pool.wait_ge(s_factor_steps, 6)
            c = slice(A_COLS["down"], A_WIDTH)
            nc.gpsimd.tensor_tensor(a_stack[ROWS_3[2]:LROWS, c], lora_a[:, c], a_stack[0:RANK, c].bitcast(F32),
                                    ALU.subtract).then_inc(s_a_lo_down, 1)
            pool.wait_ge(s_a_lo_down, 1)
            pool.wait_ge(s_b_turned, len(b_banks()))
            pool.wait_ge(s_factor_steps, 7)
            pool.wait_ge(s_a_hi, 1)
            nc.gpsimd.memset(w_split[:, slot(HT - 1)].bitcast(F32), 0.0).then_inc(s_short_tile_cleared, 1)

            def ln_rstd(n, c):
                pool.wait_ge(s_mv_ready[n], c + 1)
                half = rstd[:, c * CT:(c + 1) * CT]
                nc.gpsimd.tensor_scalar(half, mean_var[:, c * CT:(c + 1) * CT, 1], LN_EPS, None, ALU.add).then_inc(s_rstd_steps[n], 1)
                pool.wait_ge(s_rstd_steps[n], 2 * c + 1)
                nc.gpsimd.tensor_tensor(half, half, nhalf[:, 0:CT], ALU.pow).then_inc(s_rstd_steps[n], 1)
                pool.wait_ge(s_rstd_steps[n], 2 * c + 2)

            def normalized(n, t, dst):
                nc.gpsimd.tensor_scalar(dst, xres[:, t, :], mean_var[:, t, 0:1], rstd[:, t:t + 1],
                                        ALU.subtract, ALU.mult).then_inc(s_x_normed[n], 1)

            def second_half(n):
                ln_rstd(n, 1)
                pool.wait_ge(s_x_turned[n], CT)
                for t in range(CT):
                    normalized(n, CT + t, x_norm[:, t, :])

            def latents(rotary_weights):
                ln_rstd(1, 0)
                for t in range(CT):
                    normalized(1, t, x_norm_a[:, t, :])
                for t in range(TT):
                    pool.wait_ge(s_squares, 2 * (t + 1))
                    nc.gpsimd.tensor_scalar(stat[:, t, 0:1], stat[:, t, 0:1], 1.0 / QR, RMS_EPS, ALU.mult, ALU.add)
                    nc.gpsimd.tensor_scalar(stat[:, t, 1:2], stat[:, t, 1:2], 1.0 / CR, RMS_EPS, ALU.mult,
                                            ALU.add).then_inc(s_mean_squares, 1)
                    pool.wait_ge(s_mean_squares, t + 1)
                    nc.gpsimd.tensor_tensor(stat[:, t, :], stat[:, t, :], nhalf[:, 0:2], ALU.pow).then_inc(s_latent_rstd, 1)
                    if t == 1:
                        ln_rstd(1, 1)
                    if t in (2, 5):
                        rotary_weights(None, (t - 2) // 3)

            def attention():
                marks = [0]

                def carry_wait():
                    n = marks[0]
                    marks[0] += 1
                    nc.gpsimd.tensor_tensor(wait_mark[:, n:n + 1], nhalf[:, 0:1], nhalf[:, 0:1], ALU.mult)

                def rotary_weights(g, p):
                    pool.wait_ge((s_pair_loaded0, s_pair_loaded1)[p % 2], 64 * (nth(g) * 2 + p // 2 + 1))
                    carry_wait()
                    if p >= 2:
                        pool.wait_ge(s_queries_done, nth(g) * 16 + 4 * (p - 1))
                        carry_wait()
                    hi, lo = q_weights[:, p % 2, :, 0::2, :], q_weights[:, p % 2, :, 1::2, :]
                    for h in range(2):
                        c0 = 64 * h
                        for eo in range(2):
                            src = rawq[:, p % 2, :, h, NOPE + eo:QD:2]
                            at = c0 + 32 * eo
                            nc.gpsimd.tensor_copy(hi[:, h, :, at:at + 32], src)
                    nc.gpsimd.tensor_copy(pool_mark[:], nhalf[:, 0:1]).then_inc(s_rotary_w_hi, 1)
                    pool.wait_ge(s_rotary_w_hi, nth(g) * PAIRS + p + 1)
                    for h in range(2):
                        c0 = 64 * h
                        for eo in range(2):
                            src = rawq[:, p % 2, :, h, NOPE + eo:QD:2]
                            at = c0 + 32 * eo
                            last = nc.gpsimd.tensor_tensor(lo[:, h, :, at:at + 32], src,
                                                           hi[:, h, :, at:at + 32].bitcast(F32), ALU.subtract)
                    last.then_inc(s_rotary_w_ready, 1)

                def rotate(g, pb):
                    pool.wait_ge(s_q_by_tables, nth(g) * 24 + 3 * (pb + 1))
                    for h in range(2):
                        r = slice(64 * h, 64 * h + 64)
                        if h == 1:
                            pool.wait_ge(s_q_roped, nth(g) * 16 + 2 * pb + 1)
                        nc.gpsimd.tensor_tensor(q_full[r, h, :], q_full[r, h, :], q_swap[r, :], ALU.add).then_inc(s_q_roped, 1)
                    pool.wait_ge(s_q_roped, nth(g) * 16 + 2 * pb + 2)
                    for h in range(2):
                        pool.wait_ge(s_q_hi, nth(g) * 16 + 2 * pb + h + 1)
                        nc.gpsimd.tensor_tensor(q_lo[:, pb % 2, h, :], q_full[:, h, :], q_hi[:, pb % 2, h, :].bitcast(F32),
                                                ALU.subtract).then_inc(s_q_lo, 1)

                def group(g, last):
                    marks[0] = 4
                    for u in STEPS:
                        for work, i in fills(u, last):
                            if work == "turn":
                                rotary_weights(g, i)
                            if work == "queries":
                                rotate(g, i)

                latents(rotary_weights)
                for pb in range(3):
                    rotate(None, pb)
                with pool.Fori(0, GROUPS - 1) as g:
                    group(g, False)
                group(GROUPS - 1, True)

            ln_rstd(0, 0)
            second_half(0)
            attention()
            ln_rstd(2, 0)
            second_half(2)

        @block.tensor
        def _(pe):
            def turn_x(n, c, t):
                pe.wait_ge(s_x_normed[n], c * CT + t + 1)
                for k in range(KD):
                    mm = pe.matmul(x_bank(n, c, t)[:, k * P:(k + 1) * P], x_norm[:, t, k * P:(k + 1) * P], ident[:],
                                   start=(k == 0), stop=True, is_transpose=True, skip_group_check=True)
                mm.then_inc(s_x_turned[n], 1)

            def prep_weights():
                pe.wait_ge(s_b_loaded, 16 * 5)
                pe.wait_ge(s_factor_steps, 5)
                pe.wait_ge(s_ident_ready, 2)
                for first, count, b in B_BLOCKS.values():
                    for j in range(count):
                        p = rows_of(j)
                        mm = pe.matmul(bank[b + j // 4][0:LROWS, (j % 4) * P:(j % 4) * P + p], b_copies[0:p, first + j, :],
                                       ident[0:p, 0:p], start=(j % 4 == 0), stop=True, is_transpose=True,
                                       skip_group_check=True)
                        if j % 4 == 3 or j == count - 1:
                            mm.then_inc(s_b_turned, 1)
                for j in range(HT):
                    p = rows_of(j)
                    g, u, d = (prep_bank(j, i) for i in range(3))
                    pe.wait_ge(s_raw_loaded[j % RAW], 48 * (j // RAW + 1))
                    if j == HT - 1:
                        turn_x(0, 0, 0)
                        turn_x(0, 0, 1)
                        pe.wait_ge(s_w_lo, 3 * (HT - 1))
                        turn_x(0, 0, 2)
                        turn_x(0, 0, 3)
                    if j >= 2:
                        pe.wait_ge(s_w_lo, 3 * (j - 1))
                    elif j == 0:
                        pe.wait_ge(s_b_lo, 7)
                        pe.wait_ge(s_factor_steps, 7)
                        pe.wait_ge(s_a_hi, 1)
                        pe.wait_ge(s_a_lo_down, 1)
                    for i, b in enumerate((g, u)):
                        for k in range(KD):
                            pe.matmul(b[:, k * P:k * P + p], raw_gu[0:p, j % RAW, i, k * P:(k + 1) * P], ident[0:p, 0:p],
                                      start=(k == 0), stop=False, is_transpose=True, skip_group_check=True)
                    for k in range(KD):
                        pe.matmul(d[0:p, k * P:(k + 1) * P], raw_d[:, j % RAW, k, 0:p], ident[:],
                                  start=(k == 0), stop=False, is_transpose=True, skip_group_check=True)
                    for b, name in ((g, "gate"), (u, "up")):
                        for k in range(KD):
                            a0, b0 = A_COLS[name] + k * P, B_COLS[name] + j * P
                            mm = pe.matmul(b[:, k * P:k * P + p], a_stack[:, a0:a0 + P], b_stack[:, b0:b0 + p],
                                           start=False, stop=True, skip_group_check=True)
                        mm.then_inc(s_w_turned, 1)
                    a0, b0 = A_COLS["down"] + j * P, B_COLS["down"]
                    pe.matmul(d[0:p, :], a_stack[:, a0:a0 + p], b_stack[:, b0:b0 + D], start=False, stop=True,
                              skip_group_check=True).then_inc(s_w_turned, 1)

            def gate_up(n, c, j):
                p = rows_of(j)
                if n == 2:
                    pe.wait_ge(s_w_reloaded[j], 16)
                if n == 0 and j == 1:
                    pe.wait_ge(s_w_lo, 3 * HT)
                if j >= 2:
                    pe.wait_ge(s_hidden_ready[n], c * HT + j - 1)
                for i, done in enumerate((s_gate_done[n], s_up_done[n])):
                    b = bank[2 * (j % 2) + i]
                    for k in range(KD):
                        for w, x in ((0, 0), (0, 1), (1, 0)):
                            mm = pe.matmul(b[0:p, :], w_split[:, slot(j), 2 * i + w, k * P:k * P + p], x_turned[:, x, k, :],
                                           start=(k == 0 and w == 0 and x == 0), stop=(k == KD - 1 and w == 1))
                    mm.then_inc(done, 1)

            def down(n, c, j):
                p = rows_of(j)
                pe.wait_ge(s_hidden_lo[n], c * HT + j + 1)
                if j == 0:
                    pe.wait_ge(s_y_added[n], (c + 1) * CT)
                for t in range(CT):
                    for h, w in ((hidden_hi, 4), (hidden_hi, 5), (hidden_lo, 4)):
                        mm = pe.matmul(bank[4 + t][:], h[0:p, j % 2, t * P:(t + 1) * P], w_split[0:p, slot(j), w, :],
                                       start=(j == 0 and h is hidden_hi and w == 4), stop=(j == HT - 1 and h is hidden_lo))
                    mm.then_inc(s_down_done[n], 1)

            def turn_latent_x(t):
                pe.wait_ge(s_x_normed[1], t + 1)
                if t >= 2:
                    pe.wait_ge(s_x_lo[1], t - 1)
                for k in range(KD):
                    src = (x_norm_a, x_norm_b)[t // CT]
                    mm = pe.matmul(bank[t % 2][:, k * P:(k + 1) * P], src[:, t % CT, k * P:(k + 1) * P], ident[:],
                                   start=(k == 0), stop=True, is_transpose=True, skip_group_check=True)
                mm.then_inc(s_x_turned[1], 1)

            def chunk(n, c, last):
                pe.wait_ge(s_x_lo[n], (c + 1) * CT)
                gate_up(n, c, 0)
                for j in range(1, HT):
                    gate_up(n, c, j)
                    if j == HT - 1 and not last:
                        pe.wait_ge(s_hidden_ready[n], c * HT + HT - 1)
                        turn_x(n, c + 1, 0)
                        turn_x(n, c + 1, 1)
                    down(n, c, j - 1)
                if not last:
                    pe.wait_ge(s_hidden_ready[n], (c + 1) * HT)
                    turn_x(n, c + 1, 2)
                    turn_x(n, c + 1, 3)
                elif n == 0:
                    pe.wait_ge(s_hidden_ready[0], NC * HT)
                    turn_latent_x(0)
                    turn_latent_x(1)
                down(n, c, HT - 1)

            def ffn(n):
                with pe.Fori(0, NC - 1) as c:
                    chunk(n, c, False)
                chunk(n, NC - 1, True)

            def latents(first_weights):
                def project(t):
                    pe.wait_ge(s_x_lo[1], t + 1)
                    if t == 0:
                        pe.wait_ge(s_wa_lo, 1)
                    if t >= 2:
                        pe.wait_ge(s_latents_scaled, 3 * (t - 1))
                        pe.wait_ge(s_keys_roped, t - 1)
                    for k in range(KD):
                        for x, w in ((0, 0), (0, 1), (1, 0)):
                            mm = pe.matmul(bank[2 + t % 2][:, 0:LAT], latent_x[:, t % 2, x, k, :], wa_split[:, w, k, :],
                                           start=(k == 0 and x == 0 and w == 0), stop=(k == KD - 1 and x == 1))
                    mm.then_inc(s_latents_done, 1)

                def turn_latents(t):
                    pe.wait_ge(s_latents_scaled, 3 * (t + 1))
                    pe.wait_ge(s_keys_roped, t + 1)
                    if t >= 2:
                        pe.wait_ge(s_latents_lo, 4 * (t - 1))
                    if t == 0:
                        pe.wait_ge(s_y_added[0], CT * (NC + 1))
                    for k in range(4):
                        mm = pe.matmul(bank[4 + t % 2][:, k * P:(k + 1) * P], latents_tok[:, t % 2, k, :], ident[:],
                                       start=(k == 0), stop=True, is_transpose=True, skip_group_check=True)
                    mm.then_inc(s_latents_turned, 1)

                for t in range(1, TT + 3):
                    if 2 <= t < TT:
                        turn_latent_x(t)
                    if t >= 3:
                        turn_latents(t - 3)
                    if 1 <= t <= TT:
                        project(t - 1)
                    first_weights(t)

            def attention():
                def turn_weights(g, p):
                    r = p % 2
                    pe.wait_ge((s_pair_loaded0, s_pair_loaded1)[p % 2], 64 * (nth(g) * 2 + p // 2 + 1))
                    q_bank_free(pe, g, "wq", p)
                    q_bank_free(pe, g, "kv", p)
                    b = q_bank(g, "wq", p)
                    for h in range(2):
                        for i in range(2):
                            n = 2 * h + i
                            mm = pe.matmul(b[:, n * P:(n + 1) * P], rawq[:, r, i, h, 0:NOPE], ident[:],
                                           start=(n == 0), stop=True, is_transpose=True, skip_group_check=True)
                    mm.then_inc(s_pair_turned, 1)
                    b = q_bank(g, "kv", p)
                    for h in range(2):
                        for kv in range(2):
                            i = 2 * h + kv
                            mm = pe.matmul(b[:, i * CR:(i + 1) * CR], rawkv[:, r, h, kv * P:(kv + 1) * P],
                                           ident[0:CR, 0:CR], start=(i == 0), stop=True, is_transpose=True,
                                           skip_group_check=True)
                    mm.then_inc(s_pair_turned, 1)

                def absorb(g, p):
                    pe.wait_ge(s_wkv_copied, nth(g) * PAIRS + p + 1)
                    pe.wait_ge(s_wq_copied, nth(g) * PAIRS + p + 1)
                    q_bank_free(pe, g, "ab", p)
                    b = q_bank(g, "ab", p)
                    for h in range(2):
                        for i in range(2):
                            n = 2 * h + i
                            mm = pe.matmul(b[:, n * CR:(n + 1) * CR], wq_t[:, h, i, :], wk_t[:, h, :],
                                           start=True, stop=True)
                    mm.then_inc(s_absorbed, 1)

                def value_weights(g, p):
                    q_bank_free(pe, g, "wvo", p)
                    pe.wait_ge(s_wo_loaded[p % 2], 16 * (nth(g) * 2 + p // 2 + 1))
                    b = q_bank(g, "wvo", p)
                    for h in range(2):
                        mm = pe.matmul(b[64 * h:64 * h + 64, :], wv_t[:, p % 2, h, :], rawo[:, p % 2, h, :],
                                       start=True, stop=True)
                    mm.then_inc(s_wvo_done, 1)

                def queries(g, pb):
                    p, b = pb // 2, pb % 2
                    c = slice(b * SEQ, (b + 1) * SEQ)
                    if b == 0:
                        pe.wait_ge(s_absorbed_lo, nth(g) * PAIRS + p + 1)
                        pe.wait_ge(s_rotary_w_ready, nth(g) * PAIRS + p + 1)
                    for tile, name in enumerate(("q0", "q1")):
                        q_bank_free(pe, g, name, pb)
                        o = q_bank(g, name, pb)
                        w = q_weights[:, p % 2, tile]
                        pe.matmul(o[:], w[:, 0], qlat_0[:, 0, c], start=True, stop=False)
                        pe.matmul(o[:], w[:, 0], qlat_0[:, 1, c], start=False, stop=False)
                        pe.matmul(o[:], w[:, 1], qlat_0[:, 0, c], start=False, stop=False)
                        pe.matmul(o[:], w[:, 2], qlat_1[:, c], start=False, stop=False)
                        pe.matmul(o[:], w[0:64, 3], qlat_1[0:64, c], start=False, stop=True).then_inc(s_queries_done, 1)

                def scores(g, u, n):
                    pb, h = u // 2, u % 2
                    b = pb % 2
                    if n == 0:
                        pe.wait_ge(s_q_lo, nth(g) * 16 + u + 1)
                    k = keys_t[:, :, 1 - h, b * SEQ:(b + 1) * SEQ]
                    if not (g is None and u == 0):
                        pe.wait_ge(s_exp_done, nth(g) * 4 * UNITS + 4 * (u - 1) + (1, 3, 4)[n])
                    for q in ((3,), (2, 0), (1,))[n]:
                        o, N = SCORE[q][1], (q + 1) * P
                        s = bank[n]
                        qs = slice(q * P, (q + 1) * P)
                        for x, w in ((q_hi, 0), (q_hi, 1), (q_lo, 0)):
                            pe.matmul(s[:, o:o + N], x[:, pb % 2, h, qs], k[:, w, 0:N],
                                      start=(o == 0 and x is q_hi and w == 0), stop=False, skip_group_check=True)
                    n_diag = 2 if n == 1 else 1
                    pe.matmul(s[:, o + N - n_diag * P:o + N], identr[:], mask[:, 0:n_diag, :].rearrange("p a n -> p (a n)"),
                              start=False, stop=True, skip_group_check=True).then_inc(s_scores_ready, 1)

                def turn_probs(g, u, n):
                    if n == 0:
                        pe.wait_ge(s_probs_ready, nth(g) * UNITS + u + 1)
                    m = 3 * u + n
                    if not (g is None or (u == 0 and n < 2)):
                        pe.wait_ge(s_probs_copied, nth(g) * 3 * UNITS + m - 1)
                    blocks = ((0,), (1, 3), (2,))[n]
                    for k in blocks:
                        for q in range(k, 4):
                            o = TURNED[k][1] + (q - k) * P
                            i = SCORE[q][2] + k * P
                            mm = pe.matmul(bank[3 + m % 2][:, o:o + P], probs[:, u % 4, i:i + P], ident[:],
                                           start=(k == blocks[0] and q == k), stop=True, is_transpose=True,
                                           skip_group_check=True)
                    mm.then_inc(s_probs_turned, 1)

                def values(g, pb):
                    b = pb % 2
                    if pb >= 1:
                        pe.wait_ge(s_values_lo, nth(g) * 2 * PAIRS + pb)
                    for k in (0, 1, 3, 2):
                        for h in range(2):
                            if k != 3:
                                pe.wait_ge(s_probs_copied, nth(g) * 3 * UNITS + 3 * (2 * pb + 1) + (1, 2, 3)[k])
                            i, N = TURNED[k][2], SEQ - k * P
                            mm = pe.matmul(bank[5][64 * h:64 * h + 64, k * P:SEQ], kv_lat[:, 4 * b + k, :],
                                           probs_t[:, (2 * pb + h) % 3, i:i + N], start=(k == 0), stop=(k == 2),
                                           skip_group_check=True)
                    mm.then_inc(s_values_done, 1)

                def out_product(g, last):
                    for t in range(TT):
                        if last and t == TT - 1:
                            for i in range(CT):
                                turn_x(2, 0, i)
                        if t % 4 == 0:
                            pe.wait_ge(s_values_lo, (nth(g) + 1) * 2 * PAIRS - 1 + t // 4)
                        q_bank_free(pe, g, "out", t)
                        o = q_bank(g, "out", t)
                        for p in range(PAIRS):
                            for a, w in ((0, 0), (0, 1), (1, 0)):
                                mm = pe.matmul(o[:], values_t[:, t, a, p, :], wvo_split[:, w, p, :],
                                               start=(p == 0 and a == 0 and w == 0),
                                               stop=(p == PAIRS - 1 and a == 1))
                        mm.then_inc(s_out_done, 1)

                work_of = {"turn": turn_weights, "absorb": absorb, "wvo": value_weights, "queries": queries,
                           "values": values}

                def group(g, last):
                    for u in STEPS:
                        for n in range(3):
                            if u < UNITS or not last:
                                scores(g, u, n)
                            turn_probs(g, u - 2, n)
                        for work, i in fills(u, last):
                            if work in work_of:
                                work_of[work](g, i)
                    values(g, UNITS // 2 - 1)
                    out_product(g, last)
                    if not last:
                        value_weights(g, PAIRS)
                        value_weights(g, PAIRS + 1)

                def first_weights(t):
                    if t in (3, 5):
                        turn_weights(None, (t - 3) // 2)
                    if t in (4, 6):
                        absorb(None, (t - 4) // 2)
                    if t == TT:
                        pe.wait_ge(s_latents_lo, 4 * QT4)
                        queries(None, 0)
                    if t >= TT + 1:
                        value_weights(None, t - TT - 1)

                latents(first_weights)
                pe.wait_ge(s_latents_lo, 4 * TT)
                pe.wait_ge(s_mask_ready, 3)
                queries(None, 1)
                for u in range(2):
                    for n in range(3):
                        scores(None, u, n)
                queries(None, 2)
                with pe.Fori(0, GROUPS - 1) as g:
                    group(g, False)
                group(GROUPS - 1, True)

            prep_weights()
            ffn(0)
            attention()
            ffn(2)

        @block.scalar
        def _(act):
            def inputs_hi(n, c):
                for t in range(CT):
                    act.wait_ge(s_x_turned[n], c * CT + t + 1)
                    nc.scalar.copy(x_turned[:, 0, :, t * P:(t + 1) * P],
                                   x_bank(n, c, t)[:].rearrange("q (k h) -> q k h", k=KD)).then_inc(s_x_hi[n], 1)

            def prep_weights():
                full = (HT - 1) * P
                for src, name in ((gate_b, "gate"), (up_b, "up")):
                    f = B_BLOCKS[name][0]
                    act.dma_start(b_copies[:, f:f + HT - 1, 0:RANK],
                                  src[0:full].rearrange("(j p) r -> p j r", p=P)).then_inc(s_b_loaded, 16)
                    act.dma_start(b_copies[0:HID - full, f + HT - 1, 0:RANK], src[full:HID]).then_inc(s_b_loaded, 16)
                act.dma_start(b_copies[:, 2 * HT:, 0:RANK], down_b.rearrange("(k p) r -> p k r", p=P)).then_inc(s_b_loaded, 16)
                for src, name in ((gate_a, "gate"), (up_a, "up"), (down_a, "down")):
                    c = A_COLS[name]
                    act.dma_start(lora_a[:, c:c + src.shape[1]], src).then_inc(s_a_loaded, 16)
                act.wait_ge(s_a_loaded, 16 * 3)
                act.wait_ge(s_sa_cleared, 1)
                nc.scalar.copy(a_stack[ROWS_3[1]:ROWS_3[1] + RANK, :], lora_a[:]).then_inc(s_a_hi, 1)
                for i, (b, c, n) in enumerate(b_banks()):
                    act.wait_ge(s_b_turned, i + 1)
                    nc.scalar.copy(b_stack[:, c:c + n], bank[b][0:LROWS, 0:n]).then_inc(s_b_hi, 1)
                for j in range(HT):
                    p = rows_of(j)
                    if j == HT - 1:
                        inputs_hi(0, 0)
                    for i in range(3):
                        act.wait_ge(s_w_turned, 3 * j + i + 1)
                        if j == HT - 1:
                            act.wait_ge(s_short_tile_cleared, 1)
                        b = prep_bank(j, i)
                        if i < 2:
                            nc.scalar.copy(w_split[:, slot(j), 2 * i, :].rearrange("q (k h) -> q k h", k=KD)[:, :, 0:p],
                                           b[:].rearrange("q (k h) -> q k h", k=KD)[:, :, 0:p]).then_inc(s_w_hi, 1)
                        else:
                            nc.scalar.copy(w_split[0:p, slot(j), 4, :], b[0:p, :]).then_inc(s_w_hi, 1)

            def latent_inputs_hi(t):
                act.wait_ge(s_x_turned[1], t + 1)
                if t >= 2:
                    act.wait_ge(s_latents_done, t - 1)
                nc.scalar.copy(latent_x[:, t % 2, 0], bank[t % 2][:].rearrange("q (k h) -> q k h", k=KD)).then_inc(s_x_hi[1], 1)

            def chunk(n, c, last):
                for j in range(HT):
                    p = rows_of(j)
                    act.wait_ge(s_gate_done[n], c * HT + j + 1)
                    if j >= 2:
                        act.wait_ge(s_hidden_ready[n], c * HT + j - 1)
                    nc.scalar.activation(silu_out[0:p, j % 2, :], bank[2 * (j % 2)][0:p, :], ACT.Silu).then_inc(s_silu_done[n], 1)
                if not last:
                    inputs_hi(n, c + 1)
                elif n == 0:
                    act.wait_ge(s_up_done[0], NC * HT)
                    act.wait_ge(s_wa_loaded, 32)
                    nc.scalar.copy(wa_split[:, 0], wa_raw[:]).then_inc(s_wa_hi, 1)
                    latent_inputs_hi(0)
                    latent_inputs_hi(1)

            def ffn(n):
                if n == 2:
                    inputs_hi(n, 0)
                with act.Fori(0, NC - 1) as c:
                    chunk(n, c, False)
                chunk(n, NC - 1, True)

            def latents(first_weights):
                act.wait_ge(s_lnw_loaded, 16 * N_LNW)

                def squares(t):
                    act.wait_ge(s_latents_done, t + 1)
                    b = bank[2 + t % 2]
                    nc.scalar.activation(junk[:, 0:QR], b[:, 0:QR], ACT.Square, accum_out=stat[:, t, 0:1]).then_inc(s_squares, 1)
                    nc.scalar.activation(junk[:, QR:QR + CR], b[:, QR:QR + CR], ACT.Square,
                                         accum_out=stat[:, t, 1:2]).then_inc(s_squares, 1)

                def scaled(t):
                    act.wait_ge(s_latent_rstd, t + 1)
                    if t >= 2:
                        act.wait_ge(s_latents_turned, t - 1)
                    b = bank[2 + t % 2]
                    q = latents_tok[:, t % 2].rearrange("p a n -> p (a n)")
                    nc.scalar.activation(q[:, 0:QR], b[:, 0:QR], ACT.Copy, scale=stat[:, t, 0:1]).then_inc(s_latents_scaled, 1)
                    nc.scalar.activation(q[:, QR:2 * P], b[:, P:QR], ACT.Copy, scale=stat[:, t, 0:1]).then_inc(s_latents_scaled, 1)
                    nc.scalar.activation(kv_lat[:, t, :], b[:, QR:QR + CR], ACT.Copy, scale=stat[:, t, 1:2]).then_inc(s_latents_scaled, 1)

                def turned(t):
                    act.wait_ge(s_latents_turned, t + 1)
                    b = bank[4 + t % 2]
                    c = slice(t * P, (t + 1) * P)
                    nc.scalar.activation(qlat_0[:, 0, c], b[:, 0:P], ACT.Copy, scale=lnw[:, 0:1]).then_inc(s_latents_hi, 1)
                    nc.scalar.activation(qlat_1[:, c], b[:, P:2 * P], ACT.Copy, scale=lnw[:, 1:2]).then_inc(s_latents_hi, 1)
                    for a in range(2):
                        nc.scalar.activation(keys_t[:, 0, a, c], b[:, (2 + a) * P:(3 + a) * P], ACT.Copy,
                                             scale=lnw[:, 3 + a:4 + a]).then_inc(s_latents_hi, 1)

                for t in range(1, TT + 3):
                    if 2 <= t < TT:
                        latent_inputs_hi(t)
                    if 2 <= t < TT + 2:
                        scaled(t - 2)
                    if t >= 3:
                        turned(t - 3)
                    if 1 <= t <= TT:
                        squares(t - 1)
                    first_weights(t)

            def attention():
                def absorbed(g, p):
                    act.wait_ge(s_absorbed, nth(g) * PAIRS + p + 1)
                    b = q_bank(g, "ab", p)
                    for h in range(2):
                        nc.scalar.copy(q_weights[:, p % 2, h, 0::2, 64 * (1 - h):64 * (1 - h) + CR],
                                       b[:, h * P:(h + 1) * P].rearrange("p (i c) -> p i c", i=2)).then_inc(s_absorbed_hi, 1)

                def value_weights(g, p):
                    act.wait_ge(s_wvo_done, nth(g) * PAIRS + p + 1)
                    nc.scalar.activation(wvo_split[:, 0, p % PAIRS, :], q_bank(g, "wvo", p)[:], ACT.Copy,
                                         scale=lnw[:, 2:3]).then_inc(s_wvo_hi, 1)

                def weights_turned(g, p):
                    act.wait_ge(s_pair_turned, (nth(g) * PAIRS + p) * 2 + 1)
                    nc.scalar.copy(wq_t[:].rearrange("p h i r -> p (h i r)"), q_bank(g, "wq", p)[:]).then_inc(s_wq_copied, 1)

                def swapped(g, pb):
                    for h, name in enumerate(("q0", "q1")):
                        act.wait_ge(s_queries_done, nth(g) * 16 + 2 * pb + h + 1)
                        if h == 0 and not (g is None and pb == 0):
                            act.wait_ge(s_q_roped, nth(g) * 16 + 2 * pb)
                        b = q_bank(g, name, pb)
                        for i in range(2):
                            dst, src = 64 * h + 32 * i, 64 * h + 32 * (1 - i)
                            ins = nc.scalar.copy(q_swap[dst:dst + 32, :], b[src:src + 32, :])
                        ins.then_inc(s_q_swapped, 1)

                def queries_hi(g, pb):
                    for h in range(2):
                        act.wait_ge(s_q_roped, nth(g) * 16 + 2 * pb + h + 1)
                        nc.scalar.copy(q_hi[:, pb % 2, h, :], q_full[:, h, :]).then_inc(s_q_hi, 1)

                def exponentials(g, u, n):
                    act.wait_ge(s_max_ready, nth(g) * 3 * UNITS + 3 * u + n + 1)
                    for q in ((3,), (2, 0), (1,))[n]:
                        _, o, i = SCORE[q]
                        N = (q + 1) * P
                        nc.scalar.activation(probs[:, u % 4, i:i + N], bank[n][:, o:o + N], ACT.Exp,
                                             bias=small[:, 0, u % 2, q:q + 1], scale=1.0,
                                             accum_out=small[:, 2, u % 2, q:q + 1]).then_inc(s_exp_done, 1)

                def probs_turned(g, u, n):
                    m = 3 * u + n
                    act.wait_ge(s_probs_turned, nth(g) * 3 * UNITS + m + 1)
                    i, N = (0, 512, 1024)[n], TURNED_N[n]
                    nc.scalar.copy(probs_t[:, u % 3, i:i + N], bank[3 + m % 2][:, 0:N]).then_inc(s_probs_copied, 1)

                def values_hi(g, pb):
                    act.wait_ge(s_values_done, nth(g) * 2 * PAIRS + pb + 1)
                    p, b = pb // 2, pb % 2
                    nc.scalar.copy(values_t[:, QT4 * b:QT4 * (b + 1), 0, p, :],
                                   bank[5][:].rearrange("p (t n) -> p t n", t=QT4)).then_inc(s_values_hi, 1)

                work_of = {"turn": weights_turned, "absorb": absorbed, "wvo": value_weights, "queries": swapped, "values": values_hi}

                def group(g, last):
                    for u in STEPS:
                        for n in range(3):
                            probs_turned(g, u - 2, n)
                        for n in range(3):
                            if u < UNITS or not last:
                                exponentials(g, u, n)
                        if u % 2 == 0 and ("queries", u // 2 + 1) in (fills(u - 1, last) if u > 2 else [("queries", 2)]):
                            queries_hi(g, u // 2 + 1)
                        for work, i in fills(u, last):
                            if work in work_of:
                                work_of[work](g, i)
                    values_hi(g, UNITS // 2 - 1)
                    if not last:
                        value_weights(g, PAIRS)
                        value_weights(g, PAIRS + 1)

                def first_weights(t):
                    if t in (3, 5):
                        weights_turned(None, (t - 3) // 2)
                    if t in (4, 6):
                        absorbed(None, (t - 4) // 2)
                    if t == TT:
                        swapped(None, 0)
                    if t >= TT + 1:
                        value_weights(None, t - TT - 1)

                latents(first_weights)
                queries_hi(None, 0)
                swapped(None, 1)
                for n in range(3):
                    exponentials(None, 0, n)
                queries_hi(None, 1)
                for n in range(3):
                    exponentials(None, 1, n)
                swapped(None, 2)
                with act.Fori(0, GROUPS - 1) as g:
                    group(g, False)
                group(GROUPS - 1, True)

            prep_weights()
            ffn(0)
            attention()
            ffn(2)

        @block.vector
        def _(dve):
            link_count = [0]

            def link(ins):
                link_count[0] += 1
                ins.then_inc(s_dve_chain, 1)
                dve.wait_ge(s_dve_chain, link_count[0])

            def tile_stats(t):
                nc.vector.bn_stats(stat6[:, t, :], xres[:, t, :]).then_inc(s_tile_stats, 1)

            def half_stats(m, first):
                dve.wait_ge(s_tile_stats, TT * m + first + CT)
                for t in range(CT):
                    if isinstance(first, int):
                        ins = nc.vector.bn_aggr(mean_var[:, first + t, :], stat6[:, first + t, :])
                    else:
                        ins = nc.vector.bn_aggr(mean_var[:, bass.ds(first + t, 1), :], stat6[:, bass.ds(first + t, 1), :])
                ins.then_inc(s_mv_ready[m], 1)

            def normalize_tiles(n):
                dve.wait_ge(s_rstd_steps[n], 2)
                for t in range(CT):
                    nc.vector.tensor_scalar(x_norm[:, t, :], xres[:, t, :], mean_var[:, t, 0:1], rstd[:, t:t + 1],
                                            ALU.subtract, ALU.mult).then_inc(s_x_normed[n], 1)

            def inputs_lo(n, c):
                for t in range(CT):
                    dve.wait_ge(s_x_hi[n], c * CT + t + 1)
                    nc.vector.tensor_tensor(x_turned[:, 1, :, t * P:(t + 1) * P],
                                            x_bank(n, c, t)[:].rearrange("q (k h) -> q k h", k=KD),
                                            x_turned[:, 0, :, t * P:(t + 1) * P].bitcast(F32),
                                            ALU.subtract).then_inc(s_x_lo[n], 1)

            def prep_weights():
                for c in ROWS_3[:2]:
                    nc.vector.memset(b_copies[:, :, c + RANK:c + 2 * RANK], 0.0).then_inc(s_factor_steps, 1)
                nc.vector.memset(b_copies[rows_of(HT - 1):P, HT - 1:2 * HT:HT, 0:RANK], 0.0).then_inc(s_factor_steps, 1)
                dve.wait_ge(s_factor_steps, 3)
                dve.wait_ge(s_b_loaded, 16 * 5)
                for c in ROWS_3[1:]:
                    nc.vector.tensor_copy(b_copies[:, :, c:c + RANK], b_copies[:, :, 0:RANK]).then_inc(s_factor_steps, 1)
                dve.wait_ge(s_a_loaded, 16 * 3)
                dve.wait_ge(s_sa_cleared, 1)
                nc.vector.tensor_copy(a_stack[0:RANK, :], lora_a[:]).then_inc(s_factor_steps, 1)
                dve.wait_ge(s_factor_steps, 6)
                c = slice(0, A_COLS["down"])
                nc.vector.tensor_tensor(a_stack[ROWS_3[2]:LROWS, c], lora_a[:, c], a_stack[0:RANK, c].bitcast(F32),
                                        ALU.subtract).then_inc(s_factor_steps, 1)
                for i, (b, c, n) in enumerate(b_banks()):
                    dve.wait_ge(s_b_hi, i + 1)
                    r = slice(ROWS_3[1], ROWS_3[1] + RANK)
                    nc.vector.tensor_tensor(b_stack[r, c:c + n], bank[b][r, 0:n], b_stack[r, c:c + n].bitcast(F32),
                                            ALU.subtract).then_inc(s_b_lo, 1)
                for j in range(HT):
                    p = rows_of(j)
                    if j == HT - 1:
                        dve.wait_ge(s_w_turned, 3 * HT)
                        inputs_lo(0, 0)
                    for i in range(3):
                        dve.wait_ge(s_w_hi, 3 * j + i + 1)
                        b = prep_bank(j, i)
                        if i < 2:
                            v = [a.rearrange("q (k h) -> q k h", k=KD)[:, :, 0:p]
                                 for a in (w_split[:, slot(j), 2 * i + 1, :], b[:], w_split[:, slot(j), 2 * i, :].bitcast(F32))]
                        else:
                            v = [w_split[0:p, slot(j), 5, :], b[0:p, :], w_split[0:p, slot(j), 4, :].bitcast(F32)]
                        nc.vector.tensor_tensor(*v, ALU.subtract).then_inc(s_w_lo, 1)
                    if j == RAW - 1:
                        dve.wait_ge(s_x_loaded, 16)
                    if RAW - 1 <= j < RAW - 1 + CT:
                        tile_stats(j - RAW + 1)
                    if j == RAW - 1 + CT:
                        half_stats(0, 0)
                    if j == HT - 2:
                        normalize_tiles(0)

            def latent_inputs_lo(t):
                dve.wait_ge(s_x_hi[1], t + 1)
                nc.vector.tensor_tensor(latent_x[:, t % 2, 1], bank[t % 2][:].rearrange("q (k h) -> q k h", k=KD),
                                        latent_x[:, t % 2, 0].bitcast(F32), ALU.subtract).then_inc(s_x_lo[1], 1)

            def chunk(n, c, last):
                for j in range(HT):
                    p = rows_of(j)
                    r = j % 2
                    dve.wait_ge(s_silu_done[n], c * HT + j + 1)
                    dve.wait_ge(s_up_done[n], c * HT + j + 1)
                    nc.vector.tensor_tensor(hidden[0:p, r, :], bank[2 * r + 1][0:p, :], silu_out[0:p, r, :],
                                            ALU.mult).then_inc(s_hidden_ready[n], 1)
                    if j >= 2:
                        dve.wait_ge(s_down_done[n], CT * (c * HT + j - 1))
                    dve.wait_ge(s_hidden_ready[n], c * HT + j + 1)
                    nc.vector.tensor_copy(hidden_hi[0:p, r, :], hidden[0:p, r, :]).then_inc(s_hidden_hi[n], 1)
                    dve.wait_ge(s_hidden_hi[n], c * HT + j + 1)
                    nc.vector.tensor_tensor(hidden_lo[0:p, r, :], hidden[0:p, r, :], hidden_hi[0:p, r, :].bitcast(F32),
                                            ALU.subtract).then_inc(s_hidden_lo[n], 1)
                if not last:
                    inputs_lo(n, c + 1)
                elif n == 0:
                    dve.wait_ge(s_wa_hi, 1)
                    nc.vector.tensor_tensor(wa_split[:, 1], wa_raw[:], wa_split[:, 0].bitcast(F32), ALU.subtract).then_inc(s_wa_lo, 1)
                    latent_inputs_lo(0)
                    latent_inputs_lo(1)
                for t in range(CT):
                    dve.wait_ge(s_down_done[n], CT * (c * HT + HT - 1) + t + 1)
                    xt = xres[:, bass.ds(c * CT + t, 1), :]
                    nc.vector.scalar_tensor_tensor(xt, bank[4 + t][:].rearrange("q (o d) -> q o d", o=1), 0.5,
                                                   xt, ALU.mult, ALU.add).then_inc(s_y_added[n], 1)
                if n == 0 and not last:
                    for t in range(CT):
                        dve.wait_ge(s_y_added[n], (c + 1) * CT + t + 1)
                        nc.vector.bn_stats(stat6[:, bass.ds(c * CT + t, 1), :],
                                           xres[:, bass.ds(c * CT + t, 1), :]).then_inc(s_tile_stats, 1)
                    half_stats(1, c * CT)

            def ffn(n):
                nc.vector.memset(free_mark[:], 0.0).then_inc(s_y_added[n], CT)
                if n == 0:
                    for t in range(CT, TT):
                        tile_stats(t)
                    half_stats(0, CT)
                with dve.Fori(0, NC - 1) as c:
                    chunk(n, c, False)
                chunk(n, NC - 1, True)

            def latents(first_weights):
                def keys(t):
                    dve.wait_ge(s_latents_scaled, 3 * (t + 1))
                    b = bank[2 + t % 2]
                    r = t % 2
                    if t >= 2:
                        dve.wait_ge(s_latents_turned, t - 1)
                    ck, kc = latents_tok[:, r, 2, :], latents_tok[:, r, 3, :]
                    nc.vector.tensor_copy(ck[:, 0:CR], kv_lat[:, t, :])
                    nc.vector.tensor_copy(kc[:, CR:P], kv_lat[:, t, :])
                    if t == 0:
                        dve.wait_ge(s_tok_loaded, 16)
                    e, o = b[:, QR + CR:LAT:2], b[:, QR + CR + 1:LAT:2]
                    cos, sin = tok_table[:, t, 0, :], tok_table[:, t, 1, :]
                    for n, (x, y) in enumerate(((e, cos), (o, sin), (o, cos), (e, sin))):
                        ins = nc.vector.tensor_tensor(ropes[:, r, n, :], x, y, ALU.mult)
                    link(ins)
                    for dst in (ck[:, CR:P], kc[:, 0:CR]):
                        nc.vector.tensor_tensor(dst[:, 0:32], ropes[:, r, 0, :], ropes[:, r, 1, :], ALU.subtract)
                        ins = nc.vector.tensor_tensor(dst[:, 32:64], ropes[:, r, 2, :], ropes[:, r, 3, :], ALU.add)
                    ins.then_inc(s_keys_roped, 1)

                def split_turned(t):
                    b = bank[4 + t % 2]
                    c = slice(t * P, (t + 1) * P)
                    dve.wait_ge(s_latents_hi, 4 * (t + 1))
                    nc.vector.scalar_tensor_tensor(qlat_0[:, 1, c], b[:, 0:P], lnw[:, 0:1], qlat_0[:, 0, c].bitcast(F32),
                                                   ALU.mult, ALU.subtract).then_inc(s_latents_lo, 1)
                    nc.vector.scalar_tensor_tensor(qlat_1[64:P, c], b[64:P, P:2 * P], lnw[64:P, 1:2],
                                                   qlat_1[64:P, c].bitcast(F32), ALU.mult, ALU.subtract).then_inc(s_latents_lo, 1)
                    for a in range(2):
                        nc.vector.scalar_tensor_tensor(keys_t[:, 1, a, c], b[:, (2 + a) * P:(3 + a) * P],
                                                       lnw[:, 3 + a:4 + a], keys_t[:, 0, a, c].bitcast(F32),
                                                       ALU.mult, ALU.subtract).then_inc(s_latents_lo, 1)

                dve.wait_ge(s_lnw_loaded, 16 * N_LNW)
                for t in range(1, TT + 3):
                    if 2 <= t < TT:
                        latent_inputs_lo(t)
                    if t <= 2:
                        for i in (CT + 2 * (t - 1), CT + 2 * t - 1):
                            dve.wait_ge(s_y_added[0], CT + i + 1)
                            tile_stats(i)
                    if t == 2:
                        half_stats(1, CT)
                    if t == 3:
                        dve.wait_ge(s_rstd_steps[1], 4)
                        dve.wait_ge(s_x_normed[1], CT)
                    for i in {3: (CT, CT + 1), 4: (CT + 2,), 5: (CT + 3,)}.get(t, ()):
                        nc.vector.tensor_scalar(x_norm_b[:, i - CT, :], xres[:, i, :], mean_var[:, i, 0:1], rstd[:, i:i + 1],
                                                ALU.subtract, ALU.mult).then_inc(s_x_normed[1], 1)
                    if 2 <= t < TT + 2:
                        keys(t - 2)
                    if t >= 3:
                        split_turned(t - 3)
                    first_weights(t)

            def attention():
                def weights_turned(g, p):
                    dve.wait_ge(s_pair_turned, (nth(g) * PAIRS + p + 1) * 2)
                    kv = q_bank(g, "kv", p)[:, 0:4 * CR].rearrange("p (h i c) -> p h i c", h=2, i=2)
                    nc.vector.tensor_copy(wk_t[:], kv[:, :, 0, :])
                    nc.vector.tensor_copy(wv_t[:, p % 2], kv[:, :, 1, :]).then_inc(s_wkv_copied, 1)

                def absorbed(g, p):
                    dve.wait_ge(s_absorbed_hi, (nth(g) * PAIRS + p + 1) * 2)
                    b = q_bank(g, "ab", p)
                    for h in range(2):
                        c = slice(64 * (1 - h), 64 * (1 - h) + CR)
                        last = nc.vector.tensor_tensor(q_weights[:, p % 2, h, 1::2, c],
                                                       b[:, h * P:(h + 1) * P].rearrange("p (i c) -> p i c", i=2),
                                                       q_weights[:, p % 2, h, 0::2, c].bitcast(F32), ALU.subtract)
                    last.then_inc(s_absorbed_lo, 1)

                def value_weights(g, p):
                    dve.wait_ge(s_wvo_hi, nth(g) * PAIRS + p + 1)
                    nc.vector.scalar_tensor_tensor(wvo_split[:, 1, p % PAIRS, :], q_bank(g, "wvo", p)[:], lnw[:, 2:3],
                                                   wvo_split[:, 0, p % PAIRS, :].bitcast(F32), ALU.mult,
                                                   ALU.subtract).then_inc(s_wvo_lo, 1)

                def rotary(g, pb):
                    if not (g is None and pb == 0):
                        dve.wait_ge(s_q_lo, nth(g) * 16 + 2 * pb)
                    for h, name in enumerate(("q0", "q1")):
                        dve.wait_ge(s_q_swapped, nth(g) * 16 + 2 * pb + h + 1)
                        nc.vector.tensor_tensor(q_full[:, h, :], q_bank(g, name, pb)[:], tables[:, h, :],
                                                ALU.mult).then_inc(s_q_by_tables, 1)
                    nc.vector.tensor_tensor(q_swap[:], q_swap[:], tables[:, 2, :], ALU.mult).then_inc(s_q_by_tables, 1)

                def row_max(g, u, n):
                    dve.wait_ge(s_scores_ready, nth(g) * 3 * UNITS + 3 * u + n + 1)
                    for q in ((3,), (2, 0), (1,))[n]:
                        o, N = SCORE[q][1], (q + 1) * P
                        ins = nc.vector.tensor_reduce(small[:, 0, u % 2, q:q + 1], bank[n][:, o:o + N],
                                                      mybir.AxisListType.X, ALU.max, negate=True)
                    ins.then_inc(s_max_ready, 1)

                def normalize(g, u):
                    r = u % 2
                    dve.wait_ge(s_exp_done, nth(g) * 4 * UNITS + 4 * (u + 1))
                    nc.vector.reciprocal(small[:, 3, r, :], small[:, 2, r, :]).then_inc(s_recip_ready, 1)
                    dve.wait_ge(s_recip_ready, nth(g) * UNITS + u + 1)
                    for q in range(4):
                        i, N = SCORE[q][2], (q + 1) * P
                        ins = nc.vector.tensor_scalar(probs[:, u % 4, i:i + N], probs[:, u % 4, i:i + N],
                                                      small[:, 3, r, q:q + 1], None, ALU.mult)
                    ins.then_inc(s_probs_ready, 1)

                def values_lo(g, pb):
                    dve.wait_ge(s_values_hi, nth(g) * 2 * PAIRS + pb + 1)
                    p, b = pb // 2, pb % 2
                    c = slice(QT4 * b, QT4 * (b + 1))
                    nc.vector.tensor_tensor(values_t[:, c, 1, p, :], bank[5][:].rearrange("p (t n) -> p t n", t=QT4),
                                            values_t[:, c, 0, p, :].bitcast(F32), ALU.subtract).then_inc(s_values_lo, 1)

                work_of = {"turn": weights_turned, "absorb": absorbed, "wvo": value_weights, "queries": rotary,
                           "values": values_lo}

                def group(g, last):
                    for u in STEPS:
                        if u < UNITS or not last:
                            for n in range(3):
                                row_max(g, u, n)
                        if u <= UNITS or not last:
                            normalize(g, u - 1)
                        for work, i in fills(u, last):
                            if work in work_of:
                                work_of[work](g, i)
                    values_lo(g, UNITS // 2 - 1)
                    for t in range(TT):
                        if last and t == TT - 1:
                            inputs_lo(2, 0)
                        dve.wait_ge(s_out_done, nth(g) * TT + t + 1)
                        nc.vector.tensor_tensor(xres[:, t, :], q_bank(g, "out", t)[:], xres[:, t, :],
                                                ALU.add).then_inc(s_x_added, 1)
                        if last and t >= 1:
                            dve.wait_ge(s_x_added, nth(g) * TT + t)
                            tile_stats(t - 1)
                            if t == CT:
                                half_stats(2, 0)
                            if t == CT + 1:
                                normalize_tiles(2)
                    if last:
                        dve.wait_ge(s_x_added, (nth(g) + 1) * TT)
                        tile_stats(TT - 1)
                        half_stats(2, CT)
                    if not last:
                        value_weights(g, PAIRS)
                        value_weights(g, PAIRS + 1)

                def first_weights(t):
                    if t in (3, 5):
                        weights_turned(None, (t - 3) // 2)
                    if t in (4, 6):
                        absorbed(None, (t - 4) // 2)
                    if t == TT:
                        dve.wait_ge(s_tables_loaded, 16)
                        rotary(None, 0)
                    if t >= TT + 1:
                        value_weights(None, t - TT - 1)

                latents(first_weights)
                rotary(None, 1)
                for u in range(2):
                    for n in range(3):
                        row_max(None, u, n)
                normalize(None, 0)
                rotary(None, 2)
                with dve.Fori(0, GROUPS - 1) as g:
                    group(g, False)
                group(GROUPS - 1, True)

            prep_weights()
            ffn(0)
            attention()
            ffn(2)


def rope_tables():
    inv = (1.0 / np.float32(10000.0) ** (np.arange(0, ROPE, 2, dtype=np.float32) / np.float32(ROPE))).astype(np.float32)
    freqs = np.outer(np.arange(SEQ, dtype=np.float32), inv).astype(np.float32)
    cos, sin = np.cos(freqs).astype(np.float32), np.sin(freqs).astype(np.float32)
    tok = np.zeros((P, TT, 2, 32), np.float32)
    for t in range(TT):
        rows = slice((t * P) % SEQ, (t * P) % SEQ + P)
        tok[:, t, 0], tok[:, t, 1] = cos[rows], sin[rows]
    turned = np.ones((P, 3, SEQ), np.float32)
    turned *= np.float32(SCALE)
    cos, sin = cos * np.float32(SCALE), sin * np.float32(SCALE)
    turned[0:64, 0] = turned[64:128, 1] = np.concatenate([cos.T, cos.T])
    turned[0:64, 2] = turned[64:128, 2] = np.concatenate([-sin.T, sin.T])
    return tok, turned


def kernel(**inputs):
    import concourse.bacc as bacc
    from concourse.bass_utils import run_bass_kernel_spmd as run

    nc = bacc.Bacc("TRN2", target_bir_lowering=False, num_devices=1)
    tok, turned = rope_tables()
    named = [("x", np.ascontiguousarray(inputs["L0_attn_hidden_states"]).reshape(T, D))]
    for n in ("Wq_a", "q_a_ln_w", "Wq_b", "Wkv_a", "kv_a_ln_w", "Wkv_b", "Wo"):
        a = np.ascontiguousarray(inputs["L0_attn_" + n])
        named.append((n, a.reshape(-1, 1) if a.ndim == 1 else a))
    for n in ("gate_w", "up_w", "down_w", "gate_a", "gate_b", "up_a", "up_b", "down_a", "down_b"):
        named.append((n, np.ascontiguousarray(inputs["L0_ffn_" + n])))
    named += [("rope_tok", tok), ("rope_t", turned),
              ("mask", np.triu(np.full((P, P), MASKED, np.float32), 1))]
    args = [nc.dram_tensor("in_" + n, a.shape, F32, kind="ExternalInput").ap() for n, a in named]
    args.append(nc.dram_tensor("w_scratch", (HT, P, 6 * 512), F32, kind="Internal").ap())
    args.append(nc.dram_tensor("out", (T, D), F32, kind="ExternalOutput").ap())
    prog(nc, *args)
    r = run(nc, [{"in_" + n: a for n, a in named}], core_ids=[0])
    return r.results[0]["out"].reshape(2, SEQ, D)
```
